# Optimizing a Trainium2 kernel written in Bass

```python
import numpy as np
import jax
import jax.numpy as jnp

def _softmax(x, axis=-1):
    return jax.nn.softmax(x, axis=axis)

def _gelu(x):
    return jax.nn.gelu(x, approximate=True)

def _silu(x):
    return jax.nn.silu(x)

def _sigmoid(x):
    return jax.nn.sigmoid(x)

def _layernorm(x, axis=-1, eps=1e-05):
    m = jnp.mean(x, axis=axis, keepdims=True)
    v = jnp.var(x, axis=axis, keepdims=True)
    return (x - m) / jnp.sqrt(v + eps)

def _scatter_add(tgt, idx, src, axis=0):
    return tgt.at[idx].add(src)

def _segment_sum(src, seg, n):
    return jax.ops.segment_sum(src, seg, n)
kernel_name = 'mk_hybrid_d2_jaxref_r8_f45580'

def setup_inputs(seed: int=0):
    np.random.seed(seed)
    _w = jnp.asarray

    def _L0_attn_a_setup():
        import jax, jax.numpy as jnp
        import numpy as np
        B, L, C, H = (8, 256, 128, 16)
        HID = 4 * C

        def _rope(x):
            b, n, c = x.shape
            k_max = c // 2
            theta = 1.0 / 10000.0 ** (jnp.arange(k_max, dtype=jnp.float32) / k_max)
            cos_t, sin_t = (jnp.cos(theta), jnp.sin(theta))
            xr = x.reshape(b, n, k_max, 2)
            re = xr[..., 0] * cos_t - xr[..., 1] * sin_t
            im = xr[..., 0] * sin_t + xr[..., 1] * cos_t
            return jnp.stack((re, im), axis=-1).reshape(b, n, c)

        def _dwconv(x_bcl, w, bias):
            y = jax.lax.conv_general_dilated(x_bcl, w, (1,), [(1, 1)], dimension_numbers=('NCH', 'OIH', 'NCH'), feature_group_count=x_bcl.shape[1])
            return y + bias[None, :, None]

        def _ln(x, g, b, eps=1e-05):
            mu = x.mean(-1, keepdims=True)
            var = ((x - mu) ** 2).mean(-1, keepdims=True)
            return (x - mu) * jax.lax.rsqrt(var + eps) * g + b

        def _mlla_forward(x, cpe1_w, cpe1_b, norm1_g, norm1_b, in_w, in_b, actp_w, actp_b, dwc_w, dwc_b, qk_w, qk_b, lepe_w, lepe_b, out_w, out_b, cpe2_w, cpe2_b, norm2_g, norm2_b, fc1_w, fc1_b, fc2_w, fc2_b):
            b, n, c = x.shape
            h, d = (H, c // H)
            x = x + _dwconv(x.transpose(0, 2, 1), cpe1_w, cpe1_b).transpose(0, 2, 1)
            shortcut = x
            xn = _ln(x, norm1_g, norm1_b)
            act_res = jax.nn.silu(xn @ actp_w + actp_b)
            xi = xn @ in_w + in_b
            xi = jax.nn.silu(_dwconv(xi.transpose(0, 2, 1), dwc_w, dwc_b)).transpose(0, 2, 1)
            qk = xi @ qk_w + qk_b
            q = jax.nn.elu(qk[..., :c]) + 1.0
            k = jax.nn.elu(qk[..., c:]) + 1.0
            q_rope = _rope(q).reshape(b, n, h, d).transpose(0, 2, 1, 3)
            k_rope = _rope(k).reshape(b, n, h, d).transpose(0, 2, 1, 3)
            qh = q.reshape(b, n, h, d).transpose(0, 2, 1, 3)
            kh = k.reshape(b, n, h, d).transpose(0, 2, 1, 3)
            vh = xi.reshape(b, n, h, d).transpose(0, 2, 1, 3)
            k_mean = kh.mean(axis=2, keepdims=True)
            z = 1.0 / (jnp.einsum('bhnd,bhmd->bhnm', qh, k_mean) + 1e-06)
            kv = jnp.einsum('bhnd,bhne->bhde', k_rope, vh) * (1.0 / n)
            attn = jnp.einsum('bhnd,bhde->bhne', q_rope, kv) * z
            attn = attn.transpose(0, 2, 1, 3).reshape(b, n, c)
            v_bcl = vh.transpose(0, 2, 1, 3).reshape(b, n, c).transpose(0, 2, 1)
            attn = attn + _dwconv(v_bcl, lepe_w, lepe_b).transpose(0, 2, 1)
            x = shortcut + attn * act_res @ out_w + out_b
            x = x + _dwconv(x.transpose(0, 2, 1), cpe2_w, cpe2_b).transpose(0, 2, 1)
            xn2 = _ln(x, norm2_g, norm2_b)
            mlp = jax.nn.gelu(xn2 @ fc1_w + fc1_b, approximate=False) @ fc2_w + fc2_b
            return x + mlp
        key = jax.random.key(seed)
        ks = jax.random.split(key, 12)

        def nrm(k, shape, scale=0.02):
            return jax.random.normal(k, shape, jnp.float32) * scale
        return {'x': jax.random.normal(ks[0], (B, L, C), jnp.float32), 'cpe1_w': nrm(ks[1], (C, 1, 3), 0.1), 'cpe1_b': jnp.zeros((C,), jnp.float32), 'norm1_g': jnp.ones((C,), jnp.float32), 'norm1_b': jnp.zeros((C,), jnp.float32), 'in_w': nrm(ks[2], (C, C)), 'in_b': jnp.zeros((C,), jnp.float32), 'actp_w': nrm(ks[3], (C, C)), 'actp_b': jnp.zeros((C,), jnp.float32), 'dwc_w': nrm(ks[4], (C, 1, 3), 0.1), 'dwc_b': jnp.zeros((C,), jnp.float32), 'qk_w': nrm(ks[5], (C, 2 * C)), 'qk_b': jnp.zeros((2 * C,), jnp.float32), 'lepe_w': nrm(ks[6], (C, 1, 3), 0.1), 'lepe_b': jnp.zeros((C,), jnp.float32), 'out_w': nrm(ks[7], (C, C)), 'out_b': jnp.zeros((C,), jnp.float32), 'cpe2_w': nrm(ks[8], (C, 1, 3), 0.1), 'cpe2_b': jnp.zeros((C,), jnp.float32), 'norm2_g': jnp.ones((C,), jnp.float32), 'norm2_b': jnp.zeros((C,), jnp.float32), 'fc1_w': nrm(ks[9], (C, HID)), 'fc1_b': jnp.zeros((HID,), jnp.float32), 'fc2_w': nrm(ks[10], (HID, C)), 'fc2_b': jnp.zeros((C,), jnp.float32)}
    _L0_attn_a_in = _L0_attn_a_setup()

    def _L0_attn_b_setup():
        import jax, jax.numpy as jnp
        import numpy as np
        N_HEADS = 16
        CHUNK = 64
        TAU = 12.5
        THRESHOLD = 0.5
        N_FHN_STEPS = 2

        def fhn_dynamics(stimulus, a, b, dt, n_steps=N_FHN_STEPS, tau=TAU, threshold=THRESHOLD):
            stim_scale = jnp.clip(jnp.max(jnp.abs(stimulus), axis=-1, keepdims=True), 1e-06, None)
            stim_normed = stimulus / stim_scale
            gate = jax.nn.sigmoid((jnp.abs(stimulus) - threshold) * 10.0)
            I = stim_normed * (0.1 + 0.9 * gate)
            v = jnp.zeros_like(stimulus)
            w = jnp.zeros_like(stimulus)
            alpha = dt / tau
            denom = 1.0 + alpha * b
            for _ in range(n_steps):
                dv_explicit = v - v * v * v / 3.0 - w + I
                v_next = v + dt * dv_explicit
                w_next = (w + alpha * (v_next + a)) / denom
                v = jnp.clip(v_next, -3.0, 3.0)
                w = jnp.clip(w_next, -3.0, 3.0)
            response = v * stim_scale
            return (response, v)

        def chunked_fhn_attention(q, k, v, a, b, dt, chunk_size=CHUNK):
            B, H, T, Dh = q.shape
            n_chunks = (T + chunk_size - 1) // chunk_size
            scale = 1.0 / Dh ** 0.5
            out_chunks = []
            fhn_states = []
            for ci in range(n_chunks):
                s = ci * chunk_size
                e = min(s + chunk_size, T)
                q_c = q[:, :, s:e, :]
                k_c = k[:, :, :e, :]
                v_c = v[:, :, :e, :]
                scores = jnp.einsum('bhtd,bhsd->bhts', q_c, k_c) * scale
                probs = jax.nn.softmax(scores, axis=-1)
                attn_energy = probs.sum(axis=-1)
                stim = jnp.broadcast_to(attn_energy[..., None], (B, H, e - s, Dh))
                fhn_out, fhn_state = fhn_dynamics(stim, a, b, dt)
                fhn_gate = jax.nn.sigmoid(fhn_out.mean(axis=-1))[..., None]
                probs = probs * (0.5 + 0.5 * fhn_gate)
                probs = probs / (probs.sum(axis=-1, keepdims=True) + 1e-08)
                out_chunks.append(jnp.einsum('bhts,bhsd->bhtd', probs, v_c))
                fhn_states.append(fhn_state.mean())
            out = jnp.concatenate(out_chunks, axis=2)
            fhn_state_mean = jnp.stack(fhn_states).mean()
            return (out, fhn_state_mean)
        key = jax.random.key(seed)
        ks = jax.random.split(key, 5)
        B, T, E = (2, 512, 128)
        x = jax.random.normal(ks[0], (B, T, E), dtype=jnp.float32)
        spectral_basis = jax.random.normal(ks[1], (B, T, 32), dtype=jnp.float32)
        W_qkv = jax.random.normal(ks[2], (3 * E, E), dtype=jnp.float32) * E ** (-0.5)
        W_out = jax.random.normal(ks[3], (E, E), dtype=jnp.float32) * E ** (-0.5)
        a = jnp.asarray(0.7, dtype=jnp.float32)
        b = jnp.asarray(0.8, dtype=jnp.float32)
        dt = jnp.asarray(1.0, dtype=jnp.float32)
        return {'x': x, 'spectral_basis': spectral_basis, 'W_qkv': W_qkv, 'W_out': W_out, 'a': a, 'b': b, 'dt': dt}
    _L0_attn_b_in = _L0_attn_b_setup()

    def _L0_ffn_setup():
        import jax, jax.numpy as jnp
        import numpy as np
        D_MODEL = 128
        EXPERT_DIM = 512
        N_EXPERTS = 8
        CAP_FACTOR = 0.5
        key = jax.random.key(seed)
        ks = jax.random.split(key, 7)
        inp = {'input': jax.random.normal(ks[0], (4, 512, D_MODEL), dtype=jnp.float32), 'w_switch': jax.random.normal(ks[1], (D_MODEL, N_EXPERTS), dtype=jnp.float32) * 0.02, 'b_switch': jnp.zeros((N_EXPERTS,), jnp.float32), 'w1': jax.random.normal(ks[2], (N_EXPERTS, D_MODEL, EXPERT_DIM), dtype=jnp.float32) * 0.02, 'b1': jnp.zeros((N_EXPERTS, EXPERT_DIM), jnp.float32), 'w2': jax.random.normal(ks[3], (N_EXPERTS, EXPERT_DIM, D_MODEL), dtype=jnp.float32) * 0.02, 'b2': jnp.zeros((N_EXPERTS, D_MODEL), jnp.float32)}
        return inp
    _L0_ffn_in = _L0_ffn_setup()

    def _L1_attn_a_setup():
        import jax, jax.numpy as jnp
        import numpy as np
        B, M, D, H = (2, 256, 128, 16)

        def _rope(x):
            b, m, d = x.shape
            i = jnp.arange(d // 2, dtype=jnp.float32)
            theta = 10000.0 ** (-2.0 * (i - 1.0) / d)
            ang = jnp.arange(m, dtype=jnp.float32)[:, None] * theta[None, :]
            c, s = (jnp.cos(ang), jnp.sin(ang))
            xe, xo = (x[..., 0::2], x[..., 1::2])
            ye = xe * c + xo * s
            yo = -xe * s + xo * c
            return jnp.stack([ye, yo], axis=-1).reshape(b, m, d)
        key = jax.random.key(seed)
        ks = jax.random.split(key, 8)
        w = lambda k, shape: jax.random.normal(k, shape, jnp.float32) * 0.02
        return {'x': jax.random.normal(ks[0], (B, M, D), jnp.float32), 'wq': w(ks[1], (D, D)), 'wk': w(ks[2], (D, D)), 'wv': w(ks[3], (D, D)), 'in_proj_w': w(ks[4], (3 * D, D)), 'in_proj_b': w(ks[5], (3 * D,)), 'out_w': w(ks[6], (D, D)), 'out_b': w(ks[7], (D,))}
    _L1_attn_a_in = _L1_attn_a_setup()

    def _L1_attn_b_setup():
        import jax, jax.numpy as jnp
        import numpy as np
        C = 128
        RANK = 8

        def _layernorm(x, g, b, eps=1e-05):
            mu = jnp.mean(x, axis=-1, keepdims=True)
            var = jnp.var(x, axis=-1, keepdims=True)
            return (x - mu) * jax.lax.rsqrt(var + eps) * g + b

        def _reference_tuple_inner(x, W0, A_init, B_init, log_lr, Wq, Wk, Wv, Wo, Wg, ln_g, ln_b, ls_g):
            B, T, _ = x.shape
            h = _layernorm(x, ln_g, ln_b)
            Q = jnp.einsum('btc,dc->btd', h, Wq)
            K = jnp.einsum('btc,dc->btd', h, Wk)
            V = jnp.einsum('btc,dc->btd', h, Wv)
            lr = jnp.minimum(jnp.exp(log_lr), 1.0)
            y0 = jnp.einsum('btc,cd->btd', K, W0) + jnp.einsum('btr,rd->btd', jnp.einsum('btc,cr->btr', K, A_init), B_init)
            error = y0 - V
            loss = jnp.mean(error ** 2)
            gradient = K * error
            grad_cumsum = jnp.cumsum(gradient, axis=1)
            grad_shift = jnp.concatenate([jnp.zeros((B, 1, gradient.shape[-1]), gradient.dtype), grad_cumsum[:, :-1, :]], axis=1)
            correction = Q * lr[None, None, :] * grad_shift
            pos = jnp.arange(1, T + 1, dtype=correction.dtype)
            pos_scale = (1.0 / (1.0 + 0.1 * jnp.log(pos)))[None, :, None]
            out = y0 - correction * pos_scale
            gate = jax.nn.sigmoid(jnp.einsum('btc,dc->btd', x, Wg))
            out = out * gate
            out = jnp.einsum('btc,dc->btd', out, Wo) * ls_g
            return (x + out, loss)
        key = jax.random.key(seed)
        ks = jax.random.split(key, 10)
        B, T = (4, 512)
        x = jax.random.normal(ks[0], (B, T, C), dtype=jnp.float32)
        W0 = jnp.eye(C, dtype=jnp.float32) * 0.1
        A_init = jax.random.normal(ks[1], (C, RANK), dtype=jnp.float32) * 0.01
        B_init = jnp.zeros((RANK, C), dtype=jnp.float32)
        log_lr = jnp.full((C,), float(np.log(0.1)), dtype=jnp.float32)
        s = 1.0 / np.sqrt(C)
        Wq = jax.random.uniform(ks[2], (C, C), minval=-s, maxval=s, dtype=jnp.float32)
        Wk = jax.random.uniform(ks[3], (C, C), minval=-s, maxval=s, dtype=jnp.float32)
        Wv = jax.random.uniform(ks[4], (C, C), minval=-s, maxval=s, dtype=jnp.float32)
        Wo = jax.random.uniform(ks[5], (C, C), minval=-s, maxval=s, dtype=jnp.float32)
        Wg = jax.random.uniform(ks[6], (C, C), minval=-s, maxval=s, dtype=jnp.float32)
        ln_g = jnp.ones((C,), dtype=jnp.float32)
        ln_b = jnp.zeros((C,), dtype=jnp.float32)
        ls_g = jnp.full((C,), 0.0001, dtype=jnp.float32)
        return {'x': x, 'W0': W0, 'A_init': A_init, 'B_init': B_init, 'log_lr': log_lr, 'Wq': Wq, 'Wk': Wk, 'Wv': Wv, 'Wo': Wo, 'Wg': Wg, 'ln_g': ln_g, 'ln_b': ln_b, 'ls_g': ls_g}
    _L1_attn_b_in = _L1_attn_b_setup()

    def _L1_ffn_setup():
        import jax, jax.numpy as jnp
        import numpy as np
        B, S, D, H, M, E, K = (4, 256, 128, 256, 64, 8, 2)

        def _layernorm(x, g, b, eps=1e-05):
            mu = x.mean(-1, keepdims=True)
            var = ((x - mu) ** 2).mean(-1, keepdims=True)
            return (x - mu) * jax.lax.rsqrt(var + eps) * g + b

        def _forward(inputs_embeds, enc_W, enc_b, s2c_W, s2c_b, rW1, rb1, rW2, rb2, We1, be1, We2, be2, c2s_W, c2s_b, dec_W, dec_b, ln_g, ln_b):
            b, s, _ = inputs_embeds.shape
            spikes_enc = jax.nn.sigmoid(inputs_embeds @ enc_W + enc_b)
            flat = spikes_enc.reshape(b * s, H)
            cont = flat @ s2c_W + s2c_b
            logits = jnp.tanh(cont @ rW1 + rb1) @ rW2 + rb2
            probs = jax.nn.softmax(logits, axis=-1)
            topw, topi = jax.lax.top_k(probs, K)
            w = topw / topw.sum(-1, keepdims=True)
            gates = (jax.nn.one_hot(topi, E, dtype=cont.dtype) * w[..., None]).sum(1)
            h = jax.nn.relu(jnp.einsum('nm,emh->enh', cont, We1) + be1[:, None, :])
            expert_out = jnp.einsum('enh,ehm->enm', h, We2) + be2[:, None, :]
            output_flat = jnp.einsum('enm,ne->nm', expert_out, gates)
            spikes_moe = jax.nn.sigmoid(output_flat @ c2s_W + c2s_b).reshape(b, s, H)
            decoded = jax.nn.sigmoid(spikes_moe @ dec_W + dec_b)
            return _layernorm(decoded, ln_g, ln_b)
        key = jax.random.key(seed)
        ks = jax.random.split(key, 10)
        r = lambda k, shape: jax.random.normal(k, shape, dtype=jnp.float32) * 0.02
        return {'inputs_embeds': jax.random.normal(ks[0], (B, S, D), dtype=jnp.float32), 'enc_W': r(ks[1], (D, H)), 'enc_b': jnp.zeros((H,), jnp.float32), 's2c_W': r(ks[2], (H, M)), 's2c_b': jnp.zeros((M,), jnp.float32), 'rW1': r(ks[3], (M, 64)), 'rb1': jnp.zeros((64,), jnp.float32), 'rW2': r(ks[4], (64, E)), 'rb2': jnp.zeros((E,), jnp.float32), 'We1': r(ks[5], (E, M, H // 2)), 'be1': jnp.zeros((E, H // 2), jnp.float32), 'We2': r(ks[6], (E, H // 2, M)), 'be2': jnp.zeros((E, M), jnp.float32), 'c2s_W': r(ks[7], (M, H)), 'c2s_b': jnp.zeros((H,), jnp.float32), 'dec_W': r(ks[8], (H, D)), 'dec_b': jnp.zeros((D,), jnp.float32), 'ln_g': jnp.ones((D,), jnp.float32), 'ln_b': jnp.zeros((D,), jnp.float32)}
    _L1_ffn_in = _L1_ffn_setup()
    _d = {'L0_attn_a_x': _L0_attn_a_in['x'], 'L0_attn_a_cpe1_w': _L0_attn_a_in['cpe1_w'], 'L0_attn_a_cpe1_b': _L0_attn_a_in['cpe1_b'], 'L0_attn_a_norm1_g': _L0_attn_a_in['norm1_g'], 'L0_attn_a_norm1_b': _L0_attn_a_in['norm1_b'], 'L0_attn_a_in_w': _L0_attn_a_in['in_w'], 'L0_attn_a_in_b': _L0_attn_a_in['in_b'], 'L0_attn_a_actp_w': _L0_attn_a_in['actp_w'], 'L0_attn_a_actp_b': _L0_attn_a_in['actp_b'], 'L0_attn_a_dwc_w': _L0_attn_a_in['dwc_w'], 'L0_attn_a_dwc_b': _L0_attn_a_in['dwc_b'], 'L0_attn_a_qk_w': _L0_attn_a_in['qk_w'], 'L0_attn_a_qk_b': _L0_attn_a_in['qk_b'], 'L0_attn_a_lepe_w': _L0_attn_a_in['lepe_w'], 'L0_attn_a_lepe_b': _L0_attn_a_in['lepe_b'], 'L0_attn_a_out_w': _L0_attn_a_in['out_w'], 'L0_attn_a_out_b': _L0_attn_a_in['out_b'], 'L0_attn_a_cpe2_w': _L0_attn_a_in['cpe2_w'], 'L0_attn_a_cpe2_b': _L0_attn_a_in['cpe2_b'], 'L0_attn_a_norm2_g': _L0_attn_a_in['norm2_g'], 'L0_attn_a_norm2_b': _L0_attn_a_in['norm2_b'], 'L0_attn_a_fc1_w': _L0_attn_a_in['fc1_w'], 'L0_attn_a_fc1_b': _L0_attn_a_in['fc1_b'], 'L0_attn_a_fc2_w': _L0_attn_a_in['fc2_w'], 'L0_attn_a_fc2_b': _L0_attn_a_in['fc2_b'], 'L0_attn_b_spectral_basis': _L0_attn_b_in['spectral_basis'], 'L0_attn_b_W_qkv': _L0_attn_b_in['W_qkv'], 'L0_attn_b_W_out': _L0_attn_b_in['W_out'], 'L0_attn_b_a': _L0_attn_b_in['a'], 'L0_attn_b_b': _L0_attn_b_in['b'], 'L0_attn_b_dt': _L0_attn_b_in['dt'], 'L0_ffn_w_switch': _L0_ffn_in['w_switch'], 'L0_ffn_b_switch': _L0_ffn_in['b_switch'], 'L0_ffn_w1': _L0_ffn_in['w1'], 'L0_ffn_b1': _L0_ffn_in['b1'], 'L0_ffn_w2': _L0_ffn_in['w2'], 'L0_ffn_b2': _L0_ffn_in['b2'], 'L1_attn_a_wq': _L1_attn_a_in['wq'], 'L1_attn_a_wk': _L1_attn_a_in['wk'], 'L1_attn_a_wv': _L1_attn_a_in['wv'], 'L1_attn_a_in_proj_w': _L1_attn_a_in['in_proj_w'], 'L1_attn_a_in_proj_b': _L1_attn_a_in['in_proj_b'], 'L1_attn_a_out_w': _L1_attn_a_in['out_w'], 'L1_attn_a_out_b': _L1_attn_a_in['out_b'], 'L1_attn_b_W0': _L1_attn_b_in['W0'], 'L1_attn_b_A_init': _L1_attn_b_in['A_init'], 'L1_attn_b_B_init': _L1_attn_b_in['B_init'], 'L1_attn_b_log_lr': _L1_attn_b_in['log_lr'], 'L1_attn_b_Wq': _L1_attn_b_in['Wq'], 'L1_attn_b_Wk': _L1_attn_b_in['Wk'], 'L1_attn_b_Wv': _L1_attn_b_in['Wv'], 'L1_attn_b_Wo': _L1_attn_b_in['Wo'], 'L1_attn_b_Wg': _L1_attn_b_in['Wg'], 'L1_attn_b_ln_g': _L1_attn_b_in['ln_g'], 'L1_attn_b_ln_b': _L1_attn_b_in['ln_b'], 'L1_attn_b_ls_g': _L1_attn_b_in['ls_g'], 'L1_ffn_enc_W': _L1_ffn_in['enc_W'], 'L1_ffn_enc_b': _L1_ffn_in['enc_b'], 'L1_ffn_s2c_W': _L1_ffn_in['s2c_W'], 'L1_ffn_s2c_b': _L1_ffn_in['s2c_b'], 'L1_ffn_rW1': _L1_ffn_in['rW1'], 'L1_ffn_rb1': _L1_ffn_in['rb1'], 'L1_ffn_rW2': _L1_ffn_in['rW2'], 'L1_ffn_rb2': _L1_ffn_in['rb2'], 'L1_ffn_We1': _L1_ffn_in['We1'], 'L1_ffn_be1': _L1_ffn_in['be1'], 'L1_ffn_We2': _L1_ffn_in['We2'], 'L1_ffn_be2': _L1_ffn_in['be2'], 'L1_ffn_c2s_W': _L1_ffn_in['c2s_W'], 'L1_ffn_c2s_b': _L1_ffn_in['c2s_b'], 'L1_ffn_dec_W': _L1_ffn_in['dec_W'], 'L1_ffn_dec_b': _L1_ffn_in['dec_b'], 'L1_ffn_ln_g': _L1_ffn_in['ln_g'], 'L1_ffn_ln_b': _L1_ffn_in['ln_b']}
    _x0 = _d['L0_attn_a_x']
    _d['L0_attn_a_x'] = jax.random.normal(jax.random.fold_in(jax.random.key(seed), 1), (2, 1024, 128), dtype=_x0.dtype)
    del _x0
    return _d

def reference(L0_attn_a_x, L0_attn_a_cpe1_w, L0_attn_a_cpe1_b, L0_attn_a_norm1_g, L0_attn_a_norm1_b, L0_attn_a_in_w, L0_attn_a_in_b, L0_attn_a_actp_w, L0_attn_a_actp_b, L0_attn_a_dwc_w, L0_attn_a_dwc_b, L0_attn_a_qk_w, L0_attn_a_qk_b, L0_attn_a_lepe_w, L0_attn_a_lepe_b, L0_attn_a_out_w, L0_attn_a_out_b, L0_attn_a_cpe2_w, L0_attn_a_cpe2_b, L0_attn_a_norm2_g, L0_attn_a_norm2_b, L0_attn_a_fc1_w, L0_attn_a_fc1_b, L0_attn_a_fc2_w, L0_attn_a_fc2_b, L0_attn_b_spectral_basis, L0_attn_b_W_qkv, L0_attn_b_W_out, L0_attn_b_a, L0_attn_b_b, L0_attn_b_dt, L0_ffn_w_switch, L0_ffn_b_switch, L0_ffn_w1, L0_ffn_b1, L0_ffn_w2, L0_ffn_b2, L1_attn_a_wq, L1_attn_a_wk, L1_attn_a_wv, L1_attn_a_in_proj_w, L1_attn_a_in_proj_b, L1_attn_a_out_w, L1_attn_a_out_b, L1_attn_b_W0, L1_attn_b_A_init, L1_attn_b_B_init, L1_attn_b_log_lr, L1_attn_b_Wq, L1_attn_b_Wk, L1_attn_b_Wv, L1_attn_b_Wo, L1_attn_b_Wg, L1_attn_b_ln_g, L1_attn_b_ln_b, L1_attn_b_ls_g, L1_ffn_enc_W, L1_ffn_enc_b, L1_ffn_s2c_W, L1_ffn_s2c_b, L1_ffn_rW1, L1_ffn_rb1, L1_ffn_rW2, L1_ffn_rb2, L1_ffn_We1, L1_ffn_be1, L1_ffn_We2, L1_ffn_be2, L1_ffn_c2s_W, L1_ffn_c2s_b, L1_ffn_dec_W, L1_ffn_dec_b, L1_ffn_ln_g, L1_ffn_ln_b):

    def _L0_attn_a_ref(x, cpe1_w, cpe1_b, norm1_g, norm1_b, in_w, in_b, actp_w, actp_b, dwc_w, dwc_b, qk_w, qk_b, lepe_w, lepe_b, out_w, out_b, cpe2_w, cpe2_b, norm2_g, norm2_b, fc1_w, fc1_b, fc2_w, fc2_b):
        import jax, jax.numpy as jnp
        import numpy as np
        B, L, C, H = (8, 256, 128, 16)
        HID = 4 * C

        def _rope(x):
            b, n, c = x.shape
            k_max = c // 2
            theta = 1.0 / 10000.0 ** (jnp.arange(k_max, dtype=jnp.float32) / k_max)
            cos_t, sin_t = (jnp.cos(theta), jnp.sin(theta))
            xr = x.reshape(b, n, k_max, 2)
            re = xr[..., 0] * cos_t - xr[..., 1] * sin_t
            im = xr[..., 0] * sin_t + xr[..., 1] * cos_t
            return jnp.stack((re, im), axis=-1).reshape(b, n, c)

        def _dwconv(x_bcl, w, bias):
            y = jax.lax.conv_general_dilated(x_bcl, w, (1,), [(1, 1)], dimension_numbers=('NCH', 'OIH', 'NCH'), feature_group_count=x_bcl.shape[1])
            return y + bias[None, :, None]

        def _ln(x, g, b, eps=1e-05):
            mu = x.mean(-1, keepdims=True)
            var = ((x - mu) ** 2).mean(-1, keepdims=True)
            return (x - mu) * jax.lax.rsqrt(var + eps) * g + b

        def _mlla_forward(x, cpe1_w, cpe1_b, norm1_g, norm1_b, in_w, in_b, actp_w, actp_b, dwc_w, dwc_b, qk_w, qk_b, lepe_w, lepe_b, out_w, out_b, cpe2_w, cpe2_b, norm2_g, norm2_b, fc1_w, fc1_b, fc2_w, fc2_b):
            b, n, c = x.shape
            h, d = (H, c // H)
            x = x + _dwconv(x.transpose(0, 2, 1), cpe1_w, cpe1_b).transpose(0, 2, 1)
            shortcut = x
            xn = _ln(x, norm1_g, norm1_b)
            act_res = jax.nn.silu(xn @ actp_w + actp_b)
            xi = xn @ in_w + in_b
            xi = jax.nn.silu(_dwconv(xi.transpose(0, 2, 1), dwc_w, dwc_b)).transpose(0, 2, 1)
            qk = xi @ qk_w + qk_b
            q = jax.nn.elu(qk[..., :c]) + 1.0
            k = jax.nn.elu(qk[..., c:]) + 1.0
            q_rope = _rope(q).reshape(b, n, h, d).transpose(0, 2, 1, 3)
            k_rope = _rope(k).reshape(b, n, h, d).transpose(0, 2, 1, 3)
            qh = q.reshape(b, n, h, d).transpose(0, 2, 1, 3)
            kh = k.reshape(b, n, h, d).transpose(0, 2, 1, 3)
            vh = xi.reshape(b, n, h, d).transpose(0, 2, 1, 3)
            k_mean = kh.mean(axis=2, keepdims=True)
            z = 1.0 / (jnp.einsum('bhnd,bhmd->bhnm', qh, k_mean) + 1e-06)
            kv = jnp.einsum('bhnd,bhne->bhde', k_rope, vh) * (1.0 / n)
            attn = jnp.einsum('bhnd,bhde->bhne', q_rope, kv) * z
            attn = attn.transpose(0, 2, 1, 3).reshape(b, n, c)
            v_bcl = vh.transpose(0, 2, 1, 3).reshape(b, n, c).transpose(0, 2, 1)
            attn = attn + _dwconv(v_bcl, lepe_w, lepe_b).transpose(0, 2, 1)
            x = shortcut + attn * act_res @ out_w + out_b
            x = x + _dwconv(x.transpose(0, 2, 1), cpe2_w, cpe2_b).transpose(0, 2, 1)
            xn2 = _ln(x, norm2_g, norm2_b)
            mlp = jax.nn.gelu(xn2 @ fc1_w + fc1_b, approximate=False) @ fc2_w + fc2_b
            return x + mlp
        return _mlla_forward(x, cpe1_w, cpe1_b, norm1_g, norm1_b, in_w, in_b, actp_w, actp_b, dwc_w, dwc_b, qk_w, qk_b, lepe_w, lepe_b, out_w, out_b, cpe2_w, cpe2_b, norm2_g, norm2_b, fc1_w, fc1_b, fc2_w, fc2_b)

    def _L0_attn_b_ref(x, spectral_basis, W_qkv, W_out, a, b, dt):
        import jax, jax.numpy as jnp
        import numpy as np
        N_HEADS = 16
        CHUNK = 64
        TAU = 12.5
        THRESHOLD = 0.5
        N_FHN_STEPS = 2

        def fhn_dynamics(stimulus, a, b, dt, n_steps=N_FHN_STEPS, tau=TAU, threshold=THRESHOLD):
            stim_scale = jnp.clip(jnp.max(jnp.abs(stimulus), axis=-1, keepdims=True), 1e-06, None)
            stim_normed = stimulus / stim_scale
            gate = jax.nn.sigmoid((jnp.abs(stimulus) - threshold) * 10.0)
            I = stim_normed * (0.1 + 0.9 * gate)
            v = jnp.zeros_like(stimulus)
            w = jnp.zeros_like(stimulus)
            alpha = dt / tau
            denom = 1.0 + alpha * b
            for _ in range(n_steps):
                dv_explicit = v - v * v * v / 3.0 - w + I
                v_next = v + dt * dv_explicit
                w_next = (w + alpha * (v_next + a)) / denom
                v = jnp.clip(v_next, -3.0, 3.0)
                w = jnp.clip(w_next, -3.0, 3.0)
            response = v * stim_scale
            return (response, v)

        def chunked_fhn_attention(q, k, v, a, b, dt, chunk_size=CHUNK):
            B, H, T, Dh = q.shape
            n_chunks = (T + chunk_size - 1) // chunk_size
            scale = 1.0 / Dh ** 0.5
            out_chunks = []
            fhn_states = []
            for ci in range(n_chunks):
                s = ci * chunk_size
                e = min(s + chunk_size, T)
                q_c = q[:, :, s:e, :]
                k_c = k[:, :, :e, :]
                v_c = v[:, :, :e, :]
                scores = jnp.einsum('bhtd,bhsd->bhts', q_c, k_c) * scale
                probs = jax.nn.softmax(scores, axis=-1)
                attn_energy = probs.sum(axis=-1)
                stim = jnp.broadcast_to(attn_energy[..., None], (B, H, e - s, Dh))
                fhn_out, fhn_state = fhn_dynamics(stim, a, b, dt)
                fhn_gate = jax.nn.sigmoid(fhn_out.mean(axis=-1))[..., None]
                probs = probs * (0.5 + 0.5 * fhn_gate)
                probs = probs / (probs.sum(axis=-1, keepdims=True) + 1e-08)
                out_chunks.append(jnp.einsum('bhts,bhsd->bhtd', probs, v_c))
                fhn_states.append(fhn_state.mean())
            out = jnp.concatenate(out_chunks, axis=2)
            fhn_state_mean = jnp.stack(fhn_states).mean()
            return (out, fhn_state_mean)
        B, T, E = x.shape
        H = N_HEADS
        Dh = E // H
        qkv = x @ W_qkv.T
        qkv = qkv.reshape(B, T, 3, H, Dh)
        q = jnp.transpose(qkv[:, :, 0], (0, 2, 1, 3))
        k = jnp.transpose(qkv[:, :, 1], (0, 2, 1, 3))
        v = jnp.transpose(qkv[:, :, 2], (0, 2, 1, 3))
        out, fhn_state_mean = chunked_fhn_attention(q, k, v, a, b, dt)
        out = jnp.transpose(out, (0, 2, 1, 3)).reshape(B, T, E)
        out = out @ W_out.T
        return out

    def _L0_ffn_ref(input, w_switch, b_switch, w1, b1, w2, b2):
        import jax, jax.numpy as jnp
        import numpy as np
        D_MODEL = 128
        EXPERT_DIM = 512
        N_EXPERTS = 8
        CAP_FACTOR = 0.5
        B, S, D = input.shape
        T = B * S
        E = b_switch.shape[0]
        capacity = int(CAP_FACTOR * T / E)
        x = input.reshape(T, D)
        logits = x @ w_switch + b_switch
        probs = jax.nn.softmax(logits, axis=-1)
        pmax = probs.max(axis=-1)
        routes = probs.argmax(axis=-1)
        oh = (routes[:, None] == jnp.arange(E)[None, :]).astype(jnp.int32)
        pos = (jnp.cumsum(oh, axis=0) * oh).sum(-1) - 1
        keep = pos < capacity
        slot = jnp.where(keep, routes * capacity + pos, E * capacity)
        buf = jnp.zeros((E * capacity + 1, D), x.dtype).at[slot].set(x)
        buf_e = buf[:E * capacity].reshape(E, capacity, D)
        h = jax.nn.relu(jnp.einsum('ecd,edh->ech', buf_e, w1) + b1[:, None, :])
        y = jnp.einsum('ech,ehd->ecd', h, w2) + b2[:, None, :]
        y_flat = jnp.concatenate([y.reshape(E * capacity, D), jnp.zeros((1, D), x.dtype)], axis=0)
        out = jnp.where(keep[:, None], y_flat[slot], x)
        scale = pmax / jax.lax.stop_gradient(pmax)
        out = out * scale[:, None]
        return out.reshape(B, S, D)

    def _L1_attn_a_ref(x, wq, wk, wv, in_proj_w, in_proj_b, out_w, out_b):
        import jax, jax.numpy as jnp
        import numpy as np
        B, M, D, H = (2, 256, 128, 16)

        def _rope(x):
            b, m, d = x.shape
            i = jnp.arange(d // 2, dtype=jnp.float32)
            theta = 10000.0 ** (-2.0 * (i - 1.0) / d)
            ang = jnp.arange(m, dtype=jnp.float32)[:, None] * theta[None, :]
            c, s = (jnp.cos(ang), jnp.sin(ang))
            xe, xo = (x[..., 0::2], x[..., 1::2])
            ye = xe * c + xo * s
            yo = -xe * s + xo * c
            return jnp.stack([ye, yo], axis=-1).reshape(b, m, d)
        b, m, d = x.shape
        h = H
        hd = d // h
        q = _rope(x @ wq.T)
        k = _rope(x @ wk.T)
        v = _rope(x @ wv.T)
        wqi, wki, wvi = jnp.split(in_proj_w, 3, axis=0)
        bqi, bki, bvi = jnp.split(in_proj_b, 3, axis=0)
        qh = (q @ wqi.T + bqi).reshape(b, m, h, hd)
        kh = (k @ wki.T + bki).reshape(b, m, h, hd)
        vh = (v @ wvi.T + bvi).reshape(b, m, h, hd)
        scores = jnp.einsum('bqhd,bkhd->bhqk', qh, kh) / jnp.sqrt(jnp.float32(hd))
        causal = jnp.tril(jnp.ones((m, m), dtype=bool))
        scores = jnp.where(causal, scores, jnp.float32(-jnp.inf))
        attn = jax.nn.softmax(scores, axis=-1)
        o = jnp.einsum('bhqk,bkhd->bqhd', attn, vh).reshape(b, m, d)
        return o @ out_w.T + out_b

    def _L1_attn_b_ref(x, W0, A_init, B_init, log_lr, Wq, Wk, Wv, Wo, Wg, ln_g, ln_b, ls_g):
        import jax, jax.numpy as jnp
        import numpy as np
        C = 128
        RANK = 8

        def _layernorm(x, g, b, eps=1e-05):
            mu = jnp.mean(x, axis=-1, keepdims=True)
            var = jnp.var(x, axis=-1, keepdims=True)
            return (x - mu) * jax.lax.rsqrt(var + eps) * g + b

        def _reference_tuple_inner(x, W0, A_init, B_init, log_lr, Wq, Wk, Wv, Wo, Wg, ln_g, ln_b, ls_g):
            B, T, _ = x.shape
            h = _layernorm(x, ln_g, ln_b)
            Q = jnp.einsum('btc,dc->btd', h, Wq)
            K = jnp.einsum('btc,dc->btd', h, Wk)
            V = jnp.einsum('btc,dc->btd', h, Wv)
            lr = jnp.minimum(jnp.exp(log_lr), 1.0)
            y0 = jnp.einsum('btc,cd->btd', K, W0) + jnp.einsum('btr,rd->btd', jnp.einsum('btc,cr->btr', K, A_init), B_init)
            error = y0 - V
            loss = jnp.mean(error ** 2)
            gradient = K * error
            grad_cumsum = jnp.cumsum(gradient, axis=1)
            grad_shift = jnp.concatenate([jnp.zeros((B, 1, gradient.shape[-1]), gradient.dtype), grad_cumsum[:, :-1, :]], axis=1)
            correction = Q * lr[None, None, :] * grad_shift
            pos = jnp.arange(1, T + 1, dtype=correction.dtype)
            pos_scale = (1.0 / (1.0 + 0.1 * jnp.log(pos)))[None, :, None]
            out = y0 - correction * pos_scale
            gate = jax.nn.sigmoid(jnp.einsum('btc,dc->btd', x, Wg))
            out = out * gate
            out = jnp.einsum('btc,dc->btd', out, Wo) * ls_g
            return (x + out, loss)
        return _reference_tuple_inner(x, W0, A_init, B_init, log_lr, Wq, Wk, Wv, Wo, Wg, ln_g, ln_b, ls_g)[0]

    def _L1_ffn_ref(inputs_embeds, enc_W, enc_b, s2c_W, s2c_b, rW1, rb1, rW2, rb2, We1, be1, We2, be2, c2s_W, c2s_b, dec_W, dec_b, ln_g, ln_b):
        import jax, jax.numpy as jnp
        import numpy as np
        B, S, D, H, M, E, K = (4, 256, 128, 256, 64, 8, 2)

        def _layernorm(x, g, b, eps=1e-05):
            mu = x.mean(-1, keepdims=True)
            var = ((x - mu) ** 2).mean(-1, keepdims=True)
            return (x - mu) * jax.lax.rsqrt(var + eps) * g + b

        def _forward(inputs_embeds, enc_W, enc_b, s2c_W, s2c_b, rW1, rb1, rW2, rb2, We1, be1, We2, be2, c2s_W, c2s_b, dec_W, dec_b, ln_g, ln_b):
            b, s, _ = inputs_embeds.shape
            spikes_enc = jax.nn.sigmoid(inputs_embeds @ enc_W + enc_b)
            flat = spikes_enc.reshape(b * s, H)
            cont = flat @ s2c_W + s2c_b
            logits = jnp.tanh(cont @ rW1 + rb1) @ rW2 + rb2
            probs = jax.nn.softmax(logits, axis=-1)
            topw, topi = jax.lax.top_k(probs, K)
            w = topw / topw.sum(-1, keepdims=True)
            gates = (jax.nn.one_hot(topi, E, dtype=cont.dtype) * w[..., None]).sum(1)
            h = jax.nn.relu(jnp.einsum('nm,emh->enh', cont, We1) + be1[:, None, :])
            expert_out = jnp.einsum('enh,ehm->enm', h, We2) + be2[:, None, :]
            output_flat = jnp.einsum('enm,ne->nm', expert_out, gates)
            spikes_moe = jax.nn.sigmoid(output_flat @ c2s_W + c2s_b).reshape(b, s, H)
            decoded = jax.nn.sigmoid(spikes_moe @ dec_W + dec_b)
            return _layernorm(decoded, ln_g, ln_b)
        return _forward(inputs_embeds, enc_W, enc_b, s2c_W, s2c_b, rW1, rb1, rW2, rb2, We1, be1, We2, be2, c2s_W, c2s_b, dec_W, dec_b, ln_g, ln_b)
    x = L0_attn_a_x
    x = x + _L0_attn_a_ref(_layernorm(x, axis=-1), L0_attn_a_cpe1_w, L0_attn_a_cpe1_b, L0_attn_a_norm1_g, L0_attn_a_norm1_b, L0_attn_a_in_w, L0_attn_a_in_b, L0_attn_a_actp_w, L0_attn_a_actp_b, L0_attn_a_dwc_w, L0_attn_a_dwc_b, L0_attn_a_qk_w, L0_attn_a_qk_b, L0_attn_a_lepe_w, L0_attn_a_lepe_b, L0_attn_a_out_w, L0_attn_a_out_b, L0_attn_a_cpe2_w, L0_attn_a_cpe2_b, L0_attn_a_norm2_g, L0_attn_a_norm2_b, L0_attn_a_fc1_w, L0_attn_a_fc1_b, L0_attn_a_fc2_w, L0_attn_a_fc2_b)
    x = x + _L0_ffn_ref(_layernorm(x, axis=-1), L0_ffn_w_switch, L0_ffn_b_switch, L0_ffn_w1, L0_ffn_b1, L0_ffn_w2, L0_ffn_b2)
    x = x + _L0_attn_b_ref(_layernorm(x, axis=-1), L0_attn_b_spectral_basis, L0_attn_b_W_qkv, L0_attn_b_W_out, L0_attn_b_a, L0_attn_b_b, L0_attn_b_dt)
    x = x + _L0_ffn_ref(_layernorm(x, axis=-1), L0_ffn_w_switch, L0_ffn_b_switch, L0_ffn_w1, L0_ffn_b1, L0_ffn_w2, L0_ffn_b2)
    x = x + _L1_attn_a_ref(_layernorm(x, axis=-1), L1_attn_a_wq, L1_attn_a_wk, L1_attn_a_wv, L1_attn_a_in_proj_w, L1_attn_a_in_proj_b, L1_attn_a_out_w, L1_attn_a_out_b)
    x = x + _L1_ffn_ref(_layernorm(x, axis=-1), L1_ffn_enc_W, L1_ffn_enc_b, L1_ffn_s2c_W, L1_ffn_s2c_b, L1_ffn_rW1, L1_ffn_rb1, L1_ffn_rW2, L1_ffn_rb2, L1_ffn_We1, L1_ffn_be1, L1_ffn_We2, L1_ffn_be2, L1_ffn_c2s_W, L1_ffn_c2s_b, L1_ffn_dec_W, L1_ffn_dec_b, L1_ffn_ln_g, L1_ffn_ln_b)
    x = x + _L1_attn_b_ref(_layernorm(x, axis=-1), L1_attn_b_W0, L1_attn_b_A_init, L1_attn_b_B_init, L1_attn_b_log_lr, L1_attn_b_Wq, L1_attn_b_Wk, L1_attn_b_Wv, L1_attn_b_Wo, L1_attn_b_Wg, L1_attn_b_ln_g, L1_attn_b_ln_b, L1_attn_b_ls_g)
    x = x + _L1_ffn_ref(_layernorm(x, axis=-1), L1_ffn_enc_W, L1_ffn_enc_b, L1_ffn_s2c_W, L1_ffn_s2c_b, L1_ffn_rW1, L1_ffn_rb1, L1_ffn_rW2, L1_ffn_rb2, L1_ffn_We1, L1_ffn_be1, L1_ffn_We2, L1_ffn_be2, L1_ffn_c2s_W, L1_ffn_c2s_b, L1_ffn_dec_W, L1_ffn_dec_b, L1_ffn_ln_g, L1_ffn_ln_b)
    return x

_drawn_inputs = setup_inputs


def setup_inputs(seed=0):
    import zlib

    import numpy as np

    out = dict(_drawn_inputs(seed))
    spreads = {'L0_attn_a_cpe1_b': (0.0, 0.1),
     'L0_attn_a_norm1_g': (1.0, 0.6),
     'L0_attn_a_norm1_b': (0.0, 0.8),
     'L0_attn_a_in_b': (0.0, 0.8),
     'L0_attn_a_actp_b': (0.0, 0.8),
     'L0_attn_a_dwc_b': (0.0, 0.8),
     'L0_attn_a_qk_b': (0.0, 2.0),
     'L0_attn_a_lepe_b': (0.0, 0.66),
     'L0_attn_a_out_b': (0.0, 0.1),
     'L0_attn_a_cpe2_b': (0.0, 0.269),
     'L0_attn_a_norm2_g': (1.0, 0.6),
     'L0_attn_a_norm2_b': (0.0, 2.0),
     'L0_attn_a_fc1_b': (0.0, 0.975),
     'L0_attn_a_fc2_b': (0.0, 0.28),
     'L0_ffn_b_switch': (0.0, 0.1),
     'L0_ffn_b1': (0.0, 0.358),
     'L0_ffn_b2': (0.0, 0.1),
     'L1_attn_b_B_init': (0.0, 0.8),
     'L1_attn_b_log_lr': (-2.3025851249694824, 0.6),
     'L1_attn_b_ln_g': (1.0, 0.6),
     'L1_attn_b_ln_b': (0.0, 0.8),
     'L1_attn_b_ls_g': (9.999999747378752e-05, 0.6),
     'L1_ffn_enc_b': (0.0, 0.8),
     'L1_ffn_s2c_b': (0.0, 0.8),
     'L1_ffn_rb1': (0.0, 0.8),
     'L1_ffn_rb2': (0.0, 0.8),
     'L1_ffn_be1': (0.0, 2.0),
     'L1_ffn_be2': (0.0, 2.0),
     'L1_ffn_c2s_b': (0.0, 2.0),
     'L1_ffn_dec_b': (0.0, 0.1),
     'L1_ffn_ln_g': (1.0, 0.2),
     'L1_ffn_ln_b': (0.0, 0.452)}
    factors = {'L0_attn_a_in_w': 8.0,
     'L0_attn_a_actp_w': 4.841,
     'L0_attn_a_dwc_w': 8.0,
     'L0_attn_a_qk_w': 8.0,
     'L0_attn_a_lepe_w': 8.0,
     'L0_attn_a_out_w': 5.665,
     'L1_attn_a_wq': 8.0,
     'L1_attn_a_wk': 8.0,
     'L1_attn_a_wv': 8.0,
     'L1_attn_a_in_proj_w': 8.0,
     'L1_attn_a_in_proj_b': 8.0,
     'L1_attn_a_out_w': 8.0,
     'L1_attn_a_out_b': 8.0,
     'L1_attn_b_W0': 8.0,
     'L1_attn_b_A_init': 8.0,
     'L1_attn_b_Wq': 8.0,
     'L1_attn_b_Wk': 8.0,
     'L1_attn_b_Wv': 8.0,
     'L1_attn_b_Wo': 8.0,
     'L1_attn_b_Wg': 8.0,
     'L1_ffn_enc_W': 8.0,
     'L1_ffn_s2c_W': 8.0,
     'L1_ffn_rW1': 8.0,
     'L1_ffn_rW2': 8.0,
     'L1_ffn_We1': 8.0,
     'L1_ffn_We2': 8.0,
     'L1_ffn_c2s_W': 8.0}
    for name, (base, spread) in spreads.items():
        noise = np.random.default_rng([zlib.crc32(name.encode()), seed]).standard_normal(out[name].shape)
        drawn = base * np.exp(spread * noise) if base else spread * noise
        out[name] = jnp.asarray(drawn.astype(out[name].dtype))
    for name, factor in factors.items():
        out[name] = (out[name] * factor).astype(out[name].dtype)
    return out
```

```python
from contextlib import ExitStack

import concourse.bass as bass
from concourse import mybir

F32 = mybir.dt.float32
BF16 = mybir.dt.bfloat16
F16 = mybir.dt.float16
I32 = mybir.dt.int32
ALU = mybir.AluOpType
ACT = mybir.ActivationFunctionType
AX = mybir.AxisListType.X

RUN = ["mlla", "moe", "fhn", "moe", "causal", "gated", "fastw", "gated"]

P = 128
B, N, C = 2, 1024, 128
T = B * N
NT = T // P
CW = 512
NC = T // CW
TC = CW // P
H, D = 16, 8
NG = 4
GROUPS = B * NG
KT = N // P
E, CAP, HID = 8, 128, 512
SLOTS = E * CAP
M = 64
NEG = -1.0e30
UNITS = 12
MAXU = 48
RSQRT_SEED = 1597463007.0

COLS = [
    [("ident", 128), ("rot", 128), ("rotT", 128), ("blockm", 128), ("headm", 16),
     ("cpe1", 4), ("g1", 1), ("bn1", 1), ("inb", 1), ("actb", 1), ("dwc", 4), ("qb", 1), ("kb", 1), ("lepe", 4),
     ("outb", 1), ("cpe2", 4), ("g2", 1), ("bn2", 1), ("fc1b", 4), ("fc2b", 1),
     ("in", 128), ("actp", 128), ("qw", 128), ("kw", 128), ("ow", 128), ("fc1", 512), ("fc2", 512)],
    [("pcol", 8), ("wsw", 8), ("b1", 32), ("w1", E * HID),
     ("w2", 4 * E * 128)],
    [("fq", 128), ("fk", 128), ("fv", 128), ("fo", 128), ("fabd", 3),
     ("rq", 128), ("rqs", 128), ("rk", 128), ("rks", 128), ("rv", 128), ("rvs", 128),
     ("pq", 128), ("pk", 128), ("pv", 128), ("pqb", 1), ("pkb", 1), ("co", 128), ("cob", 1),
     ("W0", 128), ("AT", 128), ("Bi", 128), ("Wq", 128), ("Wk", 128), ("Wv", 128), ("Wo", 128), ("Wg", 128),
     ("lr", 1), ("lng", 1), ("lnb", 1), ("lsg", 1),
     ("enc", 256), ("encb", 2), ("s2c", 128), ("s2cb", 1), ("rW1", 64), ("rb1", 1), ("rW2", 8), ("We1", 1024),
     ("be1", 8), ("We2", 512), ("be2", 64), ("c2s", 256), ("c2sb", 2), ("dec", 256), ("decb", 1)],
]
ROWS = [("bsw", 8), ("rev", 8), ("base", 8), ("b2", E * 128), ("rb2", 8), ("fing", 128), ("finb", 128), ("pos", N),
        ("vb", 128), ("one", 1)]


def places(cols, start=0):
    at = {}
    for name, width in cols:
        at[name] = (start, width)
        start += width
    return at, start


W_AT, W_END = {}, [0]
for _part in COLS:
    _a, _e = places(_part, W_END[-1])
    W_AT.update(_a)
    W_END.append(_e)
R_AT, R_WIDTH = places(ROWS)
K_AT, K_WIDTH = places([("cmask", P), ("fmask", P), ("tri", P), ("ones", P), ("iota", SLOTS), ("esel", E * P)])
TAB_AT, TAB_WIDTH = places([("cosT", N), ("sinT", N)])


class Semaphores:
    pass


def build(nc, x_d, w_d, r_d, k_d, tab_d, out_d):
    with ExitStack() as ctx:
        def sb(name, shape, dt):
            return ctx.enter_context(nc.sbuf_tensor(name, shape, dt))

        def sem(name):
            return ctx.enter_context(nc.semaphore(name))

        s = Semaphores()
        s.k_in = sem("k_in")
        s.tab_in = sem("tab_in")
        s.x_in = sem("x_in")
        s.w_in0 = sem("w_in0")
        s.w_in1 = sem("w_in1")
        s.w_in2 = sem("w_in2")
        s.row_in = sem("row_in")
        s.dve_chain = sem("dve_chain")
        s.out_done = sem("out_done")
        s.ln_tn = sem("ln_tn")
        s.uT = sem("uT")
        s.u = sem("u")
        s.tokT = sem("tokT")
        s.tok = sem("tok")
        s.y = sem("y")
        s.resT = sem("resT")
        s.res = sem("res")
        s.c1 = sem("c1")
        s.lin = sem("lin")
        s.silu = sem("silu")
        s.xi = sem("xi")
        s.xc = sem("xc")
        s.v = sem("v")
        s.kq_relu = sem("kq_relu")
        s.kq_min = sem("kq_min")
        s.kq_exp = sem("kq_exp")
        s.qk = sem("qk")
        s.rden_den = sem("rden_den")
        s.rden_ev = sem("rden_ev")
        s.kmean = sem("kmean")
        s.vtokT = sem("vtokT")
        s.vtok = sem("vtok")
        s.gacc = sem("gacc")
        s.gev = sem("gev")
        s.z_st = sem("z_st")
        s.z_ld = sem("z_ld")
        s.z_rc = sem("z_rc")
        s.z_fs = sem("z_fs")
        s.z_fl = sem("z_fl")
        s.mnum = sem("mnum")
        s.att = sem("att")
        s.olin = sem("olin")
        s.x2 = sem("x2")
        s.x3 = sem("x3")
        s.fc1 = sem("fc1")
        s.hid = sem("hid")
        s.fc2 = sem("fc2")
        s.lg = sem("lg")
        s.oh = sem("oh")
        s.cum = sem("cum")
        s.slot = sem("slot")
        s.parts = sem("parts")
        s.slotT = sem("slotT")
        s.slotrow = sem("slotrow")
        s.slot_st = sem("slot_st")
        s.slot_ld = sem("slot_ld")
        s.onehot = sem("onehot")
        s.disp = sem("disp")
        s.xg = sem("xg")
        s.h_mm = sem("h_mm")
        s.h_act = sem("h_act")
        s.y_mm = sem("y_mm")
        s.yparts = sem("yparts")
        s.st_oh = sem("st_oh")
        s.comb = sem("comb")
        s.qkv_mm = sem("qkv_mm")
        s.q_sb = sem("q_sb")
        s.k_sb = sem("k_sb")
        s.vt_mm = sem("vt_mm")
        s.v_sb = sem("v_sb")
        s.v_st0 = sem("v_st0")
        s.v_st1 = sem("v_st1")
        s.hi = sem("hi")
        s.mid = sem("mid")
        s.lo = sem("lo")
        s.qs_st = sem("qs_st")
        s.rope_mm = sem("rope_mm")
        s.rope = sem("rope")
        s.pm_ld0 = sem("pm_ld0")
        s.pm_ld1 = sem("pm_ld1")
        s.pe_ld0 = sem("pe_ld0")
        s.pe_ld1 = sem("pe_ld1")
        s.rows_ld0 = sem("rows_ld0")
        s.rows_ld1 = sem("rows_ld1")
        s.mx_mm = sem("mx_mm")
        s.mx_red = sem("mx_red")
        s.mx_fin = sem("mx_fin")
        s.mT = sem("mT")
        s.m_sp = sem("m_sp")
        s.st_mm = sem("st_mm")
        s.pexp = sem("pexp")
        s.pmask = sem("pmask")
        s.av_mm = sem("av_mm")
        s.o_sb = sem("o_sb")
        s.o_st0 = sem("o_st0")
        s.o_st1 = sem("o_st1")
        s.fd_ld = sem("fd_ld")
        s.f_sig = sem("f_sig")
        s.f_pre = sem("f_pre")
        s.f_out = sem("f_out")
        s.f_st = sem("f_st")
        s.fb_ld = sem("fb_ld")
        s.oT = sem("oT")
        s.ofin = sem("ofin")
        s.w0x = sem("w0x")
        s.w0 = sem("w0")
        s.lwk = sem("lwk")
        s.lks = sem("lks")
        s.lerr = sem("lerr")
        s.lgrad = sem("lgrad")
        s.lq = sem("lq")
        s.lv = sem("lv")
        s.lo1 = sem("lo1")
        s.lgm = sem("lgm")
        s.lwo = sem("lwo")
        s.qk_mm = sem("qk_mm")
        s.ktokT = sem("ktokT")
        s.ktok = sem("ktok")
        s.hi2 = sem("hi2")
        s.rs2 = sem("rs2")
        s.mid2 = sem("mid2")
        s.rs = sem("rs")
        s.rope_t = sem("rope_t")
        s.v_one = sem("v_one")
        s.e_zero = sem("e_zero")
        s.m_zero = sem("m_zero")
        s.one_ld = sem("one_ld")
        s.mx_cmb = sem("mx_cmb")
        s.m_pt = sem("m_pt")
        s.x_dn = sem("x_dn")
        s.ly0 = sem("ly0")
        s.lgs = sem("lgs")
        s.llr = sem("llr")
        s.prep = sem("prep")
        s.e_mm = sem("e_mm")
        s.e_sp = sem("e_sp")
        s.s_mm = sem("s_mm")
        s.cont = sem("cont")
        s.r_mm = sem("r_mm")
        s.th = sem("th")
        s.l_mm = sem("l_mm")
        s.d12 = sem("d12")
        s.sg = sem("sg")
        s.gates = sem("gates")
        s.gT = sem("gT")
        s.g_zero = sem("g_zero")
        s.gTs = sem("gTs")
        s.x_mm = sem("x_mm")
        s.x_rl = sem("x_rl")
        s.g_mm = sem("g_mm")
        s.x_h = sem("x_h")
        s.a_mm = sem("a_mm")
        s.a_sb = sem("a_sb")
        s.c_mm = sem("c_mm")
        s.c_sb = sem("c_sb")
        s.dd_mm = sem("dd_mm")
        s.dd_sb = sem("dd_sb")

        wt = sb("weights", [P, W_END[-1]], F32)
        rows = sb("rows", [P, R_WIDTH], F32)
        x = sb("x", [P, NT, C], F32)
        tn = sb("tn", [P, 2, NT, C], F32)
        u = sb("u", [P, T], F32)
        heap = sb("heap", [P, 10, T], F32)
        ps = ctx.enter_context(nc.psum_tensor("ps", [P, 8, CW], F32))
        st6 = sb("st6", [P, NT, 6], F32)
        sm = sb("sm", [P, 8, NT], F32)
        identb = sb("identb", [P, P], BF16)
        maskb = sb("maskb", [P, 2, P], BF16)
        mx = sb("mx", [P, 2, 2, 2, KT], F32)
        mneg = sb("mneg", [P, 32], F32)
        msq = sb("msq", [P, 2, 3, 16], BF16)
        mrs = sb("mrs", [P, 32], F32)
        msp = sb("msp", [96, 2, P], BF16)
        small = sb("small", [P, 64], F32)

        qk_d = nc.dram_tensor("qk", (GROUPS, 4, 2, 48, N), BF16, kind="Internal").ap()
        vs_d = nc.dram_tensor("vs", (GROUPS, P, KT * 128), F32, kind="Internal").ap()
        nd_d = nc.dram_tensor("nd", (GROUPS, 4, D + 1, N), F32, kind="Internal").ap()
        den_d = nc.dram_tensor("den", (GROUPS, 4, N), F32, kind="Internal").ap()
        fac_d = nc.dram_tensor("fac", (GROUPS, 4, N), F32, kind="Internal").ap()
        trib = sb("trib", [P, P], BF16)
        onesb = sb("onesb", [P, P], BF16)
        iota16 = sb("iota16", [P, SLOTS], F16)
        eselb = sb("eselb", [P, E * P], BF16)
        orow = sb("orow", [GROUPS * 4, N], BF16)
        ohb = sb("ohb", [P, NT * E], BF16)
        gate = sb("gate", [P, 6, NT * E], F32)
        g24 = sb("g24", [P, NT * 24], BF16)
        mats = sb("mats", [P, 6, P], F32)
        slot_d = nc.dram_tensor("slotrow", (NT, P), F16, kind="Internal").ap()

        consts = heap[:, 6:8, :].rearrange("p a b -> p (a b)")[:, 0:K_WIDTH]

        def w(name, rows_=P):
            a, n = W_AT[name]
            return wt[0:rows_, a:a + n]

        def wc(name, j, n=P, rows_=P):
            a, _ = W_AT[name]
            return wt[0:rows_, a + j * n:a + j * n + n]

        def kw(name):
            a, n = K_AT[name]
            return consts[:, a:a + n]

        def row(name):
            a, n = R_AT[name]
            return rows[:, a:a + n]

        def A(k, a=0, b=T):
            return heap[:, k, a:b]

        def ch(c):
            return c * CW, (c + 1) * CW

        def halves(k):
            v = heap[:, k, :].bitcast(BF16)
            return v[:, 0:T], v[:, T:2 * T]

        def bank(b, a=0, e=CW):
            return ps[:, b, a:e]

        ident = w("ident")

        plan, ln, tr, tk, yy = [], 0, 0, 0, 0
        seen = {}
        for kind in RUN:
            plan.append((kind, seen.get(kind, 0), ln, tr, tk, yy))
            seen[kind] = seen.get(kind, 0) + 1
            ln += {"mlla": 3, "gated": 2, "fastw": 2}.get(kind, 1)
            tr += {"mlla": 3, "fastw": 2}.get(kind, 1)
            tk += {"mlla": 2, "gated": 1}.get(kind, 0)
            yy += 0 if kind == "gated" else 1
        attn_of = {}
        for kind in RUN:
            if kind in ("fhn", "causal"):
                attn_of[kind] = len(attn_of)

        block = ctx.enter_context(nc.Block())

        def pbuf(k):
            return heap[:, k, :].rearrange("p (j q) -> p j q", j=4)

        flat = heap[:, :, :].rearrange("p k t -> p (k t)").bitcast(BF16)

        def operands(k):
            a = 2 * 2 * T + k * 6 * N
            return flat[:, a:a + 6 * N].rearrange("p (j t) -> p j t", j=6)

        def qe(par):
            return operands(par)[:, 0:4, :]

        def ke(par):
            return operands(par)[:, 4:6, :]

        def qm(par):
            return operands(2 + par)[:, 0:4, :]

        def km(par):
            return operands(2 + par)[:, 4:6, :]

        def loads(k, i, jp):
            for o, tile in ((0, 2 * jp), (1, 4)):
                yield (operands(k)[64 * jp:64 * jp + 48, tile:tile + 2, :],
                       qk_d[i].rearrange("(j e) o r t -> e o r j t", e=2)[jp, o])

        def zeroed(k):
            a = 2 * T + k * 3 * N
            return heap[:, :, :].rearrange("p k t -> p (k t)")[:, a:a + 3 * N]

        def vst(par):
            return heap[:, 8, par * 1024:(par + 1) * 1024].rearrange("p (k j r) -> p k j r", k=KT, j=4)

        def oraw(par):
            return heap[:, 9, par * N:(par + 1) * N]

        QH, QMI = halves(2)
        QL, KH = halves(3)
        KMI, KL = halves(4)
        SPLITQ = [QH, QH, QMI, QMI, QH, QL]
        SPLITK = [KH, KMI, KH, KMI, KL, KH]

        def onehot(t):
            return heap[:, 3, :].bitcast(BF16).rearrange("p (k s) -> p k s", k=4)[:, t % 4, :]

        def back(e):
            return halves(7 + 2 * (e % 4 // 2))[e % 2]

        def hbuf(e):
            return heap[:, 6, 1024 + (e % 2) * CW:1024 + (e % 2) * CW + CW].rearrange("p (j q) -> p j q", j=4)

        def vp(k):
            return heap[:, 7 + k, :].rearrange("p (t h r) -> p t h r", t=TC, h=H)

        w_in = (s.w_in0, s.w_in1, s.w_in2)
        PART = {"mlla": 0, "moe": 1}

        pm_ld, pe_ld, rows_ld = (s.pm_ld0, s.pm_ld1), (s.pe_ld0, s.pe_ld1), (s.rows_ld0, s.rows_ld1)
        v_st, o_st = (s.v_st0, s.v_st1), (s.o_st0, s.o_st1)

        def strips():
            k = 0
            for j2 in range(2):
                for qt in range(KT):
                    for kc in range(1 + qt // 4):
                        width = min(CW, (qt + 1) * P - kc * CW)
                        for jp in range(2):
                            yield k, jp, j2, qt, kc, width
                            k += 1

        STRIPS = list(strips())

        STEPS = [(qh, kt, max(0, kt - 4 * qh) * P) for qh in range(2) for kt in range(4 * qh + 4)]

        @block.sync
        def _(sp):
            sp.dma_start(x[:, :, :], x_d.rearrange("(t p) c -> p t c", p=P)).then_inc(s.x_in, 16)
            for k in range(3):
                sp.dma_start(wt[:, W_END[k]:W_END[k + 1]], w_d[:, W_END[k]:W_END[k + 1]]).then_inc(w_in[k], 16)
                if k == 0:
                    sp.dma_start(consts, k_d).then_inc(s.k_in, 16)
                    sp.dma_start(rows[:, :], r_d.partition_broadcast(P)).then_inc(s.row_in, 16)

            def mlla():
                sp.wait_ge(s.prep, 1)
                sp.wait_ge(s.rden_ev, 4)
                for b in range(B):
                    sp.dma_start(den_d[b * NG:(b + 1) * NG, :, :].rearrange("g j t -> (g j) t"),
                                 heap[0:H, 8, b * N:(b + 1) * N]).then_inc(s.z_st, 16)
                sp.wait_ge(s.z_st, 32)
                sp.dma_start(A(7, 0, 256), den_d.rearrange("i j t -> (i j t)").rearrange("(p f) -> p f", p=P)
                             ).then_inc(s.z_ld, 16)
                sp.wait_ge(s.z_rc, 1)
                sp.dma_start(fac_d.rearrange("i j t -> (i j t)").rearrange("(p f) -> p f", p=P),
                             A(7, 256, 512)).then_inc(s.z_fs, 16)
                sp.wait_ge(s.z_fs, 16)
                broadcast_fac(6, s.z_fl)

            def broadcast_fac(slot, done):
                for b in range(B):
                    heads = fac_d[b * NG:(b + 1) * NG].rearrange("g j t -> (g j) t").unsqueeze(1)
                    sp.dma_start(heap[:, slot, b * N:(b + 1) * N], heads.broadcast_to((H, D, N))).then_inc(done, 16)

            def moe(n):
                sp.wait_ge(s.slotrow, n + 1)
                sp.dma_start(slot_d, halves(8)[1].bitcast(F16)[0:NT, 0:P]).then_inc(s.slot_st, 16)
                sp.wait_ge(s.slot_st, 16 * (n + 1))
                sp.dma_start(halves(8)[0].bitcast(F16), slot_d.rearrange("t p -> (t p)").partition_broadcast(P)
                             ).then_inc(s.slot_ld, 16)

            def stage_exp(a, i, par):
                for jp in range(2):
                    for dst, src in loads(par, i, jp):
                        sp.dma_start(dst, src).then_inc(pe_ld[par], 16)
                sp.dma_start(heap[:, 8, par * 1024:(par + 1) * 1024], vs_d[i]).then_inc(pe_ld[par], 16)
                sp.wait_ge(s.m_sp, GROUPS * a + i + 1)
                for jp in range(2):
                    sp.dma_start(qe(par)[64 * jp + 48:64 * jp + 51, 2 * jp:2 * jp + 2, :],
                                 msp[48 * jp:48 * jp + 48, par, :]).then_inc(rows_ld[par], 16)

            def store_out(a, i, par):
                sp.wait_ge(s.o_sb, 2 * (GROUPS * a + i) + 3)
                for j in range(4):
                    sp.dma_start(nd_d[i, j], oraw(par)[32 * j:32 * j + D + 1]).then_inc(o_st[par], 16)

            def attention(a):
                for c in range(NC):
                    b, k0 = c // 2, (c % 2) * TC
                    sp.wait_ge(s.v_sb, NC * a + c + 1)
                    for t in range(TC):
                        sp.dma_start(vs_d[b * NG:(b + 1) * NG, :, (k0 + t) * 128:(k0 + t + 1) * 128]
                                     .rearrange("g p r -> p g r"),
                                     heap[:, 7 + c % 2, t * 512:(t + 1) * 512].rearrange("p (g r) -> p g r", g=NG)
                                     ).then_inc(v_st[c % 2], 16)
                sp.wait_ge(s.lo, 2 * (a + 1))
                for k in range(6):
                    for o, src in enumerate((SPLITQ[k], SPLITK[k])):
                        for b in range(B):
                            sp.dma_start(qk_d[b * NG:(b + 1) * NG, :, o, 8 * k:8 * k + 8, :]
                                         .rearrange("g j d t -> (g j) d t"),
                                         src[:, b * N:(b + 1) * N]).then_inc(s.qs_st, 16)
                sp.wait_ge(s.qs_st, 16 * 24 * (a + 1))
                for k in range(2):
                    sp.wait_ge(v_st[k], 16 * TC * 2 * (a + 1))
                sp.wait_ge(s.e_zero, 2 * (a + 1))
                for par in range(2):
                    for jp in range(2):
                        sp.dma_start(ke(par)[64 * jp + 48:64 * jp + 51, :, :], orow[0:6, :]).then_inc(s.one_ld, 16)
                stage_exp(a, 0, 0)
                stage_exp(a, 1, 1)
                with sp.Fori(0, GROUPS // 2 - 1) as it:
                    for par in range(2):
                        i = 2 * it + par
                        store_out(a, i, par)
                        sp.wait_ge(s.av_mm, UNITS * GROUPS * a + UNITS * (i + 1))
                        stage_exp(a, i + 2, par)
                for i in (GROUPS - 2, GROUPS - 1):
                    store_out(a, i, i % 2)
                for k in range(2):
                    sp.wait_ge(o_st[k], 64 * (GROUPS // 2 * (a + 1) + 1))
                sp.wait_ge(s.pm_ld0, 64 * 5 * (a + 1))
                sp.wait_ge(s.pm_ld1, 64 * 4 * (a + 1))
                sp.dma_start(A(5, 0, 256), nd_d[:, :, D, :].rearrange("i j t -> (i j) t")).then_inc(s.fd_ld, 16)
                for b in range(B):
                    sp.dma_start(A(2, b * N, (b + 1) * N),
                                 nd_d[b * NG:(b + 1) * NG, :, 0:D, :].rearrange("g j d t -> (g j) d t")
                                 ).then_inc(s.fd_ld, 16)
                sp.wait_ge(s.f_out, a + 1)
                sp.dma_start(fac_d.rearrange("i j t -> (i j t)").rearrange("(p f) -> p f", p=P),
                             A(5, 256, 512)).then_inc(s.f_st, 16)
                sp.wait_ge(s.f_st, 16 * (a + 1))
                broadcast_fac(3, s.fb_ld)

            for bi, (kind, n, ln0, tr0, tk0, y0) in enumerate(plan):
                if kind == "causal":
                    sp.wait_ge(s.res, NC * bi)
                    sp.dma_start(A(2), tab_d).then_inc(s.tab_in, 16)
                if kind == "mlla":
                    mlla()
                elif kind == "moe":
                    moe(n)
                elif kind in attn_of:
                    attention(attn_of[kind])
            nout = len(RUN)
            sp.wait_ge(s.res, NC * nout)
            sp.dma_start(out_d.rearrange("(t p) c -> p t c", p=P), x[:, :, :]).then_inc(s.out_done, 16)
            sp.wait_ge(s.out_done, 16)


        def chain(eng, sem):
            count = [0]

            def link(ins):
                count[0] += 1
                ins.then_inc(sem, 1)
                eng.wait_ge(sem, count[0])
            return link

        def bc(ap, shape):
            return ap.broadcast_to(shape)

        @block.tensor
        def _(pe):
            def ln_T(n, k):
                pe.wait_ge(s.u, NC * k)
                for c in range(NC):
                    pe.wait_ge(s.ln_tn, NC * n + c + 1)
                    for t in range(TC):
                        m = pe.transpose(bank(c, t * P, t * P + P), tn[:, n % 2, TC * c + t, :], ident)
                    m.then_inc(s.uT, 1)

            def tok_T(k, slot, ready, count):
                for c in range(NC):
                    pe.wait_ge(ready, count(c))
                    for t in range(TC):
                        a = (TC * c + t) * P
                        m = pe.transpose(bank(4 + c, t * P, t * P + P), A(slot, a, a + P), ident)
                    m.then_inc(s.tokT, 1)

            def res_T(k, slot):
                for c in range(NC):
                    pe.wait_ge(s.y, NC * k + c + 1)
                    for t in range(TC):
                        a = (TC * c + t) * P
                        m = pe.transpose(bank(4 + c, t * P, t * P + P), A(slot, a, a + P), ident)
                    m.then_inc(s.resT, 1)

            def mlla(n, ln0, tr0, tk0, y0):
                tok_T(tk0, 0, s.c1, lambda c: c // 2 + 1)
                ln_T(ln0 + 1, tr0 + 1)
                for c in range(NC):
                    pe.wait_ge(s.u, NC * (tr0 + 1) + c + 1)
                    pe.matmul(bank(c), w("actp"), A(1, *ch(c)), start=True, stop=True)
                    pe.matmul(bank(4 + c), w("in"), A(1, *ch(c)), start=True, stop=True).then_inc(s.lin, 1)
                for c in range(NC):
                    pe.wait_ge(s.v, c // 2 + 1)
                    pe.wait_ge(s.silu, c + 1)
                    pe.matmul(bank(c), w("qw"), A(5, *ch(c)), start=True, stop=True)
                    pe.matmul(bank(4 + c), w("kw"), A(5, *ch(c)), start=True, stop=True).then_inc(s.qk_mm, 1)
                for c in range(NC):
                    pe.wait_ge(s.kq_min, 2 * c + 2)
                    pe.wait_ge(s.kq_relu, 2 * c + 2)
                    for t in range(TC):
                        a = (TC * c + t) * P
                        m = pe.transpose(bank(c, t * P, t * P + P), A(5, a, a + P), ident)
                    m.then_inc(s.vtokT, 1)
                for c in range(NC):
                    pe.wait_ge(s.qk, 2 * c + 2)
                    for t in range(TC):
                        a = (TC * c + t) * P
                        m = pe.transpose(bank(4 + c, t * P, t * P + P), A(4, a, a + P), ident)
                    m.then_inc(s.ktokT, 1)
                for c in range(NC):
                    pe.wait_ge(s.kmean, c // 2 + 1)
                    pe.wait_ge(s.vtok, c + 1)
                    pe.matmul(ps[0:H, c, :], small[:, 16 + H * (c // 2):16 + H * (c // 2) + H], A(3, *ch(c)),
                              start=True, stop=True).then_inc(s.rden_den, 1)
                pe.wait_ge(s.ktok, NC)
                for b in range(B):
                    for t in range(KT):
                        a = b * N + t * P
                        m = pe.matmul(bank(4 + b, 0, P), A(1, a, a + P), A(9, a, a + P),
                                      start=(t == 0), stop=(t == KT - 1))
                    m.then_inc(s.gacc, 1)
                for b in range(B):
                    pe.wait_ge(s.gev, b + 1)
                    pe.matmul(bank(4 + b, P, 2 * P), w("rot"), mats[:, b, :], start=True, stop=True).then_inc(s.gacc, 1)
                for b in range(B):
                    pe.wait_ge(s.gev, B + b + 1)
                    pe.matmul(bank(4 + b, 2 * P, 3 * P), w("rotT"), mats[:, 2 + b, :],
                              start=True, stop=True).then_inc(s.gacc, 1)
                for c in range(NC):
                    pe.wait_ge(s.gev, 2 * B + c // 2 + 1)
                    pe.wait_ge(s.rden_ev, c + 1)
                    pe.matmul(bank(c), mats[:, 4 + c // 2, :], A(3, *ch(c)), start=True, stop=True).then_inc(s.mnum, 1)
                for c in range(NC):
                    pe.wait_ge(s.att, c + 1)
                    pe.matmul(bank(4 + c), w("ow"), A(4, *ch(c)), start=True, stop=True).then_inc(s.olin, 1)
                tok_T(tk0 + 1, 5, s.x3, lambda c: c // 2 + 1)
                ln_T(ln0 + 2, tr0 + 2)
                pe.wait_ge(s.u, NC * (tr0 + 3))

                def fc1(c):
                    for j in range(4):
                        if c:
                            pe.wait_ge(s.hid, 4 * (c - 1) + j + 1)
                        pe.matmul(bank(j), wc("fc1", j), A(1, *ch(c)), start=True, stop=True).then_inc(s.fc1, 1)

                def fc2(c):
                    for j in range(4):
                        pe.wait_ge(s.hid, 4 * c + j + 1)
                        m = pe.matmul(bank(4 + c), wc("fc2", j), A(6 + c % 2, j * CW, j * CW + CW),
                                      start=(j == 0), stop=(j == 3))
                    m.then_inc(s.fc2, 1)

                for c in range(NC + 1):
                    if c < NC:
                        fc1(c)
                    if c:
                        fc2(c - 1)
                res_T(y0, 8)

            def moe(n, ln0, tr0, tk0, y0):
                pe.wait_ge(s.u, NC * (tr0 + 1))
                for t in range(NT):
                    m = pe.matmul(bank(4, t * E, t * E + E), u[:, t * P:t * P + P], w("wsw"), start=True, stop=True)
                m.then_inc(s.lg, 1)
                pe.wait_ge(s.oh, n + 1)
                pe.matmul(bank(5, 0, NT * E), trib[:, :], ohb[:, :], start=True, stop=False)
                for k in range(1, NT):
                    m = pe.matmul(bank(5, k * E, NT * E), onesb[:, :], ohb[:, 0:(NT - k) * E],
                                  start=False, stop=(k == NT - 1))
                m.then_inc(s.cum, 1)
                pe.wait_ge(s.slot, n + 1)
                pe.transpose(ps[0:NT, 5, 256:384], sm[:, 7, :], ident).then_inc(s.slotT, 1)
                parts = (halves(0)[0], halves(0)[1], halves(1)[0])
                pe.wait_ge(s.parts, n + 1)
                for t in range(NT):
                    pe.wait_ge(s.onehot, NT * n + t + 1)
                    for half in range(2):
                        for k in range(3):
                            m = pe.matmul(bank(6 + half), parts[k][:, t * P:t * P + P],
                                          onehot(t)[:, half * CW:half * CW + CW],
                                          start=(t == 0 and k == 0), stop=(t == NT - 1 and k == 2))
                    m.then_inc(s.disp, 1)
                pe.wait_ge(s.xg, 2 * (n + 1))

                def up(e):
                    if e >= 2:
                        pe.wait_ge(s.h_act, 4 * (E * n + e - 1))
                    for j in range(4):
                        m = pe.matmul(bank(e % 2, j * P, j * P + P), wc("w1", 4 * e + j),
                                      A(4, e * CAP, e * CAP + CAP), start=True, stop=True)
                    m.then_inc(s.h_mm, 1)

                def down(e):
                    pe.wait_ge(s.h_act, 4 * (E * n + e + 1))
                    for j in range(4):
                        m = pe.matmul(bank(2 + e // 4, (e % 4) * P, (e % 4) * P + P), hbuf(e)[:, j, :],
                                      wc("w2", 4 * e + j), start=(j == 0), stop=(j == 3))
                    m.then_inc(s.y_mm, 1)

                for e in range(E + 1):
                    if e < E:
                        up(e)
                    if e:
                        down(e - 1)
                yp = heap[:, 5, :].bitcast(BF16)
                pe.wait_ge(s.yparts, 2 * (n + 1))
                for e in range(E):
                    pe.wait_ge(s.st_oh, E * n + e + 1)
                    for k in range(3):
                        a = k * SLOTS + e * CAP
                        for c in range(NC):
                            m = pe.matmul(bank(c), yp[:, a:a + CAP], back(e)[:, c * CW:c * CW + CW],
                                          start=(e == 0 and k == 0), stop=(e == E - 1 and k == 2))
                    m.then_inc(s.comb, 1)
                res_T(y0, 0)

            def attention(a, kind, tr0, y0):
                if kind == "fhn":
                    for c in range(NC):
                        pe.wait_ge(s.u, NC * tr0 + c + 1)
                        pe.matmul(bank(c), w("fq"), u[:, c * CW:c * CW + CW], start=True, stop=True)
                        pe.matmul(bank(4 + c), w("fk"), u[:, c * CW:c * CW + CW],
                                  start=True, stop=True).then_inc(s.qkv_mm, 1)
                else:
                    pe.wait_ge(s.u, NC * (tr0 + 1))
                    for k, (wa, wb) in enumerate((("rq", "rqs"), ("rk", "rks"), ("rv", "rvs"))):
                        for c in range(NC):
                            p = NC * k + c
                            if p >= 4:
                                pe.wait_ge(s.rope_t, p - 3)
                            pe.matmul(bank(2 * p % 8), w(wa), u[:, c * CW:c * CW + CW], start=True, stop=True)
                            pe.matmul(bank(2 * p % 8 + 1), w(wb), u[:, c * CW:c * CW + CW],
                                      start=True, stop=True).then_inc(s.rope_mm, 1)
                    pe.wait_ge(s.rope_t, 3 * NC)
                    for c in range(NC):
                        pe.wait_ge(s.rope, NC + c + 1)
                        pe.matmul(bank(c), w("pq"), A(5, *ch(c)), start=True, stop=True)
                        pe.matmul(bank(4 + c), w("pk"), A(6, *ch(c)), start=True, stop=True).then_inc(s.qkv_mm, 1)
                    pe.wait_ge(s.rope, 3 * NC)
                for c in range(NC):
                    pe.wait_ge(s.q_sb, NC * a + c + 1)
                    for t in range(TC):
                        k = (TC * c + t) * P
                        lhs = u[:, k:k + P] if kind == "fhn" else A(9, k, k + P)
                        m = pe.matmul(bank(c, t * P, t * P + P), lhs, w("fv" if kind == "fhn" else "pv"),
                                      start=True, stop=True)
                    m.then_inc(s.vt_mm, 1)
                pe.wait_ge(s.k_sb, NC * (a + 1))
                pe.wait_ge(s.v_sb, NC * (a + 1))

                def max_pair(g, par, k):
                    for _, jp, j2, qt, kc, width in STRIPS[k:k + 2]:
                        if not (isinstance(g, int) and g == 0 and k + jp < 3):
                            pe.wait_ge(s.mx_red, MAXU * g + (k + jp - 2))
                        last = kc == qt // 4
                        m = pe.matmul(bank(5 + (k + jp) % 3, 0, width),
                                      qm(par)[:, 2 * jp + j2, qt * P:qt * P + P],
                                      km(par)[:, j2, kc * CW:kc * CW + width],
                                      start=True, stop=True)
                        if not last:
                            m.then_inc(s.mx_mm, 1)
                    if last:
                        for jp in range(2):
                            pe.matmul(bank(5 + (k + jp) % 3, width - P, width), identb[:, :],
                                      maskb[:, 0 if kind == "causal" else 1, :], start=False, stop=True,
                                      skip_group_check=True).then_inc(s.mx_mm, 1)

                def turn_max(g):
                    pe.wait_ge(s.m_pt, 4 * g + 4)
                    pe.transpose(ps[0:96, 5, 0:64].bitcast(BF16), msq[:, :, :, :].rearrange("p a k b -> p (a k b)"),
                                 identb[:, :]).then_inc(s.mT, 1)
                    pe.wait_ge(s.m_sp, g + 1)

                def scores(g, par, k):
                    qh, kt, off = STEPS[k]
                    for j2 in range(2):
                        if k:
                            pe.wait_ge(s.pexp, 2 * UNITS * g + (2 * k + j2 - 1))
                        for jp in range(2):
                            m = pe.matmul(bank(2 * j2 + jp, 0, CW - off),
                                          ke(par)[:, j2, kt * P:kt * P + P],
                                          qe(par)[:, 2 * jp + j2, qh * CW + off:qh * CW + CW],
                                          start=True, stop=True)
                        m.then_inc(s.st_mm, 1)

                def values(g, par, k):
                    qh, kt, off = STEPS[k]
                    if kt == 0:
                        pe.wait_ge(s.o_sb, 2 * g + (qh + 1))
                    if kt >= 4 * qh:
                        pe.wait_ge(s.pmask, 8 * g + (4 * qh + kt - 4 * qh + 1))
                    else:
                        pe.wait_ge(s.pexp, 2 * UNITS * g + (2 * k + 2))
                    for j in range(4):
                        m = pe.matmul(ps[32 * j:32 * j + 32, 4, off:CW], vst(par)[:, kt, j, :],
                                      pbuf(k % 2)[:, j, 0:CW - off], start=(kt == 0), stop=(kt >= 4 * qh),
                                      skip_group_check=True)
                    m.then_inc(s.av_mm, 1)

                def maxima(i, par):
                    g = GROUPS * a + i
                    pe.wait_ge(pm_ld[par], 64 * (5 - par) * a + 64)
                    for k in range(0, MAXU, 2):
                        max_pair(g, par, k)

                def group(it, par, turn, ahead):
                    g = GROUPS * a + 2 * it + par
                    r = GROUPS // 2 * a + it
                    pe.wait_ge(pe_ld[par], 80 * r + 80)
                    pe.wait_ge(rows_ld[par], 32 * r + 32)
                    scores(g, par, 0)
                    if turn:
                        turn_max(g + 1)
                    if ahead:
                        pe.wait_ge(pm_ld[par], 64 * ((5 - par) * a + it) + 128)
                    for k in range(UNITS):
                        if ahead:
                            max_pair(g + 2, par, 4 * k)
                        if k + 1 < UNITS:
                            scores(g, par, k + 1)
                        if ahead:
                            max_pair(g + 2, par, 4 * k + 2)
                        values(g, par, k)

                maxima(0, 0)
                turn_max(GROUPS * a)
                maxima(1, 1)
                pe.wait_ge(s.one_ld, 64 * (a + 1))
                with pe.Fori(0, GROUPS // 2 - 1) as it:
                    for par in range(2):
                        group(it, par, True, True)
                group(GROUPS // 2 - 1, 0, True, False)
                group(GROUPS // 2 - 1, 1, False, False)
                for c in range(NC):
                    pe.wait_ge(s.oT, NC * a + c + 1)
                    pe.matmul(bank(c), w("fo" if kind == "fhn" else "co"), A(4, *ch(c)),
                              start=True, stop=True).then_inc(s.ofin, 1)
                res_T(y0, 6)

            def gated(n, ln0, tr0, tk0, y0):
                def encode(c):
                    if c >= 2:
                        pe.wait_ge(s.e_sp, 2 * (NC * n + c - 1))
                    for hf in range(2):
                        m = pe.matmul(bank(2 * (c % 2) + hf), wc("enc", hf), u[:, c * CW:c * CW + CW],
                                      start=True, stop=True)
                    m.then_inc(s.e_mm, 1)

                def to_cont(c):
                    pe.wait_ge(s.e_sp, 2 * (NC * n + c + 1))
                    for hf in range(2):
                        a = (2 * (c % 2) + hf) * CW
                        m = pe.matmul(ps[M * hf:M * hf + M, 4 + c, :], wc("s2c", hf, M), A(0, a, a + CW),
                                      start=True, stop=True, skip_group_check=True)
                    m.then_inc(s.s_mm, 1)

                pe.wait_ge(s.u, NC * tr0 + NC)
                for c in range(NC + 1):
                    if c < NC:
                        encode(c)
                    if c:
                        to_cont(c - 1)
                for c in range(NC):
                    pe.wait_ge(s.cont, NC * n + c + 1)
                    pe.matmul(ps[0:M, 4 + c, :], w("rW1"), A(1, *ch(c)), start=True, stop=True).then_inc(s.r_mm, 1)
                for t in range(NT):
                    pe.wait_ge(s.th, NC * n + t // TC + 1)
                    m = pe.matmul(bank(0, t * E, t * E + E), heap[0:M, 2, t * P:t * P + P], w("rW2", M),
                                  start=True, stop=True)
                m.then_inc(s.l_mm, 1)
                pe.wait_ge(s.gates, n + 1)
                gview = ps[:, 1:3, :].rearrange("p a b -> p (a b)").bitcast(BF16)
                for t in range(NT):
                    m = pe.transpose(gview[0:24, t * P:t * P + P], g24[:, t * 24:t * 24 + 24], identb[:, :])
                m.then_inc(s.gT, 1)
                for t in range(NT):
                    m = pe.transpose(ps[0:E, 4 + t // TC, (t % TC) * P:(t % TC) * P + P],
                                     gate[:, 3, t * E:t * E + E], ident)
                m.then_inc(s.gT, 1)
                pe.wait_ge(s.gTs, 2 * (n + 1))

                def up(q):
                    c, e = q // E, q % E
                    g = NC * E * n + q
                    if q >= 2:
                        pe.wait_ge(s.x_rl, g - 1)
                    pe.matmul(bank(q % 2), wc("We1", e), A(1, *ch(c)), start=True, stop=True).then_inc(s.x_mm, 1)
                    if q >= 2:
                        pe.wait_ge(s.x_h, g - 1)
                    pe.matmul(bank(2 + q % 2), eselb[:, e * P:e * P + P], halves(3)[0][:, c * CW:c * CW + CW],
                              start=True, stop=True).then_inc(s.g_mm, 1)

                def down(q):
                    c, e = q // E, q % E
                    pe.wait_ge(s.x_h, NC * E * n + q + 2)
                    for k in range(2):
                        a = ((q + k) % 4) * CW
                        pe.matmul(ps[M * k:M * k + M, 4 + c, :], wc("We2", e + k, M), A(6, a, a + CW),
                                  start=(e == 0), stop=(k == 1 and e == E - 2),
                                  skip_group_check=True).then_inc(s.x_dn, 1)
                    if e == E - 2:
                        pe.matmul(ps[0:M, 4 + c, :], w("be2"), A(4, *ch(c)), start=False, stop=True,
                                  skip_group_check=True).then_inc(s.a_mm, 1)

                for q in range(0, NC * E + 2, 2):
                    if q < NC * E:
                        up(q)
                        up(q + 1)
                    if q:
                        down(q - 2)

                def to_spikes(c):
                    pe.wait_ge(s.a_sb, NC * n + c + 1)
                    if c >= 2:
                        pe.wait_ge(s.c_sb, 2 * (NC * n + c - 1))
                    for hf in range(2):
                        m = pe.matmul(bank(2 * (c % 2) + hf), wc("c2s", hf), A(7, *ch(c)), start=True, stop=True)
                    m.then_inc(s.c_mm, 1)

                def decode(c):
                    pe.wait_ge(s.c_sb, 2 * (NC * n + c + 1))
                    for hf in range(2):
                        a = (2 * (c % 2) + hf) * CW
                        m = pe.matmul(bank(4 + c), wc("dec", hf), A(8, a, a + CW), start=(hf == 0), stop=(hf == 1))
                    m.then_inc(s.dd_mm, 1)

                for c in range(NC + 1):
                    if c < NC:
                        to_spikes(c)
                    if c:
                        decode(c - 1)
                tok_T(tk0, 9, s.dd_sb, lambda c: NC * n + c + 1)

            def fastw(n, ln0, tr0, tk0, y0):
                ln_T(ln0 + 1, tr0 + 1)
                pe.matmul(bank(4, 0, P), w("AT", E), w("Bi", E), start=True, stop=True).then_inc(s.w0x, 1)
                hs = 0
                for c in range(NC):
                    pe.wait_ge(s.u, NC * (tr0 + 1) + c + 1)
                    pe.matmul(bank(c), w("Wk"), A(hs, *ch(c)), start=True, stop=True).then_inc(s.lwk, 1)
                pe.wait_ge(s.w0, 2)
                for c in range(NC):
                    pe.wait_ge(s.lks, c + 1)
                    pe.matmul(bank(4 + c), mats[:, 0, :], A(1, *ch(c)), start=True, stop=True).then_inc(s.lv, 1)
                    pe.matmul(bank(c), mats[:, 0, :], A(1, *ch(c)), start=True, stop=False)
                    pe.matmul(bank(c), mats[:, 1, :], A(hs, *ch(c)), start=False, stop=True).then_inc(s.lerr, 1)
                for c in range(NC):
                    pe.wait_ge(s.ly0, c + 1)
                    pe.matmul(bank(4 + c), w("Wq"), A(hs, *ch(c)), start=True, stop=True).then_inc(s.lq, 1)
                for c in range(NC):
                    pe.wait_ge(s.lgrad, c + 1)
                    pe.matmul(bank(c), w("Wg"), u[:, c * CW:c * CW + CW], start=True, stop=True).then_inc(s.lgm, 1)
                for c in range(NC):
                    pe.wait_ge(s.lo1, c + 1)
                    pe.matmul(bank(4 + c), w("Wo"), A(6, *ch(c)), start=True, stop=True).then_inc(s.lwo, 1)
                res_T(y0, 8)

            pe.wait_ge(s.w_in0, 16)
            for kind, n, ln0, tr0, tk0, y0 in plan:
                ln_T(ln0, tr0)
                pe.wait_ge(w_in[PART.get(kind, 2)], 16)
                if kind != "mlla":
                    pe.wait_ge(s.prep, 1)
                if kind in attn_of:
                    attention(attn_of[kind], kind, tr0, y0)
                else:
                    {"mlla": mlla, "moe": moe, "gated": gated, "fastw": fastw}[kind](n, ln0, tr0, tk0, y0)

        @block.scalar
        def _(act):
            def fn(out, in_, f=ACT.Identity, bias=0.0, scale=1.0):
                return act.activation(out, in_, f, bias=bias, scale=scale)

            def ln_copy(k, dst, g=None, b=None):
                for c in range(NC):
                    act.wait_ge(s.uT, NC * k + c + 1)
                    if g is None:
                        fn(dst[:, c * CW:c * CW + CW], bank(c), ACT.Copy).then_inc(s.u, 1)
                    else:
                        fn(dst[:, c * CW:c * CW + CW], bank(c), bias=b, scale=g).then_inc(s.u, 1)

            def tok_copy(k, slot):
                for c in range(NC):
                    act.wait_ge(s.tokT, NC * k + c + 1)
                    fn(A(slot, *ch(c)), bank(4 + c), ACT.Copy).then_inc(s.tok, 1)

            def mlla(n, ln0, tr0, tk0, y0):
                tok_copy(tk0, 9)
                ln_copy(tr0 + 1, A(1), w("g1"), w("bn1"))
                for c in range(NC):
                    act.wait_ge(s.lin, c + 1)
                    fn(A(2, *ch(c)), bank(c), ACT.Silu, bias=w("actb")).then_inc(s.silu, 1)
                for b in range(B):
                    act.wait_ge(s.xc, b + 1)
                    fn(A(5, b * N, b * N + N), A(4, b * N, b * N + N), ACT.Silu).then_inc(s.v, 1)
                for c in range(NC):
                    act.wait_ge(s.kq_min, 2 * c + 1)
                    fn(A(3, *ch(c)), bank(c), ACT.Relu, bias=w("qb")).then_inc(s.kq_relu, 1)
                    act.wait_ge(s.kq_min, 2 * c + 2)
                    fn(A(4, *ch(c)), bank(4 + c), ACT.Relu, bias=w("kb")).then_inc(s.kq_relu, 1)
                    fn(A(9, *ch(c)), A(9, *ch(c)), ACT.Exp).then_inc(s.kq_exp, 1)
                    fn(A(8, *ch(c)), A(8, *ch(c)), ACT.Exp).then_inc(s.kq_exp, 1)
                for c in range(NC):
                    act.wait_ge(s.ktokT, c + 1)
                    fn(A(1, *ch(c)), bank(4 + c), ACT.Copy).then_inc(s.ktok, 1)
                for c in range(NC):
                    act.wait_ge(s.rden_den, c + 1)
                    fn(heap[0:H, 8, c * CW:c * CW + CW], ps[0:H, c, :], ACT.Copy).then_inc(s.rden_ev, 1)
                tok_copy(tk0 + 1, 9)
                ln_copy(tr0 + 2, A(1), w("g2"), w("bn2"))
                for c in range(NC):
                    for j in range(4):
                        act.wait_ge(s.fc1, 4 * c + j + 1)
                        if c >= 2:
                            act.wait_ge(s.fc2, c - 1)
                        fn(A(6 + c % 2, j * CW, j * CW + CW), bank(j), ACT.Gelu, bias=wc("fc1b", j, 1)).then_inc(s.hid, 1)

            def moe(n, ln0, tr0, tk0, y0):
                rowsn = tn[:, ln0 % 2].rearrange("p t c -> p (t c)")
                act.wait_ge(s.ln_tn, NC * (ln0 + 1))
                fn(halves(0)[0], rowsn, ACT.Copy).then_inc(s.hi2, 1)
                act.wait_ge(s.rs2, n + 1)
                fn(halves(0)[1], A(2), ACT.Copy).then_inc(s.mid2, 1)
                act.wait_ge(s.slotT, n + 1)
                fn(halves(8)[1].bitcast(F16)[0:NT, 0:P], ps[0:NT, 5, 256:384], ACT.Copy).then_inc(s.slotrow, 1)
                for half in range(2):
                    act.wait_ge(s.disp, NT * (n + 1))
                    fn(A(4, half * CW, half * CW + CW), bank(6 + half), ACT.Copy).then_inc(s.xg, 1)
                for e in range(E):
                    act.wait_ge(s.h_mm, E * n + e + 1)
                    if e >= 2:
                        act.wait_ge(s.y_mm, E * n + e - 1)
                    for j in range(4):
                        fn(hbuf(e)[:, j, :], bank(e % 2, j * P, j * P + P), ACT.Relu,
                           bias=wc("b1", 4 * e + j, 1)).then_inc(s.h_act, 1)

            def attention(a, kind, tr0, y0):
                for c in range(NC):
                    act.wait_ge(s.qkv_mm, NC * a + c + 1)
                    if kind == "fhn":
                        fn(A(0, *ch(c)), bank(c), ACT.Copy, scale=float(D) ** -0.5).then_inc(s.q_sb, 1)
                    else:
                        fn(A(0, *ch(c)), bank(c), bias=small[:, 2:3], scale=float(D) ** -0.5).then_inc(s.q_sb, 1)
                act.wait_ge(s.q_sb, NC * (a + 1))
                fn(QH, A(0), ACT.Copy).then_inc(s.hi, 1)
                act.wait_ge(s.k_sb, NC * (a + 1))
                fn(KH, A(1), ACT.Copy).then_inc(s.hi, 1)
                act.wait_ge(s.rs, 2 * a + 1)
                fn(QMI, A(5), ACT.Copy).then_inc(s.mid, 1)
                act.wait_ge(s.rs, 2 * a + 2)
                fn(KMI, A(6), ACT.Copy).then_inc(s.mid, 1)

                def out_copy(g, par, qh):
                    act.wait_ge(s.av_mm, UNITS * g + (4 if qh == 0 else 12))
                    fn(oraw(par)[:, qh * CW:qh * CW + CW], bank(4), ACT.Copy).then_inc(s.o_sb, 1)

                def group(it, par):
                    g = GROUPS * a + 2 * it + par
                    for k, (qh, kt, off) in enumerate(STEPS):
                        if k >= 2:
                            act.wait_ge(s.av_mm, UNITS * g + (k - 1))
                        for j2 in range(2):
                            act.wait_ge(s.st_mm, 2 * UNITS * g + (2 * k + j2 + 1))
                            fn(pbuf(k % 2)[:, 2 * j2:2 * j2 + 2, 0:CW - off], ps[:, 2 * j2:2 * j2 + 2, 0:CW - off],
                               ACT.Exp).then_inc(s.pexp, 1)
                        if k == 4:
                            act.wait_ge(o_st[par], 64 * (GROUPS // 2 * a + it) + 64)
                            out_copy(g, par, 0)
                    out_copy(g, par, 1)

                with act.Fori(0, GROUPS // 2) as it:
                    for par in range(2):
                        group(it, par)
                if kind == "fhn":
                    act.wait_ge(s.f_pre, 1)
                    fn(A(5, 512, 768), A(5, 512, 768), ACT.Sigmoid, scale=10.0).then_inc(s.f_sig, 1)
                    act.wait_ge(s.f_pre, 2)
                    fn(A(5, 512, 768), A(5, 512, 768), ACT.Sigmoid).then_inc(s.f_sig, 1)
                for c in range(NC):
                    act.wait_ge(s.ofin, NC * a + c + 1)
                    if kind == "fhn":
                        fn(A(6, *ch(c)), bank(c), ACT.Copy).then_inc(s.y, 1)
                    else:
                        fn(A(6, *ch(c)), bank(c), bias=w("cob")).then_inc(s.y, 1)

            def gated(n, ln0, tr0, tk0, y0):
                for c in range(NC):
                    act.wait_ge(s.e_mm, NC * n + c + 1)
                    if c >= 2:
                        act.wait_ge(s.s_mm, NC * n + c - 1)
                    for hf in range(2):
                        a = (2 * (c % 2) + hf) * CW
                        fn(A(0, a, a + CW), bank(2 * (c % 2) + hf), ACT.Sigmoid, bias=wc("encb", hf, 1)).then_inc(s.e_sp, 1)
                for c in range(NC):
                    act.wait_ge(s.r_mm, NC * n + c + 1)
                    fn(heap[0:M, 2, c * CW:c * CW + CW], ps[0:M, 4 + c, :], ACT.Tanh, bias=w("rb1", M)).then_inc(s.th, 1)
                act.wait_ge(s.d12, n + 1)
                fn(sm[:, 4, :], sm[:, 3, :], ACT.Sigmoid).then_inc(s.sg, 1)
                fn(sm[:, 5, :], sm[:, 3, :], ACT.Sigmoid, scale=-1.0).then_inc(s.sg, 1)
                act.wait_ge(s.g_zero, n + 1)
                act.wait_ge(s.gT, 2 * n + 1)
                gview = ps[:, 1:3, :].rearrange("p a b -> p (a b)").bitcast(BF16)
                fn(halves(3)[0][0:24, :], gview[0:24, :], ACT.Copy).then_inc(s.gTs, 1)
                act.wait_ge(s.gT, 2 * n + 2)
                fn(heap[0:E, 4, :], ps[0:E, 4:8, :].rearrange("p a b -> p (a b)"), ACT.Copy).then_inc(s.gTs, 1)
                for q in range(NC * E):
                    g = NC * E * n + q
                    act.wait_ge(s.x_mm, g + 1)
                    if q >= 4:
                        act.wait_ge(s.x_h, g - 3)
                    fn(A(5, (q % 4) * CW, (q % 4) * CW + CW), bank(q % 2), ACT.Relu,
                       bias=wc("be1", q % E, 1)).then_inc(s.x_rl, 1)

                def decoded(c):
                    act.wait_ge(s.dd_mm, NC * n + c + 1)
                    fn(A(9, *ch(c)), bank(4 + c), ACT.Sigmoid, bias=w("decb")).then_inc(s.dd_sb, 1)

                for c in range(NC):
                    act.wait_ge(s.c_mm, NC * n + c + 1)
                    if c >= 2:
                        act.wait_ge(s.dd_mm, NC * n + c - 1)
                    for hf in range(2):
                        a = (2 * (c % 2) + hf) * CW
                        fn(A(8, a, a + CW), bank(2 * (c % 2) + hf), ACT.Sigmoid, bias=wc("c2sb", hf, 1)).then_inc(s.c_sb, 1)
                    if c:
                        decoded(c - 1)
                decoded(NC - 1)
                tok_copy(tk0, 0)

            def fastw(n, ln0, tr0, tk0, y0):
                fn(small[:, 8:9], w("lr"), ACT.Exp).then_inc(s.llr, 1)
                ln_copy(tr0 + 1, A(0), w("lng"), w("lnb"))
                for c in range(NC):
                    act.wait_ge(s.lwk, c + 1)
                    fn(A(1, *ch(c)), bank(c), ACT.Copy).then_inc(s.lks, 1)
                for c in range(NC):
                    act.wait_ge(s.lv, c + 1)
                    fn(A(2, *ch(c)), bank(4 + c), ACT.Copy).then_inc(s.ly0, 1)
                for c in range(NC):
                    act.wait_ge(s.lgm, c + 1)
                    fn(A(7, *ch(c)), bank(c), ACT.Sigmoid).then_inc(s.lgs, 1)

            act.sem_inc(s.o_sb, 1)
            act.sem_inc(s.o_st0, 64)
            act.sem_inc(s.o_st1, 64)
            for kind, n, ln0, tr0, tk0, y0 in plan:
                ln_copy(tr0, u)
                act.wait_ge(w_in[PART.get(kind, 2)], 16)
                if kind in attn_of:
                    attention(attn_of[kind], kind, tr0, y0)
                else:
                    {"mlla": mlla, "moe": moe, "gated": gated, "fastw": fastw}[kind](n, ln0, tr0, tk0, y0)

        @block.vector
        def _(dve):
            link = chain(dve, s.dve_chain)
            TT, TS, STT = dve.tensor_tensor, dve.tensor_scalar, dve.scalar_tensor_tensor

            def ln(n, src, ready=None):
                dst = tn[:, n % 2]
                for t in range(NT):
                    if ready is not None and t % TC == 0:
                        dve.wait_ge(ready[0], ready[1] + t // TC + 1)
                    m = dve.bn_stats(st6[:, t, :], src[:, t, :])
                link(m)
                v, y, t0, mean = sm[:, 0, :], sm[:, 1, :], sm[:, 2, :], sm[:, 6, :]
                TT(t0, st6[:, :, 1], st6[:, :, 4], ALU.subtract)
                TT(mean, st6[:, :, 1], st6[:, :, 4], ALU.add)
                link(TT(v, st6[:, :, 2], st6[:, :, 5], ALU.add))
                link(TT(t0, t0, t0, ALU.mult))
                link(STT(v, t0, C / 4.0, v, ALU.mult, ALU.add))
                link(TS(v, v, 1.0 / C, 1e-5, ALU.mult, ALU.add))
                link(TS(y.bitcast(I32), v.bitcast(I32), -0.5, RSQRT_SEED, ALU.mult, ALU.add))
                for _ in range(3):
                    link(STT(t0, y, -0.5, y, ALU.mult, ALU.mult))
                    link(TT(t0, t0, v, ALU.mult))
                    link(STT(y, t0, 1.5, y, ALU.add, ALU.mult))
                link(STT(mean, mean, -0.5, y, ALU.mult, ALU.mult))
                for t in range(NT):
                    m = TS(dst[:, t, :], src[:, t, :], y[:, t:t + 1], mean[:, t:t + 1], ALU.mult, ALU.add)
                    if t % TC == TC - 1:
                        m.then_inc(s.ln_tn, 1)
                dve.wait_ge(s.ln_tn, NC * (n + 1))

            def residual(k, bi):
                for c in range(NC):
                    dve.wait_ge(s.resT, NC * k + c + 1)
                    xs = x[:, TC * c:TC * c + TC, :]
                    TT(xs, xs, bank(4 + c).rearrange("p (t c) -> p t c", c=C), ALU.add).then_inc(s.res, 1)
                dve.wait_ge(s.res, NC * (bi + 1))

            def conv(dst, src, b, name, centre, sem):
                a, e = b * N, b * N + N
                wv = wc
                link(TS(dst[:, a:e], src[:, a:e], centre, wv(name, 3, 1), ALU.mult, ALU.add))
                link(STT(dst[:, a + 1:e], src[:, a:e - 1], wv(name, 0, 1), dst[:, a + 1:e], ALU.mult, ALU.add))
                m = STT(dst[:, a:e - 1], src[:, a + 1:e], wv(name, 2, 1), dst[:, a:e - 1], ALU.mult, ALU.add)
                if sem is None:
                    link(m)
                else:
                    m.then_inc(sem, 1)

            def mlla(n, ln0, tr0, tk0, y0):
                for b in range(B):
                    dve.wait_ge(s.u, NC * tr0 + 2 * b + 2)
                    conv(A(0), u, b, "cpe1", small[:, 0:1], s.c1)
                ln(ln0 + 1, heap[:, 9, :].rearrange("p (t c) -> p t c", c=C), (s.tok, NC * tk0))
                for c in range(NC):
                    dve.wait_ge(s.lin, c + 1)
                    TS(A(3, *ch(c)), bank(4 + c), w("inb"), None, ALU.add).then_inc(s.xi, 1)
                dve.wait_ge(s.xi, NC)
                for b in range(B):
                    conv(A(4), A(3), b, "dwc", wc("dwc", 1, 1), s.xc)
                for c in range(NC):
                    dve.wait_ge(s.qk_mm, c + 1)
                    TS(A(9, *ch(c)), bank(c), w("qb"), 0.0, ALU.add, ALU.min).then_inc(s.kq_min, 1)
                    TS(A(8, *ch(c)), bank(4 + c), w("kb"), 0.0, ALU.add, ALU.min).then_inc(s.kq_min, 1)
                lepe = tn[:, 1].rearrange("p t c -> p (t c)")
                for b in range(B):
                    conv(lepe, A(5), b, "lepe", wc("lepe", 1, 1), None)
                for b in range(B):
                    dve.wait_ge(s.qk, 4 * b + 4)
                    link(dve.tensor_reduce(small[:, 10 + b:11 + b], A(4, b * N, b * N + N), AX, ALU.add))
                    TS(small[:, 16 + H * b:16 + H * b + H], w("headm"), small[:, 10 + b:11 + b], 1.0 / N,
                       ALU.mult, ALU.mult).then_inc(s.kmean, 1)
                for c in range(NC):
                    dve.wait_ge(s.vtokT, c + 1)
                    dve.tensor_copy(A(9, *ch(c)), bank(c)).then_inc(s.vtok, 1)
                for b in range(B):
                    dve.wait_ge(s.gacc, b + 1)
                    dve.tensor_copy(mats[:, b, :], bank(4 + b, 0, P)).then_inc(s.gev, 1)
                for b in range(B):
                    dve.wait_ge(s.gacc, B + b + 1)
                    TT(mats[:, 2 + b, :], bank(4 + b, P, 2 * P), w("blockm"), ALU.mult).then_inc(s.gev, 1)
                for b in range(B):
                    dve.wait_ge(s.gacc, 2 * B + b + 1)
                    dve.tensor_copy(mats[:, 4 + b, :], bank(4 + b, 2 * P, 3 * P)).then_inc(s.gev, 1)
                dve.wait_ge(s.z_ld, 16)
                link(TS(A(7, 0, 256), A(7, 0, 256), 1e-6, None, ALU.add))
                dve.reciprocal(A(7, 256, 512), A(7, 0, 256)).then_inc(s.z_rc, 1)
                dve.wait_ge(s.z_fl, 32)
                for c in range(NC):
                    dve.wait_ge(s.mnum, c + 1)
                    link(TT(A(4, *ch(c)), bank(c), A(6, *ch(c)), ALU.mult))
                    link(TT(A(4, *ch(c)), A(4, *ch(c)), lepe[:, c * CW:c * CW + CW], ALU.add))
                    TT(A(4, *ch(c)), A(4, *ch(c)), A(2, *ch(c)), ALU.mult).then_inc(s.att, 1)
                for c in range(NC):
                    dve.wait_ge(s.olin, c + 1)
                    STT(A(3, *ch(c)), bank(4 + c), w("outb"), A(0, *ch(c)), ALU.add, ALU.add).then_inc(s.x2, 1)
                dve.wait_ge(s.x2, NC)
                for b in range(B):
                    conv(A(5), A(3), b, "cpe2", small[:, 1:2], s.x3)
                ln(ln0 + 2, heap[:, 9, :].rearrange("p (t c) -> p t c", c=C), (s.tok, NC * (tk0 + 1)))
                for c in range(NC):
                    dve.wait_ge(s.fc2, c + 1)
                    STT(A(8, *ch(c)), bank(4 + c), w("fc2b"), A(5, *ch(c)), ALU.add, ALU.add).then_inc(s.y, 1)

            def first_max(lg, m, oh, cand, mc, out):
                v = lg.rearrange("p (t e) -> p t e", e=E)
                link(dve.tensor_reduce(m, v, AX, ALU.max))
                link(TT(oh.rearrange("p (t e) -> p t e", e=E), v, bc(m.unsqueeze(2), (P, NT, E)), ALU.is_equal))
                link(TT(cand.rearrange("p (t e) -> p t e", e=E), oh.rearrange("p (t e) -> p t e", e=E),
                        bc(row("rev").unsqueeze(1), (P, NT, E)), ALU.mult))
                link(dve.tensor_reduce(mc, cand.rearrange("p (t e) -> p t e", e=E), AX, ALU.max))
                return TT(out.rearrange("p (t e) -> p t e", e=E), cand.rearrange("p (t e) -> p t e", e=E),
                          bc(mc.unsqueeze(2), (P, NT, E)), ALU.is_equal)

            def moe(n, ln0, tr0, tk0, y0):
                v3 = lambda ap: ap.rearrange("p (t e) -> p t e", e=E)
                rowsn = tn[:, ln0 % 2].rearrange("p t c -> p (t c)")
                dve.wait_ge(s.hi2, n + 1)
                TT(A(2), rowsn, halves(0)[0], ALU.subtract).then_inc(s.rs2, 1)
                dve.wait_ge(s.lg, n + 1)
                link(TT(v3(gate[:, 0, :]), v3(bank(4, 0, NT * E)), bc(row("bsw").unsqueeze(1), (P, NT, E)), ALU.add))
                first_max(gate[:, 0, :], sm[:, 0, :], gate[:, 1, :], gate[:, 2, :], sm[:, 1, :], ohb[:, :]
                          ).then_inc(s.oh, 1)
                dve.wait_ge(s.oh, n + 1)
                link(TT(v3(gate[:, 1, :]), v3(ohb[:, :]), bc(row("base").unsqueeze(1), (P, NT, E)), ALU.mult))
                link(dve.tensor_reduce(sm[:, 2, :], v3(gate[:, 1, :]), AX, ALU.add))
                dve.wait_ge(s.cum, n + 1)
                link(TT(gate[:, 2, :], bank(5, 0, NT * E), ohb[:, :], ALU.mult))
                link(dve.tensor_reduce(sm[:, 3, :], v3(gate[:, 2, :]), AX, ALU.add))
                link(TS(sm[:, 4, :], sm[:, 3, :], float(CAP), 2048.0, ALU.is_gt, ALU.mult))
                link(STT(sm[:, 5, :], sm[:, 3, :], -1.0, sm[:, 2, :], ALU.add, ALU.add))
                TT(sm[:, 7, :], sm[:, 5, :], sm[:, 4, :], ALU.add).then_inc(s.slot, 1)
                dve.wait_ge(s.mid2, n + 1)
                TT(halves(1)[0], A(2), halves(0)[1], ALU.subtract).then_inc(s.parts, 1)
                dve.wait_ge(s.slot, n + 1)
                for t in range(NT):
                    if t >= 4:
                        dve.wait_ge(s.disp, NT * n + t - 3)
                    TS(onehot(t), iota16[:, :], sm[:, 7, t:t + 1], None, ALU.is_equal).then_inc(s.onehot, 1)
                dve.wait_ge(s.parts, n + 1)
                dve.wait_ge(s.slot_ld, 16 * (n + 1))
                slotb = halves(8)[0].bitcast(F16)
                link(STT(A(2), slotb, float(SLOTS), u[:, :], ALU.is_ge, ALU.mult))
                for e in range(4):
                    TS(back(e), slotb, wc("pcol", e, 1), None, ALU.is_equal).then_inc(s.st_oh, 1)
                ysb, ry = A(4, 1024, 2048), A(6, 0, 1024)
                yp = heap[:, 5, :].bitcast(BF16)
                for hf in range(2):
                    a, e = hf * CW, hf * CW + CW
                    dve.wait_ge(s.y_mm, E * n + 4 * hf + 4)
                    link(TT(ysb[:, a:e], bank(2 + hf), row("b2")[:, a:e], ALU.add))
                    link(dve.tensor_copy(yp[:, a:e], ysb[:, a:e]))
                    link(TT(ry[:, a:e], ysb[:, a:e], yp[:, a:e], ALU.subtract))
                    link(dve.tensor_copy(yp[:, SLOTS + a:SLOTS + e], ry[:, a:e]))
                    TT(yp[:, 2 * SLOTS + a:2 * SLOTS + e], ry[:, a:e], yp[:, SLOTS + a:SLOTS + e],
                       ALU.subtract).then_inc(s.yparts, 1)
                for e in range(4, E):
                    dve.wait_ge(s.comb, E * n + e - 3)
                    TS(back(e), slotb, wc("pcol", e, 1), None, ALU.is_equal).then_inc(s.st_oh, 1)
                dve.wait_ge(s.comb, E * (n + 1))
                for c in range(NC):
                    TT(A(0, *ch(c)), A(2, *ch(c)), bank(c), ALU.add).then_inc(s.y, 1)

            def attention(a, kind, ln0, tr0, y0):
                if kind == "causal":
                    link(TS(small[:, 2:3], w("pqb"), float(D) ** -0.5, None, ALU.mult))
                    tmp = tn[:, (ln0 + 1) % 2].rearrange("p (k t) c -> p k (t c)", k=4)
                    dve.wait_ge(s.tab_in, 16)
                    for k in range(3):
                        for c in range(NC):
                            p = NC * k + c
                            dve.wait_ge(s.rope_mm, p + 1)
                            if p >= 2:
                                dve.wait_ge(s.rope, p - 1)
                            h0 = (c % 2) * CW
                            TT(tmp[:, 2 * (p % 2), :], bank(2 * p % 8), A(2, h0, h0 + CW), ALU.mult)
                            TT(tmp[:, 2 * (p % 2) + 1, :], bank(2 * p % 8 + 1), A(2, N + h0, N + h0 + CW),
                               ALU.mult).then_inc(s.rope_t, 1)
                for c in range(NC):
                    dve.wait_ge(s.qkv_mm, NC * a + c + 1)
                    if kind == "fhn":
                        dve.tensor_copy(A(1, *ch(c)), bank(4 + c)).then_inc(s.k_sb, 1)
                    else:
                        TS(A(1, *ch(c)), bank(4 + c), w("pkb"), None, ALU.add).then_inc(s.k_sb, 1)
                dve.wait_ge(s.v_one, a + 1)
                for c in range(NC):
                    dve.wait_ge(s.vt_mm, NC * a + c + 1)
                    if c >= 2:
                        dve.wait_ge(v_st[c % 2], 16 * TC * (2 * a + 1))
                    for t in range(TC):
                        src = bank(c, t * P, t * P + P).rearrange("p (h d) -> p h d", d=D)
                        if kind == "fhn":
                            m = dve.tensor_copy(vp(c % 2)[:, t, :, 0:D], src)
                        else:
                            m = TT(vp(c % 2)[:, t, :, 0:D], src, row("vb").rearrange("p (h d) -> p h d", d=D), ALU.add)
                    m.then_inc(s.v_sb, 1)
                dve.wait_ge(s.hi, 2 * a + 1)
                TT(A(5), A(0), QH, ALU.subtract).then_inc(s.rs, 1)
                dve.wait_ge(s.hi, 2 * a + 2)
                TT(A(6), A(1), KH, ALU.subtract).then_inc(s.rs, 1)
                dve.wait_ge(s.mid, 2 * a + 1)
                dve.wait_ge(s.rs, 2 * a + 2)
                TT(QL, A(5), QMI, ALU.subtract).then_inc(s.lo, 1)
                dve.wait_ge(s.mid, 2 * a + 2)
                TT(KL, A(6), KMI, ALU.subtract).then_inc(s.lo, 1)
                dve.wait_ge(s.lo, 2 * a + 2)
                dve.memset(zeroed(2), 0.0).then_inc(s.m_zero, 1)

                def maxima(g):
                    for k, jp, j2, qt, kc, width in STRIPS:
                        dve.wait_ge(s.mx_mm, MAXU * g + (k + 1))
                        dve.tensor_reduce(mx[:, kc, jp, j2, qt:qt + 1], bank(5 + k % 3, 0, width), AX,
                                          ALU.max).then_inc(s.mx_red, 1)
                    dve.wait_ge(s.mx_red, MAXU * g + MAXU)
                    far, near = mx[:, 0, :, :, 4:KT], mx[:, 1, :, :, 4:KT]
                    TT(far, far, near, ALU.max).then_inc(s.mx_cmb, 1)
                    dve.wait_ge(s.mx_cmb, g + 1)
                    dve.wait_ge(s.mT, g)
                    TS(mneg[:, :], mx[:, 0].rearrange("p a b q -> p (a b q)"), -1.0, None,
                       ALU.mult).then_inc(s.mx_fin, 1)
                    dve.wait_ge(s.mx_fin, g + 1)

                def split_max(g, par, turn):
                    neg = mneg[:, :].rearrange("p (a b) -> p a b", a=2)
                    rest = mrs[:, :].rearrange("p (a b) -> p a b", a=2)
                    dve.tensor_copy(msq[:, :, 0, :], neg).then_inc(s.m_pt, 1)
                    dve.wait_ge(s.m_pt, 4 * g + 1)
                    TT(rest, neg, msq[:, :, 0, :], ALU.subtract).then_inc(s.m_pt, 1)
                    dve.wait_ge(s.m_pt, 4 * g + 2)
                    dve.tensor_copy(msq[:, :, 1, :], rest).then_inc(s.m_pt, 1)
                    dve.wait_ge(s.m_pt, 4 * g + 3)
                    TT(msq[:, :, 2, :], rest, msq[:, :, 1, :], ALU.subtract).then_inc(s.m_pt, 1)
                    dve.wait_ge(s.mT, g + 1)
                    dve.wait_ge(rows_ld[par], 32 * turn)
                    dve.tensor_copy(msp[:, par, :], ps[0:96, 5, 0:64].bitcast(BF16)).then_inc(s.m_sp, 1)

                maxima(GROUPS * a)
                split_max(GROUPS * a, 0, GROUPS // 2 * a)
                maxima(GROUPS * a + 1)
                split_max(GROUPS * a + 1, 1, GROUPS // 2 * a)
                with dve.Fori(0, GROUPS // 2 - 1) as it:
                    for par in range(2):
                        maxima(GROUPS * a + (2 * it + par) + 2)
                        split_max(GROUPS * a + (2 * it + par) + 2, par, GROUPS // 2 * a + it + 1)
                dve.wait_ge(s.fd_ld, 48 * (a + 1))
                f = lambda k: A(5, 256 * k, 256 * k + 256)
                den, fac, t2, inp, scl, rec, e_, t7 = (f(k) for k in range(8))
                if kind == "causal":
                    dve.reciprocal(fac, den).then_inc(s.f_out, 1)
                else:
                    pa, pb, pd = (wc("fabd", k, 1) for k in range(3))
                    al, da, rd, q0 = small[:, 3:4], small[:, 4:5], small[:, 5:6], small[:, 6:7]
                    link(TS(al, pd, 1.0 / 12.5, None, ALU.mult))
                    link(STT(da, al, pb, al, ALU.mult, ALU.bypass))
                    link(TS(da, da, 1.0, None, ALU.add))
                    link(dve.reciprocal(rd, da))
                    link(dve.reciprocal(rec, den))
                    link(TT(e_, den, rec, ALU.mult))
                    link(STT(t7, e_, -1.0, e_, ALU.mult, ALU.max))
                    link(TS(scl, t7, 1e-6, None, ALU.max))
                    TS(t2, t7, -0.5, None, ALU.add).then_inc(s.f_pre, 1)
                    link(dve.reciprocal(fac, scl))
                    link(TT(inp, e_, fac, ALU.mult))
                    dve.wait_ge(s.f_sig, 1)
                    link(TS(t2, t2, 0.9, 0.1, ALU.mult, ALU.add))
                    link(TT(inp, inp, t2, ALU.mult))
                    link(TS(t2, inp, pd, None, ALU.mult))
                    link(TS(t7, t2, pa, al, ALU.add, ALU.mult))
                    link(TS(t7, t7, rd, 3.0, ALU.mult, ALU.min))
                    link(TS(t7, t7, -3.0, None, ALU.max))
                    link(TS(t2, t2, 3.0, -3.0, ALU.min, ALU.max))
                    link(TT(fac, t2, t2, ALU.mult))
                    link(TT(fac, fac, t2, ALU.mult))
                    link(STT(fac, fac, -1.0 / 3.0, t2, ALU.mult, ALU.add))
                    link(TT(fac, fac, t7, ALU.subtract))
                    link(TT(fac, fac, inp, ALU.add))
                    link(STT(fac, fac, pd, t2, ALU.mult, ALU.add))
                    link(TS(fac, fac, 3.0, -3.0, ALU.min, ALU.max))
                    TT(t2, fac, scl, ALU.mult).then_inc(s.f_pre, 1)
                    dve.wait_ge(s.f_sig, 2)
                    link(TS(t2, t2, 0.5, 0.5, ALU.mult, ALU.add))
                    link(TT(t7, e_, t2, ALU.mult))
                    link(TS(t7, t7, 1e-8, None, ALU.add))
                    link(dve.reciprocal(inp, t7))
                    link(TT(inp, inp, t2, ALU.mult))
                    TT(fac, inp, rec, ALU.mult).then_inc(s.f_out, 1)
                dve.wait_ge(s.fb_ld, 32 * (a + 1))
                for c in range(NC):
                    TT(A(4, *ch(c)), A(2, *ch(c)), A(3, *ch(c)), ALU.mult).then_inc(s.oT, 1)

            def gated(n, ln0, tr0, tk0, y0, bi):
                v3 = lambda ap: ap.rearrange("p (t e) -> p t e", e=E)
                for c in range(NC):
                    dve.wait_ge(s.s_mm, NC * n + c + 1)
                    TS(A(1, *ch(c)), bank(4 + c), w("s2cb"), None, ALU.add).then_inc(s.cont, 1)
                dve.wait_ge(s.l_mm, n + 1)
                link(TT(v3(gate[:, 0, :]), v3(bank(0, 0, NT * E)), bc(row("rb2").unsqueeze(1), (P, NT, E)), ALU.add))
                link(first_max(gate[:, 0, :], sm[:, 0, :], gate[:, 1, :], gate[:, 2, :], sm[:, 1, :], gate[:, 4, :]))
                link(STT(gate[:, 0, :], gate[:, 4, :], NEG, gate[:, 0, :], ALU.mult, ALU.add))
                link(first_max(gate[:, 0, :], sm[:, 2, :], gate[:, 1, :], gate[:, 2, :], sm[:, 1, :], gate[:, 5, :]))
                TT(sm[:, 3, :], sm[:, 0, :], sm[:, 2, :], ALU.subtract).then_inc(s.d12, 1)
                dve.wait_ge(s.sg, 2 * (n + 1))
                link(TT(v3(gate[:, 1, :]), v3(gate[:, 4, :]), bc(sm[:, 4, :].unsqueeze(2), (P, NT, E)), ALU.mult))
                link(TT(v3(gate[:, 2, :]), v3(gate[:, 5, :]), bc(sm[:, 5, :].unsqueeze(2), (P, NT, E)), ALU.mult))
                link(TT(gate[:, 3, :], gate[:, 1, :], gate[:, 2, :], ALU.add))
                gp = g24[:, :].rearrange("p (t k e) -> p t k e", k=3, e=E)
                link(dve.tensor_copy(gp[:, :, 0, :], v3(gate[:, 3, :])))
                link(TT(v3(gate[:, 1, :]), v3(gate[:, 3, :]), gp[:, :, 0, :], ALU.subtract))
                link(dve.tensor_copy(gp[:, :, 1, :], v3(gate[:, 1, :])))
                TT(gp[:, :, 2, :], v3(gate[:, 1, :]), gp[:, :, 1, :], ALU.subtract).then_inc(s.gates, 1)
                for q in range(NC * E):
                    g = NC * E * n + q
                    dve.wait_ge(s.x_rl, g + 1)
                    dve.wait_ge(s.g_mm, g + 1)
                    if q >= 4:
                        dve.wait_ge(s.x_dn, g - 3)
                    a = (q % 4) * CW
                    TT(A(6, a, a + CW), A(5, a, a + CW), bank(2 + q % 2), ALU.mult).then_inc(s.x_h, 1)
                    if q % E == 1 and q > E:
                        copy_cont(n, q // E - 1)
                copy_cont(n, NC - 1)
                ln(ln0 + 1, heap[:, 0, :].rearrange("p (t c) -> p t c", c=C), (s.tok, NC * tk0))
                for c in range(NC):
                    y = tn[:, (ln0 + 1) % 2, TC * c:TC * c + TC, :]
                    xs = x[:, TC * c:TC * c + TC, :]
                    link(TT(y, y, bc(row("fing").unsqueeze(1), (P, TC, C)), ALU.mult))
                    link(TT(y, y, bc(row("finb").unsqueeze(1), (P, TC, C)), ALU.add))
                    TT(xs, xs, y, ALU.add).then_inc(s.res, 1)
                dve.wait_ge(s.res, NC * (bi + 1))

            def copy_cont(n, c):
                dve.wait_ge(s.a_mm, NC * n + c + 1)
                dve.tensor_copy(A(7, *ch(c)), bank(4 + c)).then_inc(s.a_sb, 1)

            def fastw(n, ln0, tr0, tk0, y0):
                ln(ln0 + 1, tn[:, ln0 % 2])
                dve.wait_ge(s.w0x, 1)
                TT(mats[:, 0, :], bank(4, 0, P), w("W0"), ALU.add).then_inc(s.w0, 1)
                TS(mats[:, 1, :], w("Wv"), -1.0, None, ALU.mult).then_inc(s.w0, 1)
                dve.wait_ge(s.llr, 1)
                link(TS(small[:, 9:10], small[:, 8:9], 1.0, None, ALU.min))
                for c in range(NC):
                    dve.wait_ge(s.lerr, c + 1)
                    TT(A(3, *ch(c)), A(1, *ch(c)), bank(c), ALU.mult).then_inc(s.lgrad, 1)
                dve.wait_ge(s.lgrad, NC)
                for b in range(B):
                    m = dve.tensor_tensor_scan(A(4, b * N, b * N + N), bc(row("one"), (P, N)), A(3, b * N, b * N + N), 0.0,
                                               ALU.mult, ALU.add)
                link(m)
                for c in range(NC):
                    dve.wait_ge(s.lq, c + 1)
                    a = c * CW
                    f = 1 if c % 2 == 0 else 0
                    link(STT(A(5, *ch(c)), bank(4 + c), small[:, 9:10], row("pos")[:, (c % 2) * CW:(c % 2) * CW + CW],
                             ALU.mult, ALU.mult))
                    link(TT(A(5, a + f, a + CW), A(5, a + f, a + CW), A(4, a + f - 1, a + CW - 1), ALU.mult))
                    if f:
                        dve.tensor_copy(A(6, a, a + 1), A(2, a, a + 1))
                    link(TT(A(6, a + f, a + CW), A(2, a + f, a + CW), A(5, a + f, a + CW), ALU.subtract))
                    dve.wait_ge(s.lgs, c + 1)
                    TT(A(6, *ch(c)), A(6, *ch(c)), A(7, *ch(c)), ALU.mult).then_inc(s.lo1, 1)
                for c in range(NC):
                    dve.wait_ge(s.lwo, c + 1)
                    STT(A(8, *ch(c)), bank(4 + c), w("lsg"), u[:, c * CW:c * CW + CW], ALU.mult, ALU.add).then_inc(s.y, 1)

            dve.wait_ge(s.x_in, 16)
            for bi, (kind, n, ln0, tr0, tk0, y0) in enumerate(plan):
                ln(ln0, x[:, :, :])
                dve.wait_ge(w_in[PART.get(kind, 2)], 16)
                if kind == "mlla":
                    TS(small[:, 0:1], wc("cpe1", 1, 1), 1.0, None, ALU.add)
                    link(TS(small[:, 1:2], wc("cpe2", 1, 1), 1.0, None, ALU.add))
                else:
                    dve.wait_ge(s.row_in, 16)
                    dve.wait_ge(s.prep, 1)
                if kind in attn_of:
                    attention(attn_of[kind], kind, ln0, tr0, y0)
                elif kind == "gated":
                    gated(n, ln0, tr0, tk0, y0, bi)
                else:
                    {"mlla": mlla, "moe": moe, "fastw": fastw}[kind](n, ln0, tr0, tk0, y0)
                if kind != "gated":
                    residual(y0, bi)

        @block.gpsimd
        def _(pool):
            pool.memset(orow[:, :], 1.0)
            pool.wait_ge(s.w_in0, 16)
            pool.tensor_copy(identb[:, :], ident)
            pool.wait_ge(s.k_in, 16)
            pool.tensor_copy(maskb[:, 0, :], kw("cmask"))
            pool.tensor_copy(maskb[:, 1, :], kw("fmask"))
            pool.tensor_copy(trib[:, :], kw("tri"))
            pool.tensor_copy(onesb[:, :], kw("ones"))
            pool.tensor_copy(iota16[:, :], kw("iota"))
            pool.tensor_copy(eselb[:, :], kw("esel")).then_inc(s.prep, 1)

            def mlla():
                for c in range(NC):
                    for k, (dst, src) in enumerate(((3, 9), (4, 8))):
                        pool.wait_ge(s.kq_exp, 2 * c + k + 1)
                        pool.tensor_tensor(A(dst, *ch(c)), A(dst, *ch(c)), A(src, *ch(c)), ALU.add).then_inc(s.qk, 1)

            def stage_max(i, par):
                for jp in range(2):
                    for dst, src in loads(2 + par, i, jp):
                        pool.dma_start(dst, src).then_inc(pm_ld[par], 16)

            def attention(a, kind, ln0, tr0, bi):
                pool.wait_ge(s.ln_tn, NC * (ln0 + 1))
                pool.memset(heap[:, 7:9, :], 1.0).then_inc(s.v_one, 1)
                if kind == "causal":
                    tmp = tn[:, (ln0 + 1) % 2].rearrange("p (k t) c -> p k (t c)", k=4)
                    for k, slot in enumerate((5, 6, 9)):
                        for c in range(NC):
                            p = NC * k + c
                            pool.wait_ge(s.rope_t, p + 1)
                            pool.tensor_tensor(A(slot, *ch(c)), tmp[:, 2 * (p % 2), :], tmp[:, 2 * (p % 2) + 1, :],
                                               ALU.add).then_inc(s.rope, 1)
                for k in range(2):
                    pool.wait_ge(v_st[k], 16 * TC * 2 * (a + 1))
                pool.wait_ge(s.lo, 2 * (a + 1))
                pool.memset(zeroed(3), 0.0).then_inc(s.m_zero, 1)
                pool.wait_ge(s.qs_st, 16 * 24 * (a + 1))
                pool.wait_ge(s.m_zero, 2 * (a + 1))
                stage_max(0, 0)
                stage_max(1, 1)
                for k in range(2):
                    pool.memset(zeroed(k), 0.0).then_inc(s.e_zero, 1)
                pool.wait_ge(s.mx_mm, MAXU * (GROUPS * a + 1))
                stage_max(2, 0)

                def group(i, par, ahead):
                    g = GROUPS * a + i
                    if ahead:
                        pool.wait_ge(s.mx_mm, MAXU * g + 2 * MAXU)
                        stage_max(ahead_of(i), 1 - par)
                    d = 0
                    for k, (qh, kt, off) in enumerate(STEPS):
                        if kt < 4 * qh:
                            continue
                        pool.wait_ge(s.pexp, 2 * UNITS * g + (2 * k + 2))
                        pool.nop(nofuse=True)
                        if kind == "fhn":
                            m = pool.memset(pbuf(k % 2)[64:P, :, 0:64], 0.0)
                        else:
                            m = pool.affine_select(out=pbuf(k % 2)[:, :, 0:P], in_=pbuf(k % 2)[:, :, 0:P],
                                                   compare_op=ALU.is_ge, fill=0.0, base=0,
                                                   pattern=[[0, 4], [1, P]], channel_multiplier=-1)
                        m.then_inc(s.pmask, 1)

                def ahead_of(i):
                    return (i + 3) % GROUPS

                with pool.Fori(0, GROUPS // 2 - 1) as it:
                    for par in range(2):
                        group(2 * it + par, par, True)
                group(GROUPS - 2, 0, False)
                group(GROUPS - 1, 1, False)

            def gated(n, bi):
                if bi:
                    pool.wait_ge(s.res, NC * bi)
                pool.memset(heap[:, 3:5, :], 0.0).then_inc(s.g_zero, 1)

            for bi, (kind, n, ln0, tr0, tk0, y0) in enumerate(plan):
                if kind == "mlla":
                    mlla()
                elif kind == "gated":
                    gated(n, bi)
                elif kind in attn_of:
                    attention(attn_of[kind], kind, ln0, tr0, bi)


def kernel(**inputs):
    import numpy as np
    import concourse.bacc as bacc
    from concourse.bass_utils import run_bass_kernel_spmd

    i = {k: np.asarray(v) for k, v in inputs.items()}
    m, h, f, q = "L0_attn_a_", "L0_attn_b_", "L0_ffn_", "L1_attn_a_"
    b, g = "L1_attn_b_", "L1_ffn_"
    f4 = np.float32
    p = np.arange(P)
    half = C // 2
    th = (1.0 / (10000.0 ** (np.arange(half, dtype=f4) / half))).astype(f4)
    rot = np.zeros((C, C), f4)
    k = np.arange(half)
    rot[2 * k, 2 * k] = rot[2 * k + 1, 2 * k + 1] = np.cos(th)
    rot[2 * k, 2 * k + 1] = np.sin(th)
    rot[2 * k + 1, 2 * k] = -np.sin(th)
    theta = (f4(10000.0) ** (f4(-2.0) * (np.arange(half, dtype=f4) - f4(1.0)) / f4(C))).astype(f4)
    ang = (np.arange(N, dtype=f4)[:, None] * theta[None, :]).astype(f4)
    cos_t = np.repeat(np.cos(ang), 2, axis=1).T.astype(f4)
    sin_t = np.stack([np.sin(ang), -np.sin(ang)], -1).reshape(N, C).T.astype(f4)
    swap = p ^ 1
    pos = np.arange(1, N + 1, dtype=f4)

    def col(v):
        return v.reshape(-1, 1)

    def tiles(v, n):
        return v.reshape(n, P, -1).transpose(1, 0, 2).reshape(P, -1)

    def taps(wt, bias):
        return np.concatenate([wt.reshape(C, 3), col(bias)], 1)

    W = h + "W_qkv"
    ip, ib = i[q + "in_proj_w"], i[q + "in_proj_b"]
    cols = {
        "ident": np.eye(P, dtype=f4), "rot": rot, "rotT": rot.T,
        "blockm": (p[:, None] // D == p[None, :] // D).astype(f4) / f4(N),
        "headm": (p[:, None] // D == np.arange(H)[None, :]).astype(f4),
        "cpe1": taps(i[m + "cpe1_w"], i[m + "cpe1_b"]), "g1": col(i[m + "norm1_g"]), "bn1": col(i[m + "norm1_b"]),
        "inb": col(i[m + "in_b"]), "actb": col(i[m + "actp_b"]), "dwc": taps(i[m + "dwc_w"], i[m + "dwc_b"]),
        "qb": col(i[m + "qk_b"][:C]), "kb": col(i[m + "qk_b"][C:]), "lepe": taps(i[m + "lepe_w"], i[m + "lepe_b"]),
        "outb": col(i[m + "out_b"]), "cpe2": taps(i[m + "cpe2_w"], i[m + "cpe2_b"]),
        "g2": col(i[m + "norm2_g"]), "bn2": col(i[m + "norm2_b"]), "fc1b": i[m + "fc1_b"].reshape(4, P).T,
        "fc2b": col(i[m + "fc2_b"]), "in": i[m + "in_w"], "actp": i[m + "actp_w"],
        "qw": i[m + "qk_w"][:, :C], "kw": i[m + "qk_w"][:, C:], "ow": i[m + "out_w"],
        "fc1": i[m + "fc1_w"], "fc2": tiles(i[m + "fc2_w"], 4),
        "tri": (p[:, None] <= p[None, :]).astype(f4), "ones": np.ones((P, P), f4),
        "iota": np.broadcast_to(np.arange(SLOTS, dtype=f4), (P, SLOTS)),
        "pcol": (p[:, None] + CAP * np.arange(E)[None, :]).astype(f4),
        "wsw": i[f + "w_switch"], "b1": i[f + "b1"].reshape(E * 4, P).T,
        "w1": i[f + "w1"].transpose(1, 0, 2).reshape(C, E * HID),
        "w2": i[f + "w2"].reshape(E * 4, P, C).transpose(1, 0, 2).reshape(P, -1),
        "cmask": np.where(p[None, :] > p[:, None], f4(NEG), f4(0)),
        "fmask": np.where((p[None, :] >= 64) & (p[:, None] < 64), f4(NEG), f4(0)),
        "fq": i[W][:C].T, "fk": i[W][C:2 * C].T, "fv": i[W][2 * C:].T, "fo": i[h + "W_out"].T,
        "fabd": np.broadcast_to(np.stack([i[h + "a"], i[h + "b"], i[h + "dt"]]), (P, 3)),
        "rq": i[q + "wq"].T, "rqs": i[q + "wq"].T[:, swap], "rk": i[q + "wk"].T, "rks": i[q + "wk"].T[:, swap],
        "rv": i[q + "wv"].T, "rvs": i[q + "wv"].T[:, swap],
        "pq": ip[:C].T, "pk": ip[C:2 * C].T, "pv": ip[2 * C:].T, "pqb": col(ib[:C]), "pkb": col(ib[C:2 * C]),
        "co": i[q + "out_w"].T, "cob": col(i[q + "out_b"]), "cosT": cos_t, "sinT": sin_t,
        "W0": i[b + "W0"], "AT": i[b + "A_init"].T, "Bi": i[b + "B_init"],
        "Wq": i[b + "Wq"].T, "Wk": i[b + "Wk"].T, "Wv": i[b + "Wv"].T, "Wo": i[b + "Wo"].T, "Wg": i[b + "Wg"].T,
        "lr": col(i[b + "log_lr"]), "lng": col(i[b + "ln_g"]), "lnb": col(i[b + "ln_b"]), "lsg": col(i[b + "ls_g"]),
        "enc": i[g + "enc_W"], "encb": i[g + "enc_b"].reshape(2, P).T, "s2c": tiles(i[g + "s2c_W"], 2),
        "s2cb": col(i[g + "s2c_b"]), "rW1": np.tile(i[g + "rW1"], (2, 1)), "rb1": col(i[g + "rb1"]), "rW2": i[g + "rW2"],
        "We1": np.tile(i[g + "We1"].transpose(1, 0, 2).reshape(M, -1), (2, 1)), "be1": i[g + "be1"].T,
        "We2": i[g + "We2"].transpose(1, 0, 2).reshape(P, -1), "be2": i[g + "be2"],
        "c2s": np.tile(i[g + "c2s_W"], (2, 1)), "c2sb": i[g + "c2s_b"].reshape(2, P).T, "dec": tiles(i[g + "dec_W"], 2),
        "decb": col(i[g + "dec_b"]),
        "esel": np.kron(np.tile(np.eye(E, dtype=f4), (3, 1)), np.ones((1, P), f4)),
    }
    weights = np.zeros((P, sum(wd for part in COLS for _, wd in part)), f4)
    for name, (at, width) in W_AT.items():
        v = cols[name]
        assert v.shape[1] == width, (name, v.shape, width)
        weights[:v.shape[0], at:at + width] = v
    consts = np.concatenate([np.broadcast_to(cols[name][:P] if name != "esel" else
                                             np.pad(cols[name], ((0, P - 24), (0, 0))), (P, width))
                             for name, (_, width) in K_AT.items()], 1)
    tables = np.concatenate([cols[name] for name in TAB_AT], 1)
    row_values = {
        "bsw": i[f + "b_switch"], "rev": E - np.arange(E, dtype=f4), "base": CAP * np.arange(E, dtype=f4),
        "b2": i[f + "b2"].reshape(-1), "rb2": i[g + "rb2"], "fing": i[g + "ln_g"], "finb": i[g + "ln_b"],
        "pos": f4(1.0) / (f4(1.0) + f4(0.1) * np.log(pos)), "vb": ib[2 * C:], "one": np.ones(1, f4),
    }
    rows = np.zeros(R_WIDTH, f4)
    for name, (at, width) in R_AT.items():
        rows[at:at + width] = row_values[name]
    x = np.ascontiguousarray(i[m + "x"]).reshape(T, C)

    nc = bacc.Bacc("TRN2", target_bir_lowering=False, num_devices=1)
    x_d = nc.dram_tensor("x_in", x.shape, F32, kind="ExternalInput").ap()
    w_d = nc.dram_tensor("weights_in", weights.shape, F32, kind="ExternalInput").ap()
    r_d = nc.dram_tensor("rows_in", rows.shape, F32, kind="ExternalInput").ap()
    k_d = nc.dram_tensor("consts_in", consts.shape, F32, kind="ExternalInput").ap()
    tab_d = nc.dram_tensor("tables_in", tables.shape, F32, kind="ExternalInput").ap()
    out_d = nc.dram_tensor("out", (T, C), F32, kind="ExternalOutput").ap()
    build(nc, x_d, w_d, r_d, k_d, tab_d, out_d)
    r = run_bass_kernel_spmd(nc, [{"x_in": x, "weights_in": weights, "rows_in": rows, "consts_in": consts, "tables_in": tables}], core_ids=[0])
    return r.results[0]["out"].reshape(B, N, C)
```

```python
from contextlib import ExitStack

import concourse.bass as bass
from concourse import mybir

F32 = mybir.dt.float32
BF16 = mybir.dt.bfloat16
F16 = mybir.dt.float16
I32 = mybir.dt.int32
ALU = mybir.AluOpType
ACT = mybir.ActivationFunctionType
AX = mybir.AxisListType.X

RUN = ["mlla", "moe", "fhn", "moe", "causal", "gated", "fastw", "gated"]

P = 128
B, N, C = 2, 1024, 128
T = B * N
NT = T // P
CW = 512
NC = T // CW
TC = CW // P
H, D = 16, 8
NG = 4
GROUPS = B * NG
KT = N // P
E, CAP, HID = 8, 128, 512
SLOTS = E * CAP
M = 64
NEG = -1.0e30
UNITS = 12
MAXU = 48
HEAD = 16
RSQRT_SEED = 1597463007.0

COLS = [
    [("ident", 128), ("rot", 128), ("rotT", 128), ("blockm", 128), ("headm", 16),
     ("cpe1", 4), ("g1", 1), ("bn1", 1), ("inb", 1), ("actb", 1), ("dwc", 4), ("qb", 1), ("kb", 1), ("lepe", 4),
     ("outb", 1), ("cpe2", 4), ("g2", 1), ("bn2", 1), ("fc1b", 4), ("fc2b", 1),
     ("in", 128), ("actp", 128), ("qw", 128), ("kw", 128), ("ow", 128), ("fc1", 512), ("fc2", 512)],
    [("pcol", 8), ("wsw", 8), ("b1", 32), ("w1", E * HID),
     ("w2", 4 * E * 128)],
    [("fq", 128), ("fk", 128), ("fv", 128), ("fo", 128), ("fabd", 3),
     ("rq", 128), ("rqs", 128), ("rk", 128), ("rks", 128), ("rv", 128), ("rvs", 128),
     ("pq", 128), ("pk", 128), ("pv", 128), ("pqb", 1), ("pkb", 1), ("co", 128), ("cob", 1),
     ("W0", 128), ("AT", 128), ("Bi", 128), ("Wq", 128), ("Wk", 128), ("Wv", 128), ("Wo", 128), ("Wg", 128),
     ("lr", 1), ("lng", 1), ("lnb", 1), ("lsg", 1),
     ("enc", 256), ("encb", 2), ("s2c", 128), ("s2cb", 1), ("rW1", 64), ("rb1", 1), ("rW2", 8), ("We1", 1024),
     ("be1", 8), ("We2", 512), ("be2", 64), ("c2s", 256), ("c2sb", 2), ("dec", 256), ("decb", 1)],
]
ROWS = [("bsw", 8), ("rev", 8), ("base", 8), ("b2", E * 128), ("rb2", 8), ("fing", 128), ("finb", 128), ("pos", N),
        ("vb", 128), ("one", 1)]


def places(cols, start=0):
    at = {}
    for name, width in cols:
        at[name] = (start, width)
        start += width
    return at, start


W_AT, W_END = {}, [0]
for _part in COLS:
    _a, _e = places(_part, W_END[-1])
    W_AT.update(_a)
    W_END.append(_e)
R_AT, R_WIDTH = places(ROWS)
K_AT, K_WIDTH = places([("cmask", P), ("fmask", P), ("tri", P), ("ones", P), ("iota", SLOTS), ("esel", E * P)])
TAB_AT, TAB_WIDTH = places([("cosT", N), ("sinT", N)])


class Semaphores:
    pass


def build(nc, x_d, w_d, r_d, k_d, tab_d, out_d):
    with ExitStack() as ctx:
        def sb(name, shape, dt):
            return ctx.enter_context(nc.sbuf_tensor(name, shape, dt))

        def sem(name):
            return ctx.enter_context(nc.semaphore(name))

        s = Semaphores()
        s.k_in = sem("k_in")
        s.tab_in = sem("tab_in")
        s.x_in = sem("x_in")
        s.w_in0 = sem("w_in0")
        s.w_in1 = sem("w_in1")
        s.w_in2 = sem("w_in2")
        s.row_in = sem("row_in")
        s.dve_chain = sem("dve_chain")
        s.out_done = sem("out_done")
        s.ln_tn = sem("ln_tn")
        s.uT = sem("uT")
        s.u = sem("u")
        s.tokT = sem("tokT")
        s.ln_st = sem("ln_st")
        s.ln_ta = sem("ln_ta")
        s.y = sem("y")
        s.resT = sem("resT")
        s.res = sem("res")
        s.c1 = sem("c1")
        s.lin = sem("lin")
        s.silu = sem("silu")
        s.xc = sem("xc")
        s.v = sem("v")
        s.kq_relu = sem("kq_relu")
        s.kq_min = sem("kq_min")
        s.kq_exp = sem("kq_exp")
        s.qk = sem("qk")
        s.rden_den = sem("rden_den")
        s.rden_ev = sem("rden_ev")
        s.kmean = sem("kmean")
        s.vtokT = sem("vtokT")
        s.vtok = sem("vtok")
        s.gacc = sem("gacc")
        s.gev = sem("gev")
        s.z_st = sem("z_st")
        s.z_ld = sem("z_ld")
        s.z_rc = sem("z_rc")
        s.z_fs = sem("z_fs")
        s.z_fl = sem("z_fl")
        s.mnum = sem("mnum")
        s.att = sem("att")
        s.olin = sem("olin")
        s.x3 = sem("x3")
        s.fc1 = sem("fc1")
        s.hid = sem("hid")
        s.fc2 = sem("fc2")
        s.lg = sem("lg")
        s.oh = sem("oh")
        s.cum = sem("cum")
        s.slot = sem("slot")
        s.parts = sem("parts")
        s.slotT = sem("slotT")
        s.slotrow = sem("slotrow")
        s.slot_st = sem("slot_st")
        s.slot_ld = sem("slot_ld")
        s.onehot = sem("onehot")
        s.disp = sem("disp")
        s.xg = sem("xg")
        s.h_mm = sem("h_mm")
        s.h_act = sem("h_act")
        s.y_mm = sem("y_mm")
        s.yparts = sem("yparts")
        s.st_oh = sem("st_oh")
        s.comb = sem("comb")
        s.qkv_mm = sem("qkv_mm")
        s.q_sb = sem("q_sb")
        s.k_sb = sem("k_sb")
        s.vt_mm = sem("vt_mm")
        s.v_sb = sem("v_sb")
        s.v_st0 = sem("v_st0")
        s.v_st1 = sem("v_st1")
        s.hi = sem("hi")
        s.mid = sem("mid")
        s.lo = sem("lo")
        s.qs_st0 = sem("qs_st0")
        s.qs_st1 = sem("qs_st1")
        s.rope_mm = sem("rope_mm")
        s.rope = sem("rope")
        s.pm_ld0 = sem("pm_ld0")
        s.pm_ld1 = sem("pm_ld1")
        s.pe_ld0 = sem("pe_ld0")
        s.pe_ld1 = sem("pe_ld1")
        s.rows_ld0 = sem("rows_ld0")
        s.rows_ld1 = sem("rows_ld1")
        s.mx_mm = sem("mx_mm")
        s.mx_red = sem("mx_red")
        s.mT = sem("mT")
        s.m_sp = sem("m_sp")
        s.st_mm = sem("st_mm")
        s.pexp = sem("pexp")
        s.pmask = sem("pmask")
        s.av_mm = sem("av_mm")
        s.o_sb = sem("o_sb")
        s.o_st0 = sem("o_st0")
        s.o_st1 = sem("o_st1")
        s.fd_ld = sem("fd_ld")
        s.f_sig = sem("f_sig")
        s.f_pre = sem("f_pre")
        s.f_out = sem("f_out")
        s.sum_io = sem("sum_io")
        s.fb_ld = sem("fb_ld")
        s.oT = sem("oT")
        s.ofin = sem("ofin")
        s.w0x = sem("w0x")
        s.w0 = sem("w0")
        s.lwk = sem("lwk")
        s.lks = sem("lks")
        s.lerr = sem("lerr")
        s.lgrad = sem("lgrad")
        s.lq = sem("lq")
        s.lv = sem("lv")
        s.lo1 = sem("lo1")
        s.lgm = sem("lgm")
        s.lwo = sem("lwo")
        s.qk_mm = sem("qk_mm")
        s.ktokT = sem("ktokT")
        s.ktok = sem("ktok")
        s.hi2 = sem("hi2")
        s.rs2 = sem("rs2")
        s.mid2 = sem("mid2")
        s.rs = sem("rs")
        s.rope_t = sem("rope_t")
        s.v_one = sem("v_one")
        s.e_zero = sem("e_zero")
        s.m_zero = sem("m_zero")
        s.one_ld = sem("one_ld")
        s.mx_cmb = sem("mx_cmb")
        s.m_pt = sem("m_pt")
        s.x_dn = sem("x_dn")
        s.ly0 = sem("ly0")
        s.lgs = sem("lgs")
        s.llr = sem("llr")
        s.prep = sem("prep")
        s.e_mm = sem("e_mm")
        s.e_sp = sem("e_sp")
        s.s_mm = sem("s_mm")
        s.cont = sem("cont")
        s.r_mm = sem("r_mm")
        s.th = sem("th")
        s.l_mm = sem("l_mm")
        s.d12 = sem("d12")
        s.sg = sem("sg")
        s.gates = sem("gates")
        s.gT = sem("gT")
        s.g_zero = sem("g_zero")
        s.x_fb = sem("x_fb")
        s.gTs = sem("gTs")
        s.x_mm = sem("x_mm")
        s.x_rl = sem("x_rl")
        s.g_mm = sem("g_mm")
        s.x_h = sem("x_h")
        s.a_mm = sem("a_mm")
        s.a_sb = sem("a_sb")
        s.c_mm = sem("c_mm")
        s.c_sb = sem("c_sb")
        s.dd_mm = sem("dd_mm")
        s.dd_sb = sem("dd_sb")

        wt = sb("weights", [P, W_END[-1]], F32)
        rows = sb("rows", [P, R_WIDTH], F32)
        x = sb("x", [P, NT, C], F32)
        tn = sb("tn", [P, 2, NT, C], F32)
        u = sb("u", [P, T], F32)
        heap = sb("heap", [P, 10, T], F32)
        ps = ctx.enter_context(nc.psum_tensor("ps", [P, 8, CW], F32))
        st6 = sb("st6", [P, NT, 6], F32)
        sm = sb("sm", [P, 8, NT], F32)
        identb = sb("identb", [P, P], BF16)
        maskb = sb("maskb", [P, 2, P], BF16)
        mx = sb("mx", [P, 2, 2, 2, KT], F32)
        mneg = sb("mneg", [P, 32], F32)
        msq = sb("msq", [P, 2, 3, 16], BF16)
        mrs = sb("mrs", [P, 32], F32)
        msp = sb("msp", [96, 2, P], BF16)
        small = sb("small", [P, 64], F32)

        qk_d = nc.dram_tensor("qk", (GROUPS, 4, 2, 48, N), BF16, kind="Internal").ap()
        vs_d = nc.dram_tensor("vs", (GROUPS, P, KT * 128), F32, kind="Internal").ap()
        nd_d = nc.dram_tensor("nd", (GROUPS, 4, D + 1, N), F32, kind="Internal").ap()
        den_d = nc.dram_tensor("den", (GROUPS, 4, N), F32, kind="Internal").ap()
        fac_d = nc.dram_tensor("fac", (GROUPS, 4, N), F32, kind="Internal").ap()
        trib = sb("trib", [P, P], BF16)
        onesb = sb("onesb", [P, P], BF16)
        iota16 = sb("iota16", [P, SLOTS], F16)
        eselb = sb("eselb", [P, E * P], BF16)
        orow = sb("orow", [GROUPS * 4, N], BF16)
        ohb = sb("ohb", [P, NT * E], BF16)
        gate = sb("gate", [P, 6, NT * E], F32)
        g24 = sb("g24", [P, NT * 24], BF16)
        mats = sb("mats", [P, 6, P], F32)
        slot_d = nc.dram_tensor("slotrow", (NT, P), F16, kind="Internal").ap()

        consts = heap[:, 6:8, :].rearrange("p a b -> p (a b)")[:, 0:K_WIDTH]

        def w(name, rows_=P):
            a, n = W_AT[name]
            return wt[0:rows_, a:a + n]

        def wc(name, j, n=P, rows_=P):
            a, _ = W_AT[name]
            return wt[0:rows_, a + j * n:a + j * n + n]

        def kw(name):
            a, n = K_AT[name]
            return consts[:, a:a + n]

        def row(name):
            a, n = R_AT[name]
            return rows[:, a:a + n]

        def A(k, a=0, b=T):
            return heap[:, k, a:b]

        def ch(c):
            return c * CW, (c + 1) * CW

        def halves(k):
            v = heap[:, k, :].bitcast(BF16)
            return v[:, 0:T], v[:, T:2 * T]

        def bank(b, a=0, e=CW):
            return ps[:, b, a:e]

        ident = w("ident")

        plan, ln, tr, tk, yy = [], 0, 0, 0, 0
        seen = {}
        for kind in RUN:
            plan.append((kind, seen.get(kind, 0), ln, tr, tk, yy))
            seen[kind] = seen.get(kind, 0) + 1
            ln += {"mlla": 3, "fastw": 2}.get(kind, 1)
            tr += {"mlla": 3, "fastw": 2}.get(kind, 1)
            tk += {"mlla": 2, "gated": 1}.get(kind, 0)
            yy += 0 if kind == "gated" else 1
        attn_of = {}
        for kind in RUN:
            if kind in ("fhn", "causal"):
                attn_of[kind] = len(attn_of)

        block = ctx.enter_context(nc.Block())

        def pbuf(k):
            buf = heap[:, k % 4, :] if k % 4 < 2 else tn[:, k % 4 - 2].rearrange("p t c -> p (t c)")
            return buf.rearrange("p (j q) -> p j q", j=4)

        flat = heap[:, :, :].rearrange("p k t -> p (k t)").bitcast(BF16)

        def operands(k):
            a = 2 * 2 * T + k * 6 * N
            return flat[:, a:a + 6 * N].rearrange("p (j t) -> p j t", j=6)

        def qe(par):
            return operands(par)[:, 0:4, :]

        def ke(par):
            return operands(par)[:, 4:6, :]

        def qm(par):
            return operands(2 + par)[:, 0:4, :]

        def km(par):
            return operands(2 + par)[:, 4:6, :]

        def loads(k, i, jp):
            for o, tile in ((0, 2 * jp), (1, 4)):
                yield (operands(k)[64 * jp:64 * jp + 48, tile:tile + 2, :],
                       qk_d[i].rearrange("(j e) o r t -> e o r j t", e=2)[jp, o])

        def zeroed(k):
            a = 2 * T + k * 3 * N
            return heap[:, :, :].rearrange("p k t -> p (k t)")[:, a:a + 3 * N]

        def vst(par):
            return heap[:, 8, par * 1024:(par + 1) * 1024].rearrange("p (k j r) -> p k j r", k=KT, j=4)

        def oraw(par):
            return heap[:, 9, par * N:(par + 1) * N]

        QH, QMI = halves(2)
        QL, KH = halves(3)
        KMI, KL = halves(4)
        SPLITQ = [QH, QH, QMI, QMI, QH, QL]
        SPLITK = [KH, KMI, KH, KMI, KL, KH]

        def tiles_of(ap):
            return lambda t: ap[:, t, :]

        def psum_tile(t):
            return bank(4 + t // TC, (t % TC) * P, (t % TC) * P + P)

        LN_DVE, LN_ACT = (0, 2), (1, 3)

        def wait_ln(eng, n):
            eng.wait_ge(s.ln_tn, len(LN_DVE) * (n + 1))
            eng.wait_ge(s.ln_ta, len(LN_ACT) * (n + 1))

        def seq(ap, b):
            return ap[:, b * N:(b + 1) * N]

        rest_q, rest_k = (tn[:, k].rearrange("p t c -> p (t c)") for k in range(2))

        def onehot(t):
            return heap[:, 3, :].bitcast(BF16).rearrange("p (k s) -> p k s", k=4)[:, t % 4, :]

        def back(e):
            return halves(7 + 2 * (e % 4 // 2))[e % 2]

        def hbuf(e):
            return heap[:, 6, 1024 + (e % 2) * CW:1024 + (e % 2) * CW + CW].rearrange("p (j q) -> p j q", j=4)

        def vp(k):
            return heap[:, 7 + k, :].rearrange("p (t h r) -> p t h r", t=TC, h=H)

        w_in = (s.w_in0, s.w_in1, s.w_in2)
        PART = {"mlla": 0, "moe": 1}

        pm_ld, pe_ld, rows_ld = (s.pm_ld0, s.pm_ld1), (s.pe_ld0, s.pe_ld1), (s.rows_ld0, s.rows_ld1)
        v_st, o_st = (s.v_st0, s.v_st1), (s.o_st0, s.o_st1)
        qs_st = (s.qs_st0, s.qs_st1)

        def strips():
            k = 0
            for j2 in range(2):
                for qt in range(KT):
                    for kc in range(1 + qt // 4):
                        width = min(CW, (qt + 1) * P - kc * CW)
                        for jp in range(2):
                            yield k, jp, j2, qt, kc, width
                            k += 1

        STRIPS = list(strips())

        STEPS = [(qh, kt, max(0, kt - 4 * qh) * P) for qh in range(2) for kt in range(4 * qh + 4)]

        SPREAD = (1, 1, 2)
        TURN = (MAXU - HEAD) // 4

        @block.sync
        def _(sp):
            sp.dma_start(x[:, :, :], x_d.rearrange("(t p) c -> p t c", p=P)).then_inc(s.x_in, 16)
            for k in range(3):
                sp.dma_start(wt[:, W_END[k]:W_END[k + 1]], w_d[:, W_END[k]:W_END[k + 1]]).then_inc(w_in[k], 16)
                if k == 0:
                    sp.dma_start(consts, k_d).then_inc(s.k_in, 16)
                    sp.dma_start(rows[:, :], r_d.partition_broadcast(P)).then_inc(s.row_in, 16)

            def mlla():
                sp.wait_ge(s.prep, 1)
                sp.wait_ge(s.rden_ev, 4)
                for b in range(B):
                    sp.dma_start(den_d[b * NG:(b + 1) * NG, :, :].rearrange("g j t -> (g j) t"),
                                 heap[0:H, 8, b * N:(b + 1) * N]).then_inc(s.z_st, 16)
                sp.wait_ge(s.z_st, 32)
                sp.dma_start(A(7, 0, 256), den_d.rearrange("i j t -> (i j t)").rearrange("(p f) -> p f", p=P)
                             ).then_inc(s.z_ld, 16)
                sp.wait_ge(s.z_rc, 1)
                sp.dma_start(fac_d.rearrange("i j t -> (i j t)").rearrange("(p f) -> p f", p=P),
                             A(7, 256, 512)).then_inc(s.z_fs, 16)
                sp.wait_ge(s.z_fs, 16)
                broadcast_fac(6, s.z_fl)

            def broadcast_fac(slot, done):
                for b in range(B):
                    heads = fac_d[b * NG:(b + 1) * NG].rearrange("g j t -> (g j) t").unsqueeze(1)
                    sp.dma_start(heap[:, slot, b * N:(b + 1) * N], heads.broadcast_to((H, D, N))).then_inc(done, 16)

            def moe(n):
                sp.wait_ge(s.slotrow, n + 1)
                sp.dma_start(slot_d, halves(8)[1].bitcast(F16)[0:NT, 0:P]).then_inc(s.slot_st, 16)
                sp.wait_ge(s.slot_st, 16 * (n + 1))
                sp.dma_start(halves(8)[0].bitcast(F16), slot_d.rearrange("t p -> (t p)").partition_broadcast(P)
                             ).then_inc(s.slot_ld, 16)

            def stage_exp(a, i, par):
                for jp in range(2):
                    for dst, src in loads(par, i, jp):
                        sp.dma_start(dst, src).then_inc(pe_ld[par], 16)
                sp.dma_start(heap[:, 8, par * 1024:(par + 1) * 1024], vs_d[i]).then_inc(pe_ld[par], 16)
                sp.wait_ge(s.m_sp, GROUPS * a + i + 1)
                for jp in range(2):
                    sp.dma_start(qe(par)[64 * jp + 48:64 * jp + 51, 2 * jp:2 * jp + 2, :],
                                 msp[48 * jp:48 * jp + 48, par, :]).then_inc(rows_ld[par], 16)

            def store_out(a, i, par):
                sp.wait_ge(s.o_sb, 2 * (GROUPS * a + i) + 3)
                for j in range(4):
                    sp.dma_start(nd_d[i, j], oraw(par)[32 * j:32 * j + D + 1]).then_inc(o_st[par], 16)

            def attention(a):
                for b in range(B):
                    for made, parts in ((s.hi, (QH, KH)), (s.mid, (QMI, KMI)), (s.lo, (QL, KL))):
                        for o, part in enumerate(parts):
                            sp.wait_ge(made, 2 * B * a + 2 * b + o + 1)
                            for k in range(6):
                                if (SPLITQ, SPLITK)[o][k] is part:
                                    sp.dma_start(qk_d[b * NG:(b + 1) * NG, :, o, 8 * k:8 * k + 8, :]
                                                 .rearrange("g j d t -> (g j) d t"), seq(part, b)
                                                 ).then_inc(qs_st[b], 16)
                    for c in (2 * b, 2 * b + 1):
                        sp.wait_ge(s.v_sb, NC * a + c + 1)
                        for t in range(TC):
                            k0 = ((c % 2) * TC + t) * 128
                            sp.dma_start(vs_d[b * NG:(b + 1) * NG, :, k0:k0 + 128].rearrange("g p r -> p g r"),
                                         heap[:, 7 + c % 2, t * 512:(t + 1) * 512].rearrange("p (g r) -> p g r", g=NG)
                                         ).then_inc(v_st[c % 2], 16)
                for b in range(B):
                    sp.wait_ge(qs_st[b], 16 * 12 * (a + 1))
                for k in range(2):
                    sp.wait_ge(v_st[k], 16 * TC * 2 * (a + 1))
                sp.wait_ge(s.e_zero, 2 * (a + 1))
                for par in range(2):
                    for jp in range(2):
                        sp.dma_start(ke(par)[64 * jp + 48:64 * jp + 51, :, :], orow[0:6, :]).then_inc(s.one_ld, 16)
                stage_exp(a, 0, 0)
                stage_exp(a, 1, 1)
                with sp.Fori(0, GROUPS // 2 - 1) as it:
                    for par in range(2):
                        i = 2 * it + par
                        store_out(a, i, par)
                        sp.wait_ge(s.av_mm, UNITS * GROUPS * a + UNITS * (i + 1))
                        stage_exp(a, i + 2, par)
                for i in (GROUPS - 2, GROUPS - 1):
                    store_out(a, i, i % 2)
                for k in range(2):
                    sp.wait_ge(o_st[k], 64 * (GROUPS // 2 * (a + 1) + 1))
                sp.wait_ge(s.pm_ld0, 64 * 4 * (a + 1))
                sp.wait_ge(s.pm_ld1, 64 * 4 * (a + 1))
                sp.dma_start(A(5, 0, 256), nd_d[:, :, D, :].rearrange("i j t -> (i j) t")).then_inc(s.sum_io, 16)
                for b in range(B):
                    sp.dma_start(A(2, b * N, (b + 1) * N),
                                 nd_d[b * NG:(b + 1) * NG, :, 0:D, :].rearrange("g j d t -> (g j) d t")
                                 ).then_inc(s.fd_ld, 16)
                sp.wait_ge(s.f_out, a + 1)
                sp.dma_start(fac_d.rearrange("i j t -> (i j t)").rearrange("(p f) -> p f", p=P),
                             A(5, 256, 512)).then_inc(s.sum_io, 16)
                sp.wait_ge(s.sum_io, 32 * (a + 1))
                broadcast_fac(3, s.fb_ld)

            for bi, (kind, n, ln0, tr0, tk0, y0) in enumerate(plan):
                if kind == "causal":
                    sp.wait_ge(s.res, NC * bi)
                    sp.dma_start(A(2), tab_d).then_inc(s.tab_in, 16)
                if kind == "mlla":
                    mlla()
                elif kind == "moe":
                    moe(n)
                elif kind in attn_of:
                    attention(attn_of[kind])
            nout = len(RUN)
            for c in range(NC):
                sp.wait_ge(s.res, NC * (nout - 1) + c + 1)
                sp.dma_start(out_d[c * CW:(c + 1) * CW, :].rearrange("(t p) c -> p t c", p=P),
                             x[:, TC * c:TC * c + TC, :]).then_inc(s.out_done, 16)
            sp.wait_ge(s.out_done, 16 * NC)


        def chain(eng, sem):
            count = [0]

            def link(ins):
                count[0] += 1
                ins.then_inc(sem, 1)
                eng.wait_ge(sem, count[0])
            return link

        def bc(ap, shape):
            return ap.broadcast_to(shape)

        @block.tensor
        def _(pe):
            def ln_T(n, k):
                pe.wait_ge(s.u, NC * k)
                for c in range(NC):
                    pe.wait_ge(s.ln_tn if c in LN_DVE else s.ln_ta, 2 * n + c // 2 + 1)
                    for t in range(TC):
                        m = pe.transpose(bank(c, t * P, t * P + P), tn[:, n % 2, TC * c + t, :], ident)
                    m.then_inc(s.uT, 1)

            def tok_T(k, slot, ready, count):
                for c in range(NC):
                    pe.wait_ge(ready, count(c))
                    for t in range(TC):
                        a = (TC * c + t) * P
                        m = pe.transpose(bank(4 + c, t * P, t * P + P), A(slot, a, a + P), ident)
                    m.then_inc(s.tokT, 1)

            def res_T(k, slot):
                for c in range(NC):
                    pe.wait_ge(s.y, NC * k + c + 1)
                    for t in range(TC):
                        a = (TC * c + t) * P
                        m = pe.transpose(bank(4 + c, t * P, t * P + P), A(slot, a, a + P), ident)
                    m.then_inc(s.resT, 1)

            def mlla(n, ln0, tr0, tk0, y0):
                tok_T(tk0, 0, s.c1, lambda c: c // 2 + 1)
                ln_T(ln0 + 1, tr0 + 1)
                for c in range(NC):
                    pe.wait_ge(s.u, NC * (tr0 + 1) + c + 1)
                    pe.matmul(bank(c), w("actp"), A(1, *ch(c)), start=True, stop=True)
                    pe.matmul(bank(4 + c), w("in"), A(1, *ch(c)), start=True, stop=True).then_inc(s.lin, 1)
                for c in range(NC):
                    pe.wait_ge(s.v, c // 2 + 1)
                    pe.wait_ge(s.silu, c + 1)
                    pe.matmul(bank(c), w("qw"), A(5, *ch(c)), start=True, stop=True)
                    pe.matmul(bank(4 + c), w("kw"), A(5, *ch(c)), start=True, stop=True).then_inc(s.qk_mm, 1)
                for c in range(NC):
                    pe.wait_ge(s.kq_min, 2 * c + 2)
                    pe.wait_ge(s.kq_relu, 2 * c + 2)
                    for t in range(TC):
                        a = (TC * c + t) * P
                        m = pe.transpose(bank(c, t * P, t * P + P), A(5, a, a + P), ident)
                    m.then_inc(s.vtokT, 1)
                for c in range(NC):
                    pe.wait_ge(s.qk, 2 * c + 2)
                    for t in range(TC):
                        a = (TC * c + t) * P
                        m = pe.transpose(bank(4 + c, t * P, t * P + P), A(4, a, a + P), ident)
                    m.then_inc(s.ktokT, 1)
                for c in range(NC):
                    pe.wait_ge(s.kmean, c // 2 + 1)
                    pe.wait_ge(s.vtok, c + 1)
                    pe.matmul(ps[0:H, c, :], small[:, 16 + H * (c // 2):16 + H * (c // 2) + H], A(3, *ch(c)),
                              start=True, stop=True).then_inc(s.rden_den, 1)
                pe.wait_ge(s.ktok, NC)
                for b in range(B):
                    for t in range(KT):
                        a = b * N + t * P
                        m = pe.matmul(bank(4 + b, 0, P), A(1, a, a + P), A(9, a, a + P),
                                      start=(t == 0), stop=(t == KT - 1))
                    m.then_inc(s.gacc, 1)
                for b in range(B):
                    pe.wait_ge(s.gev, b + 1)
                    pe.matmul(bank(4 + b, P, 2 * P), w("rot"), mats[:, b, :], start=True, stop=True).then_inc(s.gacc, 1)
                for b in range(B):
                    pe.wait_ge(s.gev, B + b + 1)
                    pe.matmul(bank(4 + b, 2 * P, 3 * P), w("rotT"), mats[:, 2 + b, :],
                              start=True, stop=True).then_inc(s.gacc, 1)
                for c in range(NC):
                    pe.wait_ge(s.gev, 2 * B + c // 2 + 1)
                    pe.wait_ge(s.rden_ev, c + 1)
                    pe.matmul(bank(c), mats[:, 4 + c // 2, :], A(3, *ch(c)), start=True, stop=True).then_inc(s.mnum, 1)
                for c in range(NC):
                    pe.wait_ge(s.att, c + 1)
                    pe.matmul(bank(4 + c), w("ow"), A(4, *ch(c)), start=True, stop=True).then_inc(s.olin, 1)
                tok_T(tk0 + 1, 5, s.x3, lambda c: c // 2 + 1)
                ln_T(ln0 + 2, tr0 + 2)
                pe.wait_ge(s.u, NC * (tr0 + 3))

                def fc1(c):
                    for j in range(4):
                        if c:
                            pe.wait_ge(s.hid, 4 * (c - 1) + j + 1)
                        pe.matmul(bank(j), wc("fc1", j), A(1, *ch(c)), start=True, stop=True).then_inc(s.fc1, 1)

                def fc2(c):
                    for j in range(4):
                        pe.wait_ge(s.hid, 4 * c + j + 1)
                        m = pe.matmul(bank(4 + c), wc("fc2", j), A(6 + c % 2, j * CW, j * CW + CW),
                                      start=(j == 0), stop=(j == 3))
                    m.then_inc(s.fc2, 1)

                for c in range(NC + 1):
                    if c < NC:
                        fc1(c)
                    if c:
                        fc2(c - 1)
                res_T(y0, 8)

            def moe(n, ln0, tr0, tk0, y0):
                pe.wait_ge(s.u, NC * (tr0 + 1))
                for t in range(NT):
                    m = pe.matmul(bank(4, t * E, t * E + E), u[:, t * P:t * P + P], w("wsw"), start=True, stop=True)
                m.then_inc(s.lg, 1)
                pe.wait_ge(s.oh, n + 1)
                pe.matmul(bank(5, 0, NT * E), trib[:, :], ohb[:, :], start=True, stop=False)
                for k in range(1, NT):
                    m = pe.matmul(bank(5, k * E, NT * E), onesb[:, :], ohb[:, 0:(NT - k) * E],
                                  start=False, stop=(k == NT - 1))
                m.then_inc(s.cum, 1)
                pe.wait_ge(s.slot, n + 1)
                pe.transpose(ps[0:NT, 5, 256:384], sm[:, 7, :], ident).then_inc(s.slotT, 1)
                parts = (halves(0)[0], halves(0)[1], halves(1)[0])
                pe.wait_ge(s.parts, n + 1)
                for t in range(NT):
                    pe.wait_ge(s.onehot, NT * n + t + 1)
                    for half in range(2):
                        for k in range(3):
                            m = pe.matmul(bank(6 + half), parts[k][:, t * P:t * P + P],
                                          onehot(t)[:, half * CW:half * CW + CW],
                                          start=(t == 0 and k == 0), stop=(t == NT - 1 and k == 2))
                    m.then_inc(s.disp, 1)
                pe.wait_ge(s.xg, 2 * (n + 1))

                def up(e):
                    if e >= 2:
                        pe.wait_ge(s.h_act, 4 * (E * n + e - 1))
                    for j in range(4):
                        m = pe.matmul(bank(e % 2, j * P, j * P + P), wc("w1", 4 * e + j),
                                      A(4, e * CAP, e * CAP + CAP), start=True, stop=True)
                    m.then_inc(s.h_mm, 1)

                def down(e):
                    pe.wait_ge(s.h_act, 4 * (E * n + e + 1))
                    for j in range(4):
                        m = pe.matmul(bank(2 + e // 4, (e % 4) * P, (e % 4) * P + P), hbuf(e)[:, j, :],
                                      wc("w2", 4 * e + j), start=(j == 0), stop=(j == 3))
                    m.then_inc(s.y_mm, 1)

                for e in range(E + 1):
                    if e < E:
                        up(e)
                    if e:
                        down(e - 1)
                yp = heap[:, 5, :].bitcast(BF16)
                pe.wait_ge(s.yparts, 2 * (n + 1))
                for e in range(E):
                    pe.wait_ge(s.st_oh, E * n + e + 1)
                    for k in range(3):
                        a = k * SLOTS + e * CAP
                        for c in range(NC):
                            m = pe.matmul(bank(c), yp[:, a:a + CAP], back(e)[:, c * CW:c * CW + CW],
                                          start=(e == 0 and k == 0), stop=(e == E - 1 and k == 2))
                    m.then_inc(s.comb, 1)
                res_T(y0, 0)

            def attention(a, kind, tr0, y0):
                if kind == "fhn":
                    for c in range(NC):
                        pe.wait_ge(s.u, NC * tr0 + c + 1)
                        pe.matmul(bank(c), w("fq"), u[:, c * CW:c * CW + CW], start=True, stop=True)
                        pe.matmul(bank(4 + c), w("fk"), u[:, c * CW:c * CW + CW],
                                  start=True, stop=True).then_inc(s.qkv_mm, 1)
                else:
                    pe.wait_ge(s.u, NC * (tr0 + 1))
                    for k, (wa, wb) in enumerate((("rq", "rqs"), ("rk", "rks"), ("rv", "rvs"))):
                        for c in range(NC):
                            p = NC * k + c
                            if p >= 4:
                                pe.wait_ge(s.rope_t, p - 3)
                            pe.matmul(bank(2 * p % 8), w(wa), u[:, c * CW:c * CW + CW], start=True, stop=True)
                            pe.matmul(bank(2 * p % 8 + 1), w(wb), u[:, c * CW:c * CW + CW],
                                      start=True, stop=True).then_inc(s.rope_mm, 1)
                    pe.wait_ge(s.rope_t, 3 * NC)
                    for c in range(NC):
                        pe.wait_ge(s.rope, NC + c + 1)
                        pe.matmul(bank(c), w("pq"), A(5, *ch(c)), start=True, stop=True)
                        pe.matmul(bank(4 + c), w("pk"), A(6, *ch(c)), start=True, stop=True).then_inc(s.qkv_mm, 1)
                    pe.wait_ge(s.rope, 3 * NC)
                for c in range(NC):
                    pe.wait_ge(s.q_sb, NC * a + c + 1)
                    for t in range(TC):
                        k = (TC * c + t) * P
                        lhs = u[:, k:k + P] if kind == "fhn" else A(9, k, k + P)
                        m = pe.matmul(bank(c, t * P, t * P + P), lhs, w("fv" if kind == "fhn" else "pv"),
                                      start=True, stop=True)
                    m.then_inc(s.vt_mm, 1)
                pe.wait_ge(s.k_sb, NC * (a + 1))

                def strip(g, par, k):
                    _, jp, j2, qt, kc, width = STRIPS[k]
                    if not (isinstance(g, int) and g == 0 and k < 3):
                        pe.wait_ge(s.mx_red, MAXU * g + (k - 2))
                    last = kc == qt // 4
                    m = pe.matmul(bank(5 + k % 3, 0, width), qm(par)[:, 2 * jp + j2, qt * P:qt * P + P],
                                  km(par)[:, j2, kc * CW:kc * CW + width], start=True, stop=True)
                    if last:
                        m = pe.matmul(bank(5 + k % 3, width - P, width), identb[:, :],
                                      maskb[:, 0 if kind == "causal" else 1, :], start=False, stop=True,
                                      skip_group_check=True)
                    m.then_inc(s.mx_mm, 1)

                def turn_max(g):
                    pe.wait_ge(s.m_pt, 4 * g + 4)
                    pe.transpose(ps[0:96, 7, 0:64].bitcast(BF16), msq[:, :, :, :].rearrange("p a k b -> p (a k b)"),
                                 identb[:, :]).then_inc(s.mT, 1)

                def scores(g, par, k, j2, first=False):
                    qh, kt, off = STEPS[k]
                    if not first:
                        pe.wait_ge(s.pexp, 2 * UNITS * g + (2 * k + j2 - 1))
                    for jp in range(2):
                        m = pe.matmul(bank(2 * j2 + jp, 0, CW - off),
                                      ke(par)[:, j2, kt * P:kt * P + P],
                                      qe(par)[:, 2 * jp + j2, qh * CW + off:qh * CW + CW],
                                      start=True, stop=True)
                    m.then_inc(s.st_mm, 1)

                def values(g, par, k):
                    qh, kt, off = STEPS[k]
                    if kt == 0:
                        pe.wait_ge(s.o_sb, 2 * g + (qh + 1))
                    if kt >= 4 * qh:
                        pe.wait_ge(s.pmask, 8 * g + (4 * qh + kt - 4 * qh + 1))
                    else:
                        pe.wait_ge(s.pexp, 2 * UNITS * g + (2 * k + 2))
                    for j in range(4):
                        m = pe.matmul(ps[32 * j:32 * j + 32, 4, off:CW], vst(par)[:, kt, j, :],
                                      pbuf(k)[:, j, 0:CW - off], start=(kt == 0), stop=(kt >= 4 * qh),
                                      skip_group_check=True)
                    m.then_inc(s.av_mm, 1)

                def loaded(it, par):
                    r = GROUPS // 2 * a + it
                    pe.wait_ge(pe_ld[par], 80 * r + 80)
                    pe.wait_ge(rows_ld[par], 32 * r + 32)

                def group(it, par, turn, ahead):
                    g = GROUPS * a + 2 * it + par
                    r = GROUPS // 2 * a + it

                    def strips_at(k, place):
                        at = 4 * k + sum(SPREAD[:place])
                        for p in range(HEAD + at, HEAD + at + SPREAD[place]):
                            if p < MAXU and turn:
                                strip(g + 1, 1 - par, p)
                            elif p >= MAXU and ahead:
                                if p == MAXU:
                                    pe.wait_ge(pm_ld[par], 64 * (r + 1) + 64)
                                if p == MAXU + 2:
                                    pe.wait_ge(s.m_sp, g + 2)
                                strip(g + 2, par, p - MAXU)

                    for k in range(UNITS):
                        for j2 in range(2):
                            strips_at(k, j2)
                            if k + 1 < UNITS:
                                scores(g, par, k + 1, j2)
                        if turn and k == TURN:
                            turn_max(g + 1)
                        strips_at(k, 2)
                        if k:
                            values(g, par, k - 1)
                    if turn:
                        loaded(it + par, 1 - par)
                        for j2 in range(2):
                            scores(g + 1, 1 - par, 0, j2)
                    values(g, par, UNITS - 1)

                g0 = GROUPS * a
                pe.wait_ge(pm_ld[0], 64 * (GROUPS // 2 * a) + 64)
                for k in range(MAXU):
                    strip(g0, 0, k)
                pe.wait_ge(pm_ld[1], 64 * (GROUPS // 2 * a) + 64)
                for k in range(2):
                    strip(g0 + 1, 1, k)
                turn_max(g0)
                pe.wait_ge(s.m_sp, g0 + 1)
                for k in range(2, HEAD):
                    strip(g0 + 1, 1, k)
                pe.wait_ge(s.v_sb, NC * (a + 1))
                pe.wait_ge(s.one_ld, 64 * (a + 1))
                loaded(0, 0)
                for j2 in range(2):
                    scores(g0, 0, 0, j2, first=True)
                with pe.Fori(0, GROUPS // 2 - 1) as it:
                    for par in range(2):
                        group(it, par, True, True)
                group(GROUPS // 2 - 1, 0, True, False)
                group(GROUPS // 2 - 1, 1, False, False)
                for c in range(NC):
                    pe.wait_ge(s.oT, NC * a + c + 1)
                    pe.matmul(bank(c), w("fo" if kind == "fhn" else "co"), A(4, *ch(c)),
                              start=True, stop=True).then_inc(s.ofin, 1)
                res_T(y0, 6)

            def gated(n, ln0, tr0, tk0, y0):
                def encode(c):
                    if c >= 2:
                        pe.wait_ge(s.e_sp, 2 * (NC * n + c - 1))
                    for hf in range(2):
                        m = pe.matmul(bank(2 * (c % 2) + hf), wc("enc", hf), u[:, c * CW:c * CW + CW],
                                      start=True, stop=True)
                    m.then_inc(s.e_mm, 1)

                def to_cont(c):
                    pe.wait_ge(s.e_sp, 2 * (NC * n + c + 1))
                    for hf in range(2):
                        a = (2 * (c % 2) + hf) * CW
                        m = pe.matmul(ps[M * hf:M * hf + M, 4 + c, :], wc("s2c", hf, M), A(0, a, a + CW),
                                      start=True, stop=True, skip_group_check=True)
                    m.then_inc(s.s_mm, 1)

                pe.wait_ge(s.u, NC * tr0 + NC)
                for c in range(NC + 1):
                    if c < NC:
                        encode(c)
                    if c:
                        to_cont(c - 1)
                for c in range(NC):
                    pe.wait_ge(s.cont, NC * n + c + 1)
                    pe.matmul(ps[0:M, 4 + c, :], w("rW1"), A(1, *ch(c)), start=True, stop=True).then_inc(s.r_mm, 1)
                for t in range(NT):
                    pe.wait_ge(s.th, NC * n + t // TC + 1)
                    m = pe.matmul(bank(2, t * E, t * E + E), heap[0:M, 2, t * P:t * P + P], w("rW2", M),
                                  start=True, stop=True)
                m.then_inc(s.l_mm, 1)

                def hidden(q):
                    if q >= 2:
                        pe.wait_ge(s.x_rl, NC * E * n + q - 1)
                    pe.matmul(bank(q % 2), wc("We1", q % E), A(1, *ch(q // E)), start=True, stop=True).then_inc(s.x_mm, 1)

                for q in range(4):
                    hidden(q)
                pe.wait_ge(s.gates, n + 1)
                gview = ps[:, 2:4, :].rearrange("p a b -> p (a b)").bitcast(BF16)
                for t in range(NT):
                    m = pe.transpose(gview[0:24, t * P:t * P + P], g24[:, t * 24:t * 24 + 24], identb[:, :])
                m.then_inc(s.gT, 1)
                for t in range(NT):
                    m = pe.transpose(ps[0:E, 4 + t // TC, (t % TC) * P:(t % TC) * P + P],
                                     gate[:, 3, t * E:t * E + E], ident)
                m.then_inc(s.gT, 1)
                pe.wait_ge(s.gTs, 2 * (n + 1))

                def up(q):
                    c, e = q // E, q % E
                    g = NC * E * n + q
                    if q >= 4:
                        hidden(q)
                    if q >= 2:
                        pe.wait_ge(s.x_h, g - 1)
                    pe.matmul(bank(2 + q % 2), eselb[:, e * P:e * P + P], halves(3)[0][:, c * CW:c * CW + CW],
                              start=True, stop=True).then_inc(s.g_mm, 1)

                def down(q):
                    c, e = q // E, q % E
                    pe.wait_ge(s.x_h, NC * E * n + q + 2)
                    for k in range(2):
                        a = ((q + k) % 4) * CW
                        pe.matmul(ps[M * k:M * k + M, 4 + c, :], wc("We2", e + k, M), A(6, a, a + CW),
                                  start=(e == 0), stop=(k == 1 and e == E - 2),
                                  skip_group_check=True).then_inc(s.x_dn, 1)
                    if e == E - 2:
                        pe.matmul(ps[0:M, 4 + c, :], w("be2"), A(4, *ch(c)), start=False, stop=True,
                                  skip_group_check=True).then_inc(s.a_mm, 1)

                for q in range(0, NC * E + 2, 2):
                    if q < NC * E:
                        up(q)
                        up(q + 1)
                    if q:
                        down(q - 2)

                def to_spikes(c):
                    pe.wait_ge(s.a_sb, NC * n + c + 1)
                    if c >= 2:
                        pe.wait_ge(s.c_sb, 2 * (NC * n + c - 1))
                    for hf in range(2):
                        m = pe.matmul(bank(2 * (c % 2) + hf), wc("c2s", hf), A(7, *ch(c)), start=True, stop=True)
                    m.then_inc(s.c_mm, 1)

                def decode(c):
                    pe.wait_ge(s.c_sb, 2 * (NC * n + c + 1))
                    for hf in range(2):
                        a = (2 * (c % 2) + hf) * CW
                        m = pe.matmul(bank(4 + c), wc("dec", hf), A(8, a, a + CW), start=(hf == 0), stop=(hf == 1))
                    m.then_inc(s.dd_mm, 1)

                for c in range(NC + 1):
                    if c < NC:
                        to_spikes(c)
                    if c:
                        decode(c - 1)
                tok_T(tk0, 9, s.dd_sb, lambda c: NC * n + c + 1)

            def fastw(n, ln0, tr0, tk0, y0):
                ln_T(ln0 + 1, tr0 + 1)
                pe.matmul(bank(4, 0, P), w("AT", E), w("Bi", E), start=True, stop=True).then_inc(s.w0x, 1)
                hs = 0
                for c in range(NC):
                    pe.wait_ge(s.u, NC * (tr0 + 1) + c + 1)
                    pe.matmul(bank(c), w("Wk"), A(hs, *ch(c)), start=True, stop=True).then_inc(s.lwk, 1)
                pe.wait_ge(s.w0, 2)
                for c in range(NC):
                    pe.wait_ge(s.lks, c + 1)
                    pe.matmul(bank(4 + c), mats[:, 0, :], A(1, *ch(c)), start=True, stop=True).then_inc(s.lv, 1)
                    pe.matmul(bank(c), mats[:, 0, :], A(1, *ch(c)), start=True, stop=False)
                    pe.matmul(bank(c), mats[:, 1, :], A(hs, *ch(c)), start=False, stop=True).then_inc(s.lerr, 1)
                for c in range(NC):
                    pe.wait_ge(s.ly0, c + 1)
                    pe.matmul(bank(4 + c), w("Wq"), A(hs, *ch(c)), start=True, stop=True).then_inc(s.lq, 1)
                for c in range(NC):
                    pe.wait_ge(s.lgrad, c + 1)
                    pe.matmul(bank(c), w("Wg"), u[:, c * CW:c * CW + CW], start=True, stop=True).then_inc(s.lgm, 1)
                for c in range(NC):
                    pe.wait_ge(s.lo1, c + 1)
                    pe.matmul(bank(4 + c), w("Wo"), A(6, *ch(c)), start=True, stop=True).then_inc(s.lwo, 1)
                res_T(y0, 8)

            pe.wait_ge(s.w_in0, 16)
            for kind, n, ln0, tr0, tk0, y0 in plan:
                ln_T(ln0, tr0)
                pe.wait_ge(w_in[PART.get(kind, 2)], 16)
                if kind != "mlla":
                    pe.wait_ge(s.prep, 1)
                if kind in attn_of:
                    attention(attn_of[kind], kind, tr0, y0)
                else:
                    {"mlla": mlla, "moe": moe, "gated": gated, "fastw": fastw}[kind](n, ln0, tr0, tk0, y0)

        @block.scalar
        def _(act):
            def fn(out, in_, f=ACT.Identity, bias=0.0, scale=1.0):
                return act.activation(out, in_, f, bias=bias, scale=scale)

            def ln_copy(k, dst, g=None, b=None):
                for c in range(NC):
                    act.wait_ge(s.uT, NC * k + c + 1)
                    if g is None:
                        fn(dst[:, c * CW:c * CW + CW], bank(c), ACT.Copy).then_inc(s.u, 1)
                    else:
                        fn(dst[:, c * CW:c * CW + CW], bank(c), bias=b, scale=g).then_inc(s.u, 1)

            def normalise(n, tile):
                act.wait_ge(s.ln_st, n + 1)
                for c in LN_ACT:
                    for t in range(TC * c, TC * c + TC):
                        m = fn(tn[:, n % 2, t, :], tile(t), bias=sm[:, 6, t:t + 1], scale=sm[:, 1, t:t + 1])
                    m.then_inc(s.ln_ta, 1)

            def mlla(n, ln0, tr0, tk0, y0):
                normalise(ln0 + 1, psum_tile)
                ln_copy(tr0 + 1, A(1), w("g1"), w("bn1"))
                for c in range(NC):
                    act.wait_ge(s.lin, c + 1)
                    fn(A(2, *ch(c)), bank(c), ACT.Silu, bias=w("actb")).then_inc(s.silu, 1)
                for b in range(B):
                    act.wait_ge(s.xc, b + 1)
                    fn(A(5, b * N, b * N + N), A(4, b * N, b * N + N), ACT.Silu).then_inc(s.v, 1)
                for c in range(NC):
                    act.wait_ge(s.kq_min, 2 * c + 1)
                    fn(A(3, *ch(c)), bank(c), ACT.Relu, bias=w("qb")).then_inc(s.kq_relu, 1)
                    act.wait_ge(s.kq_min, 2 * c + 2)
                    fn(A(4, *ch(c)), bank(4 + c), ACT.Relu, bias=w("kb")).then_inc(s.kq_relu, 1)
                    fn(A(9, *ch(c)), A(9, *ch(c)), ACT.Exp).then_inc(s.kq_exp, 1)
                    fn(A(8, *ch(c)), A(8, *ch(c)), ACT.Exp).then_inc(s.kq_exp, 1)
                for c in range(NC):
                    act.wait_ge(s.ktokT, c + 1)
                    fn(A(1, *ch(c)), bank(4 + c), ACT.Copy).then_inc(s.ktok, 1)
                for c in range(NC):
                    act.wait_ge(s.rden_den, c + 1)
                    fn(heap[0:H, 8, c * CW:c * CW + CW], ps[0:H, c, :], ACT.Copy).then_inc(s.rden_ev, 1)
                normalise(ln0 + 2, psum_tile)
                ln_copy(tr0 + 2, A(1), w("g2"), w("bn2"))
                for c in range(NC):
                    for j in range(4):
                        act.wait_ge(s.fc1, 4 * c + j + 1)
                        if c >= 2:
                            act.wait_ge(s.fc2, c - 1)
                        fn(A(6 + c % 2, j * CW, j * CW + CW), bank(j), ACT.Gelu, bias=wc("fc1b", j, 1)).then_inc(s.hid, 1)

            def moe(n, ln0, tr0, tk0, y0):
                rowsn = tn[:, ln0 % 2].rearrange("p t c -> p (t c)")
                wait_ln(act, ln0)
                fn(halves(0)[0], rowsn, ACT.Copy).then_inc(s.hi2, 1)
                act.wait_ge(s.rs2, n + 1)
                fn(halves(0)[1], A(2), ACT.Copy).then_inc(s.mid2, 1)
                act.wait_ge(s.slotT, n + 1)
                fn(halves(8)[1].bitcast(F16)[0:NT, 0:P], ps[0:NT, 5, 256:384], ACT.Copy).then_inc(s.slotrow, 1)
                for half in range(2):
                    act.wait_ge(s.disp, NT * (n + 1))
                    fn(A(4, half * CW, half * CW + CW), bank(6 + half), ACT.Copy).then_inc(s.xg, 1)
                for e in range(E):
                    act.wait_ge(s.h_mm, E * n + e + 1)
                    if e >= 2:
                        act.wait_ge(s.y_mm, E * n + e - 1)
                    for j in range(4):
                        fn(hbuf(e)[:, j, :], bank(e % 2, j * P, j * P + P), ACT.Relu,
                           bias=wc("b1", 4 * e + j, 1)).then_inc(s.h_act, 1)

            def attention(a, kind, tr0, y0):
                for b in range(B):
                    for c in (2 * b, 2 * b + 1):
                        act.wait_ge(s.qkv_mm, NC * a + c + 1)
                        if kind == "fhn":
                            fn(A(0, *ch(c)), bank(c), ACT.Copy, scale=float(D) ** -0.5).then_inc(s.q_sb, 1)
                        else:
                            fn(A(0, *ch(c)), bank(c), bias=small[:, 2:3], scale=float(D) ** -0.5).then_inc(s.q_sb, 1)
                    act.wait_ge(s.q_sb, NC * a + 2 * b + 2)
                    fn(seq(QH, b), seq(A(0), b), ACT.Copy).then_inc(s.hi, 1)
                    act.wait_ge(s.k_sb, NC * a + 2 * b + 2)
                    fn(seq(KH, b), seq(A(1), b), ACT.Copy).then_inc(s.hi, 1)
                    act.wait_ge(s.rs, 2 * B * a + 2 * b + 1)
                    fn(seq(QMI, b), seq(rest_q, b), ACT.Copy).then_inc(s.mid, 1)
                    act.wait_ge(s.rs, 2 * B * a + 2 * b + 2)
                    fn(seq(KMI, b), seq(rest_k, b), ACT.Copy).then_inc(s.mid, 1)

                def out_copy(g, par, qh):
                    act.wait_ge(s.av_mm, UNITS * g + (4 if qh == 0 else 12))
                    fn(oraw(par)[:, qh * CW:qh * CW + CW], bank(4), ACT.Copy).then_inc(s.o_sb, 1)

                def group(it, par):
                    g = GROUPS * a + 2 * it + par
                    for k, (qh, kt, off) in enumerate(STEPS):
                        for j2 in range(2):
                            act.wait_ge(s.st_mm, 2 * UNITS * g + (2 * k + j2 + 1))
                            fn(pbuf(k)[:, 2 * j2:2 * j2 + 2, 0:CW - off], ps[:, 2 * j2:2 * j2 + 2, 0:CW - off],
                               ACT.Exp).then_inc(s.pexp, 1)
                        if k == 5:
                            act.wait_ge(o_st[par], 64 * (GROUPS // 2 * a + it) + 64)
                            out_copy(g, par, 0)
                    out_copy(g, par, 1)

                with act.Fori(0, GROUPS // 2) as it:
                    for par in range(2):
                        group(it, par)
                if kind == "fhn":
                    act.wait_ge(s.f_pre, 1)
                    fn(A(5, 512, 768), A(5, 512, 768), ACT.Sigmoid, scale=10.0).then_inc(s.f_sig, 1)
                    act.wait_ge(s.f_pre, 2)
                    fn(A(5, 512, 768), A(5, 512, 768), ACT.Sigmoid).then_inc(s.f_sig, 1)
                for c in range(NC):
                    act.wait_ge(s.ofin, NC * a + c + 1)
                    if kind == "fhn":
                        fn(A(6, *ch(c)), bank(c), ACT.Copy).then_inc(s.y, 1)
                    else:
                        fn(A(6, *ch(c)), bank(c), bias=w("cob")).then_inc(s.y, 1)

            def gated(n, ln0, tr0, tk0, y0):
                for c in range(NC):
                    act.wait_ge(s.e_mm, NC * n + c + 1)
                    if c >= 2:
                        act.wait_ge(s.s_mm, NC * n + c - 1)
                    for hf in range(2):
                        a = (2 * (c % 2) + hf) * CW
                        fn(A(0, a, a + CW), bank(2 * (c % 2) + hf), ACT.Sigmoid, bias=wc("encb", hf, 1)).then_inc(s.e_sp, 1)
                for c in range(NC):
                    act.wait_ge(s.r_mm, NC * n + c + 1)
                    fn(heap[0:M, 2, c * CW:c * CW + CW], ps[0:M, 4 + c, :], ACT.Tanh, bias=w("rb1", M)).then_inc(s.th, 1)

                def hidden(q):
                    g = NC * E * n + q
                    act.wait_ge(s.x_mm, g + 1)
                    if q >= 4:
                        act.wait_ge(s.x_h, g - 3)
                    fn(A(5, (q % 4) * CW, (q % 4) * CW + CW), bank(q % 2), ACT.Relu,
                       bias=wc("be1", q % E, 1)).then_inc(s.x_rl, 1)

                for q in range(4):
                    hidden(q)
                act.wait_ge(s.d12, n + 1)
                fn(sm[:, 4, :], sm[:, 3, :], ACT.Sigmoid).then_inc(s.sg, 1)
                fn(sm[:, 5, :], sm[:, 3, :], ACT.Sigmoid, scale=-1.0).then_inc(s.sg, 1)
                act.wait_ge(s.g_zero, n + 1)
                act.wait_ge(s.gT, 2 * n + 1)
                gview = ps[:, 2:4, :].rearrange("p a b -> p (a b)").bitcast(BF16)
                fn(halves(3)[0][0:24, :], gview[0:24, :], ACT.Copy).then_inc(s.gTs, 1)
                act.wait_ge(s.gT, 2 * n + 2)
                fn(heap[0:E, 4, :], ps[0:E, 4:8, :].rearrange("p a b -> p (a b)"), ACT.Copy).then_inc(s.gTs, 1)
                for q in range(4, NC * E):
                    hidden(q)

                def decoded(c):
                    act.wait_ge(s.dd_mm, NC * n + c + 1)
                    fn(A(9, *ch(c)), bank(4 + c), ACT.Sigmoid, bias=w("decb")).then_inc(s.dd_sb, 1)

                for c in range(NC):
                    act.wait_ge(s.c_mm, NC * n + c + 1)
                    if c >= 2:
                        act.wait_ge(s.dd_mm, NC * n + c - 1)
                    for hf in range(2):
                        a = (2 * (c % 2) + hf) * CW
                        fn(A(8, a, a + CW), bank(2 * (c % 2) + hf), ACT.Sigmoid, bias=wc("c2sb", hf, 1)).then_inc(s.c_sb, 1)
                    if c:
                        decoded(c - 1)
                decoded(NC - 1)

            def fastw(n, ln0, tr0, tk0, y0):
                fn(small[:, 8:9], w("lr"), ACT.Exp).then_inc(s.llr, 1)
                normalise(ln0 + 1, tiles_of(tn[:, ln0 % 2]))
                ln_copy(tr0 + 1, A(0), w("lng"), w("lnb"))
                for c in range(NC):
                    act.wait_ge(s.lwk, c + 1)
                    fn(A(1, *ch(c)), bank(c), ACT.Copy).then_inc(s.lks, 1)
                for c in range(NC):
                    act.wait_ge(s.lv, c + 1)
                    fn(A(2, *ch(c)), bank(4 + c), ACT.Copy).then_inc(s.ly0, 1)
                for c in range(NC):
                    act.wait_ge(s.lgm, c + 1)
                    fn(A(7, *ch(c)), bank(c), ACT.Sigmoid).then_inc(s.lgs, 1)

            act.sem_inc(s.o_sb, 1)
            act.sem_inc(s.o_st0, 64)
            act.sem_inc(s.o_st1, 64)
            for kind, n, ln0, tr0, tk0, y0 in plan:
                normalise(ln0, tiles_of(x))
                ln_copy(tr0, u)
                act.wait_ge(w_in[PART.get(kind, 2)], 16)
                if kind in attn_of:
                    attention(attn_of[kind], kind, tr0, y0)
                else:
                    {"mlla": mlla, "moe": moe, "gated": gated, "fastw": fastw}[kind](n, ln0, tr0, tk0, y0)

        @block.vector
        def _(dve):
            link = chain(dve, s.dve_chain)
            TT, TS, STT = dve.tensor_tensor, dve.tensor_scalar, dve.scalar_tensor_tensor

            def row_stats(tile, c):
                for t in range(TC * c, TC * c + TC):
                    m = dve.bn_stats(st6[:, t, :], tile(t))
                return m

            def scales(mean_first):
                v, y, t0, mean = sm[:, 0, :], sm[:, 1, :], sm[:, 2, :], sm[:, 6, :]
                TT(t0, st6[:, :, 1], st6[:, :, 4], ALU.subtract)
                TT(mean, st6[:, :, 1], st6[:, :, 4], ALU.add)
                link(TT(v, st6[:, :, 2], st6[:, :, 5], ALU.add))
                link(TT(t0, t0, t0, ALU.mult))
                link(STT(v, t0, C / 4.0, v, ALU.mult, ALU.add))
                link(TS(v, v, 1.0 / C, 1e-5, ALU.mult, ALU.add))
                link(TS(y.bitcast(I32), v.bitcast(I32), -0.5, RSQRT_SEED, ALU.mult, ALU.add))
                for _ in range(3):
                    link(STT(t0, y, -0.5, y, ALU.mult, ALU.mult))
                    link(TT(t0, t0, v, ALU.mult))
                    link(STT(y, t0, 1.5, y, ALU.add, ALU.mult))
                if mean_first:
                    return TS(mean, mean, -0.5, None, ALU.mult)
                return STT(mean, mean, -0.5, y, ALU.mult, ALU.mult)

            def ln(n, tile, ready=None, stats=True):
                if stats:
                    for c in range(NC):
                        if ready is not None:
                            dve.wait_ge(s.tokT, NC * ready + c + 1)
                        m = row_stats(tile, c)
                    link(m)
                scales(False).then_inc(s.ln_st, 1)
                dve.wait_ge(s.ln_st, n + 1)
                for c in LN_DVE:
                    for t in range(TC * c, TC * c + TC):
                        m = TS(tn[:, n % 2, t, :], tile(t), sm[:, 1, t:t + 1], sm[:, 6, t:t + 1], ALU.mult, ALU.add)
                    m.then_inc(s.ln_tn, 1)
                wait_ln(dve, n)

            def next_stats(bi, c):
                if bi + 1 < len(plan):
                    dve.wait_ge(s.res, NC * bi + c + 1)
                    m = row_stats(tiles_of(x), c)
                    if c == NC - 1:
                        link(m)

            def residual(k, bi):
                for c in range(NC):
                    dve.wait_ge(s.resT, NC * k + c + 1)
                    xs = x[:, TC * c:TC * c + TC, :]
                    TT(xs, xs, bank(4 + c).rearrange("p (t c) -> p t c", c=C), ALU.add).then_inc(s.res, 1)
                    next_stats(bi, c)

            def conv(dst, src, b, name, centre, sem):
                a, e = b * N, b * N + N
                wv = wc
                link(TS(dst[:, a:e], src[:, a:e], centre, wv(name, 3, 1), ALU.mult, ALU.add))
                link(STT(dst[:, a + 1:e], src[:, a:e - 1], wv(name, 0, 1), dst[:, a + 1:e], ALU.mult, ALU.add))
                m = STT(dst[:, a:e - 1], src[:, a + 1:e], wv(name, 2, 1), dst[:, a:e - 1], ALU.mult, ALU.add)
                if sem is None:
                    link(m)
                else:
                    m.then_inc(sem, 1)

            def mlla(n, ln0, tr0, tk0, y0):
                for b in range(B):
                    dve.wait_ge(s.u, NC * tr0 + 2 * b + 2)
                    conv(A(0), u, b, "cpe1", small[:, 0:1], s.c1)
                ln(ln0 + 1, psum_tile, ready=tk0)
                for c in range(NC):
                    dve.wait_ge(s.lin, c + 1)
                    m = TS(A(3, *ch(c)), bank(4 + c), w("inb"), None, ALU.add)
                link(m)
                for b in range(B):
                    conv(A(4), A(3), b, "dwc", wc("dwc", 1, 1), s.xc)
                for c in range(NC):
                    dve.wait_ge(s.qk_mm, c + 1)
                    TS(A(9, *ch(c)), bank(c), w("qb"), 0.0, ALU.add, ALU.min).then_inc(s.kq_min, 1)
                    TS(A(8, *ch(c)), bank(4 + c), w("kb"), 0.0, ALU.add, ALU.min).then_inc(s.kq_min, 1)
                lepe = tn[:, 1].rearrange("p t c -> p (t c)")
                for b in range(B):
                    conv(lepe, A(5), b, "lepe", wc("lepe", 1, 1), None)
                for b in range(B):
                    dve.wait_ge(s.qk, 4 * b + 4)
                    link(dve.tensor_reduce(small[:, 10 + b:11 + b], A(4, b * N, b * N + N), AX, ALU.add))
                    TS(small[:, 16 + H * b:16 + H * b + H], w("headm"), small[:, 10 + b:11 + b], 1.0 / N,
                       ALU.mult, ALU.mult).then_inc(s.kmean, 1)
                for c in range(NC):
                    dve.wait_ge(s.vtokT, c + 1)
                    dve.tensor_copy(A(9, *ch(c)), bank(c)).then_inc(s.vtok, 1)
                for b in range(B):
                    dve.wait_ge(s.gacc, b + 1)
                    dve.tensor_copy(mats[:, b, :], bank(4 + b, 0, P)).then_inc(s.gev, 1)
                for b in range(B):
                    dve.wait_ge(s.gacc, B + b + 1)
                    TT(mats[:, 2 + b, :], bank(4 + b, P, 2 * P), w("blockm"), ALU.mult).then_inc(s.gev, 1)
                for b in range(B):
                    dve.wait_ge(s.gacc, 2 * B + b + 1)
                    dve.tensor_copy(mats[:, 4 + b, :], bank(4 + b, 2 * P, 3 * P)).then_inc(s.gev, 1)
                dve.wait_ge(s.z_ld, 16)
                link(TS(A(7, 0, 256), A(7, 0, 256), 1e-6, None, ALU.add))
                dve.reciprocal(A(7, 256, 512), A(7, 0, 256)).then_inc(s.z_rc, 1)
                dve.wait_ge(s.z_fl, 32)
                for c in range(NC):
                    dve.wait_ge(s.mnum, c + 1)
                    link(TT(A(4, *ch(c)), bank(c), A(6, *ch(c)), ALU.mult))
                    link(TT(A(4, *ch(c)), A(4, *ch(c)), lepe[:, c * CW:c * CW + CW], ALU.add))
                    TT(A(4, *ch(c)), A(4, *ch(c)), A(2, *ch(c)), ALU.mult).then_inc(s.att, 1)
                for c in range(NC):
                    dve.wait_ge(s.olin, c + 1)
                    m = STT(A(3, *ch(c)), bank(4 + c), w("outb"), A(0, *ch(c)), ALU.add, ALU.add)
                link(m)
                for b in range(B):
                    conv(A(5), A(3), b, "cpe2", small[:, 1:2], s.x3)
                ln(ln0 + 2, psum_tile, ready=tk0 + 1)
                for c in range(NC):
                    dve.wait_ge(s.fc2, c + 1)
                    STT(A(8, *ch(c)), bank(4 + c), w("fc2b"), A(5, *ch(c)), ALU.add, ALU.add).then_inc(s.y, 1)

            def first_max(lg, m, oh, cand, mc, out):
                v = lg.rearrange("p (t e) -> p t e", e=E)
                link(dve.tensor_reduce(m, v, AX, ALU.max))
                link(TT(oh.rearrange("p (t e) -> p t e", e=E), v, bc(m.unsqueeze(2), (P, NT, E)), ALU.is_equal))
                link(TT(cand.rearrange("p (t e) -> p t e", e=E), oh.rearrange("p (t e) -> p t e", e=E),
                        bc(row("rev").unsqueeze(1), (P, NT, E)), ALU.mult))
                link(dve.tensor_reduce(mc, cand.rearrange("p (t e) -> p t e", e=E), AX, ALU.max))
                return TT(out.rearrange("p (t e) -> p t e", e=E), cand.rearrange("p (t e) -> p t e", e=E),
                          bc(mc.unsqueeze(2), (P, NT, E)), ALU.is_equal)

            def moe(n, ln0, tr0, tk0, y0):
                v3 = lambda ap: ap.rearrange("p (t e) -> p t e", e=E)
                rowsn = tn[:, ln0 % 2].rearrange("p t c -> p (t c)")
                dve.wait_ge(s.hi2, n + 1)
                TT(A(2), rowsn, halves(0)[0], ALU.subtract).then_inc(s.rs2, 1)
                dve.wait_ge(s.lg, n + 1)
                link(TT(v3(gate[:, 0, :]), v3(bank(4, 0, NT * E)), bc(row("bsw").unsqueeze(1), (P, NT, E)), ALU.add))
                first_max(gate[:, 0, :], sm[:, 0, :], gate[:, 1, :], gate[:, 2, :], sm[:, 1, :], ohb[:, :]
                          ).then_inc(s.oh, 1)
                dve.wait_ge(s.oh, n + 1)
                link(TT(v3(gate[:, 1, :]), v3(ohb[:, :]), bc(row("base").unsqueeze(1), (P, NT, E)), ALU.mult))
                link(dve.tensor_reduce(sm[:, 2, :], v3(gate[:, 1, :]), AX, ALU.add))
                dve.wait_ge(s.cum, n + 1)
                link(TT(gate[:, 2, :], bank(5, 0, NT * E), ohb[:, :], ALU.mult))
                link(dve.tensor_reduce(sm[:, 3, :], v3(gate[:, 2, :]), AX, ALU.add))
                link(TS(sm[:, 4, :], sm[:, 3, :], float(CAP), 2048.0, ALU.is_gt, ALU.mult))
                link(STT(sm[:, 5, :], sm[:, 3, :], -1.0, sm[:, 2, :], ALU.add, ALU.add))
                TT(sm[:, 7, :], sm[:, 5, :], sm[:, 4, :], ALU.add).then_inc(s.slot, 1)
                dve.wait_ge(s.mid2, n + 1)
                TT(halves(1)[0], A(2), halves(0)[1], ALU.subtract).then_inc(s.parts, 1)
                dve.wait_ge(s.slot, n + 1)
                for t in range(NT):
                    if t >= 4:
                        dve.wait_ge(s.disp, NT * n + t - 3)
                    TS(onehot(t), iota16[:, :], sm[:, 7, t:t + 1], None, ALU.is_equal).then_inc(s.onehot, 1)
                dve.wait_ge(s.parts, n + 1)
                dve.wait_ge(s.slot_ld, 16 * (n + 1))
                slotb = halves(8)[0].bitcast(F16)
                link(STT(A(2), slotb, float(SLOTS), u[:, :], ALU.is_ge, ALU.mult))
                for e in range(4):
                    TS(back(e), slotb, wc("pcol", e, 1), None, ALU.is_equal).then_inc(s.st_oh, 1)
                ysb, ry = A(4, 1024, 2048), A(6, 0, 1024)
                yp = heap[:, 5, :].bitcast(BF16)
                for hf in range(2):
                    a, e = hf * CW, hf * CW + CW
                    dve.wait_ge(s.y_mm, E * n + 4 * hf + 4)
                    link(TT(ysb[:, a:e], bank(2 + hf), row("b2")[:, a:e], ALU.add))
                    link(dve.tensor_copy(yp[:, a:e], ysb[:, a:e]))
                    link(TT(ry[:, a:e], ysb[:, a:e], yp[:, a:e], ALU.subtract))
                    link(dve.tensor_copy(yp[:, SLOTS + a:SLOTS + e], ry[:, a:e]))
                    TT(yp[:, 2 * SLOTS + a:2 * SLOTS + e], ry[:, a:e], yp[:, SLOTS + a:SLOTS + e],
                       ALU.subtract).then_inc(s.yparts, 1)
                for e in range(4, E):
                    dve.wait_ge(s.comb, E * n + e - 3)
                    TS(back(e), slotb, wc("pcol", e, 1), None, ALU.is_equal).then_inc(s.st_oh, 1)
                dve.wait_ge(s.comb, E * (n + 1))
                for c in range(NC):
                    TT(A(0, *ch(c)), A(2, *ch(c)), bank(c), ALU.add).then_inc(s.y, 1)

            def attention(a, kind, ln0, tr0, y0):
                if kind == "causal":
                    link(TS(small[:, 2:3], w("pqb"), float(D) ** -0.5, None, ALU.mult))
                    tmp = tn[:, (ln0 + 1) % 2].rearrange("p (k t) c -> p k (t c)", k=4)
                    dve.wait_ge(s.tab_in, 16)
                    for k in range(3):
                        for c in range(NC):
                            p = NC * k + c
                            dve.wait_ge(s.rope_mm, p + 1)
                            if p >= 2:
                                dve.wait_ge(s.rope, p - 1)
                            h0 = (c % 2) * CW
                            TT(tmp[:, 2 * (p % 2), :], bank(2 * p % 8), A(2, h0, h0 + CW), ALU.mult)
                            TT(tmp[:, 2 * (p % 2) + 1, :], bank(2 * p % 8 + 1), A(2, N + h0, N + h0 + CW),
                               ALU.mult).then_inc(s.rope_t, 1)
                if kind == "causal":
                    dve.wait_ge(s.rope, 3 * NC)

                def values_out(c):
                    dve.wait_ge(s.vt_mm, NC * a + c + 1)
                    if c >= 2:
                        dve.wait_ge(v_st[c % 2], 16 * TC * (2 * a + 1))
                    for t in range(TC):
                        src = bank(c, t * P, t * P + P).rearrange("p (h d) -> p h d", d=D)
                        if kind == "fhn":
                            m = dve.tensor_copy(vp(c % 2)[:, t, :, 0:D], src)
                        else:
                            m = TT(vp(c % 2)[:, t, :, 0:D], src, row("vb").rearrange("p (h d) -> p h d", d=D), ALU.add)
                    m.then_inc(s.v_sb, 1)

                for b in range(B):
                    for c in (2 * b, 2 * b + 1):
                        dve.wait_ge(s.qkv_mm, NC * a + c + 1)
                        if kind == "fhn":
                            dve.tensor_copy(A(1, *ch(c)), bank(4 + c)).then_inc(s.k_sb, 1)
                        else:
                            TS(A(1, *ch(c)), bank(4 + c), w("pkb"), None, ALU.add).then_inc(s.k_sb, 1)
                    dve.wait_ge(s.hi, 2 * B * a + 2 * b + 1)
                    TT(seq(rest_q, b), seq(A(0), b), seq(QH, b), ALU.subtract).then_inc(s.rs, 1)
                    dve.wait_ge(s.hi, 2 * B * a + 2 * b + 2)
                    TT(seq(rest_k, b), seq(A(1), b), seq(KH, b), ALU.subtract).then_inc(s.rs, 1)
                    dve.wait_ge(s.mid, 2 * B * a + 2 * b + 1)
                    dve.wait_ge(s.rs, 2 * B * a + 2 * b + 2)
                    TT(seq(QL, b), seq(rest_q, b), seq(QMI, b), ALU.subtract).then_inc(s.lo, 1)
                    dve.wait_ge(s.mid, 2 * B * a + 2 * b + 2)
                    TT(seq(KL, b), seq(rest_k, b), seq(KMI, b), ALU.subtract).then_inc(s.lo, 1)
                    if b == 0:
                        dve.wait_ge(s.v_one, a + 1)
                    for c in (2 * b, 2 * b + 1):
                        values_out(c)

                def strip_maxima(g, first, last):
                    for k, jp, j2, qt, kc, width in STRIPS[first:last]:
                        dve.wait_ge(s.mx_mm, MAXU * g + (k + 1))
                        dve.tensor_reduce(mx[:, kc, jp, j2, qt:qt + 1], bank(5 + k % 3, 0, width), AX,
                                          ALU.max).then_inc(s.mx_red, 1)

                def combine(g):
                    dve.wait_ge(s.mx_red, MAXU * g + MAXU)
                    far, near = mx[:, 0, :, :, 4:KT], mx[:, 1, :, :, 4:KT]
                    TT(far, far, near, ALU.max).then_inc(s.mx_cmb, 1)
                    dve.wait_ge(s.mx_cmb, 2 * g + 1)
                    dve.wait_ge(s.mT, g)
                    TS(mneg[:, :], mx[:, 0].rearrange("p a b q -> p (a b q)"), -1.0, None,
                       ALU.mult).then_inc(s.mx_cmb, 1)
                    dve.wait_ge(s.mx_cmb, 2 * g + 2)

                    neg = mneg[:, :].rearrange("p (a b) -> p a b", a=2)
                    rest = mrs[:, :].rearrange("p (a b) -> p a b", a=2)
                    dve.tensor_copy(msq[:, :, 0, :], neg).then_inc(s.m_pt, 1)
                    dve.wait_ge(s.m_pt, 4 * g + 1)
                    TT(rest, neg, msq[:, :, 0, :], ALU.subtract).then_inc(s.m_pt, 1)
                    dve.wait_ge(s.m_pt, 4 * g + 2)
                    dve.tensor_copy(msq[:, :, 1, :], rest).then_inc(s.m_pt, 1)
                    dve.wait_ge(s.m_pt, 4 * g + 3)
                    TT(msq[:, :, 2, :], rest, msq[:, :, 1, :], ALU.subtract).then_inc(s.m_pt, 1)

                def keep_turned(g, par, turn):
                    dve.wait_ge(s.mT, g + 1)
                    dve.wait_ge(rows_ld[par], 32 * turn)
                    dve.tensor_copy(msp[:, par, :], ps[0:96, 7, 0:64].bitcast(BF16)).then_inc(s.m_sp, 1)

                g0 = GROUPS * a
                strip_maxima(g0, 0, MAXU)
                combine(g0)
                strip_maxima(g0 + 1, 0, 2)
                keep_turned(g0, 0, GROUPS // 2 * a)
                strip_maxima(g0 + 1, 2, HEAD)

                def maxima_beside(it, par, ahead):
                    g = g0 + 2 * it + par
                    strip_maxima(g + 1, HEAD, MAXU)
                    combine(g + 1)
                    if ahead:
                        strip_maxima(g + 2, 0, 2)
                    keep_turned(g + 1, 1 - par, GROUPS // 2 * a + it + par)
                    if ahead:
                        strip_maxima(g + 2, 2, HEAD)

                with dve.Fori(0, GROUPS // 2 - 1) as it:
                    for par in range(2):
                        maxima_beside(it, par, True)
                maxima_beside(GROUPS // 2 - 1, 0, False)
                if kind == "fhn":
                    pa, pb, pd = (wc("fabd", k, 1) for k in range(3))
                    al, da, rd = small[:, 3:4], small[:, 4:5], small[:, 5:6]
                    link(TS(al, pd, 1.0 / 12.5, None, ALU.mult))
                    link(STT(da, al, pb, al, ALU.mult, ALU.bypass))
                    link(TS(da, da, 1.0, None, ALU.add))
                    link(dve.reciprocal(rd, da))
                dve.wait_ge(s.sum_io, 32 * a + 16)
                f = lambda k: A(5, 256 * k, 256 * k + 256)
                den, fac, t2, inp, scl, rec, e_, t7 = (f(k) for k in range(8))
                if kind == "causal":
                    dve.reciprocal(fac, den).then_inc(s.f_out, 1)
                else:
                    link(dve.reciprocal(rec, den))
                    link(TT(e_, den, rec, ALU.mult))
                    link(STT(t7, e_, -1.0, e_, ALU.mult, ALU.max))
                    link(TS(scl, t7, 1e-6, None, ALU.max))
                    TS(t2, t7, -0.5, None, ALU.add).then_inc(s.f_pre, 1)
                    link(dve.reciprocal(fac, scl))
                    link(TT(inp, e_, fac, ALU.mult))
                    dve.wait_ge(s.f_sig, 1)
                    link(TS(t2, t2, 0.9, 0.1, ALU.mult, ALU.add))
                    link(TT(inp, inp, t2, ALU.mult))
                    link(TS(t2, inp, pd, None, ALU.mult))
                    link(TS(t7, t2, pa, al, ALU.add, ALU.mult))
                    link(TS(t7, t7, rd, 3.0, ALU.mult, ALU.min))
                    link(TS(t7, t7, -3.0, None, ALU.max))
                    link(TS(t2, t2, 3.0, -3.0, ALU.min, ALU.max))
                    link(TT(fac, t2, t2, ALU.mult))
                    link(TT(fac, fac, t2, ALU.mult))
                    link(STT(fac, fac, -1.0 / 3.0, t2, ALU.mult, ALU.add))
                    link(TT(fac, fac, t7, ALU.subtract))
                    link(TT(fac, fac, inp, ALU.add))
                    link(STT(fac, fac, pd, t2, ALU.mult, ALU.add))
                    link(TS(fac, fac, 3.0, -3.0, ALU.min, ALU.max))
                    TT(t2, fac, scl, ALU.mult).then_inc(s.f_pre, 1)
                    dve.wait_ge(s.f_sig, 2)
                    link(TS(t2, t2, 0.5, 0.5, ALU.mult, ALU.add))
                    link(TT(t7, e_, t2, ALU.mult))
                    link(TS(t7, t7, 1e-8, None, ALU.add))
                    link(dve.reciprocal(inp, t7))
                    link(TT(inp, inp, t2, ALU.mult))
                    TT(fac, inp, rec, ALU.mult).then_inc(s.f_out, 1)
                dve.wait_ge(s.fd_ld, 32 * (a + 1))
                dve.wait_ge(s.fb_ld, 32 * (a + 1))
                for c in range(NC):
                    TT(A(4, *ch(c)), A(2, *ch(c)), A(3, *ch(c)), ALU.mult).then_inc(s.oT, 1)

            def gated(n, ln0, tr0, tk0, y0, bi):
                v3 = lambda ap: ap.rearrange("p (t e) -> p t e", e=E)
                for c in range(NC):
                    dve.wait_ge(s.s_mm, NC * n + c + 1)
                    TS(A(1, *ch(c)), bank(4 + c), w("s2cb"), None, ALU.add).then_inc(s.cont, 1)
                dve.wait_ge(s.l_mm, n + 1)
                link(TT(v3(gate[:, 0, :]), v3(bank(2, 0, NT * E)), bc(row("rb2").unsqueeze(1), (P, NT, E)), ALU.add))
                link(first_max(gate[:, 0, :], sm[:, 0, :], gate[:, 1, :], gate[:, 2, :], sm[:, 1, :], gate[:, 4, :]))
                link(STT(gate[:, 0, :], gate[:, 4, :], NEG, gate[:, 0, :], ALU.mult, ALU.add))
                link(first_max(gate[:, 0, :], sm[:, 2, :], gate[:, 1, :], gate[:, 2, :], sm[:, 1, :], gate[:, 5, :]))
                TT(sm[:, 3, :], sm[:, 0, :], sm[:, 2, :], ALU.subtract).then_inc(s.d12, 1)
                dve.wait_ge(s.sg, 2 * (n + 1))
                link(TT(v3(gate[:, 1, :]), v3(gate[:, 4, :]), bc(sm[:, 4, :].unsqueeze(2), (P, NT, E)), ALU.mult))
                link(TT(v3(gate[:, 2, :]), v3(gate[:, 5, :]), bc(sm[:, 5, :].unsqueeze(2), (P, NT, E)), ALU.mult))
                link(TT(gate[:, 3, :], gate[:, 1, :], gate[:, 2, :], ALU.add))
                gp = g24[:, :].rearrange("p (t k e) -> p t k e", k=3, e=E)
                link(dve.tensor_copy(gp[:, :, 0, :], v3(gate[:, 3, :])))
                link(TT(v3(gate[:, 1, :]), v3(gate[:, 3, :]), gp[:, :, 0, :], ALU.subtract))
                link(dve.tensor_copy(gp[:, :, 1, :], v3(gate[:, 1, :])))
                TT(gp[:, :, 2, :], v3(gate[:, 1, :]), gp[:, :, 1, :], ALU.subtract).then_inc(s.gates, 1)
                for q in range(NC * E):
                    g = NC * E * n + q
                    dve.wait_ge(s.x_rl, g + 1)
                    dve.wait_ge(s.g_mm, g + 1)
                    if q >= 4:
                        dve.wait_ge(s.x_dn, g - 3)
                    a = (q % 4) * CW
                    TT(A(6, a, a + CW), A(5, a, a + CW), bank(2 + q % 2), ALU.mult).then_inc(s.x_h, 1)
                    if q % E == 1 and q > E:
                        copy_cont(n, q // E - 1)
                copy_cont(n, NC - 1)
                for c in range(NC):
                    dve.wait_ge(s.tokT, NC * tk0 + c + 1)
                    m = row_stats(psum_tile, c)
                link(m)
                link(scales(True))
                dve.wait_ge(s.x_fb, n + 1)
                for c in range(NC):
                    for t in range(TC * c, TC * c + TC):
                        m = STT(tn[:, (ln0 + 1) % 2, t, :], psum_tile(t), sm[:, 6, t:t + 1], row("fing"), ALU.add, ALU.mult)
                    link(m)
                    for t in range(TC * c, TC * c + TC):
                        m = STT(x[:, t, :], tn[:, (ln0 + 1) % 2, t, :], sm[:, 1, t:t + 1], x[:, t, :], ALU.mult, ALU.add)
                    m.then_inc(s.res, 1)
                    next_stats(bi, c)

            def copy_cont(n, c):
                dve.wait_ge(s.a_mm, NC * n + c + 1)
                dve.tensor_copy(A(7, *ch(c)), bank(4 + c)).then_inc(s.a_sb, 1)

            def fastw(n, ln0, tr0, tk0, y0):
                ln(ln0 + 1, tiles_of(tn[:, ln0 % 2]))
                dve.wait_ge(s.w0x, 1)
                TT(mats[:, 0, :], bank(4, 0, P), w("W0"), ALU.add).then_inc(s.w0, 1)
                TS(mats[:, 1, :], w("Wv"), -1.0, None, ALU.mult).then_inc(s.w0, 1)
                dve.wait_ge(s.llr, 1)
                link(TS(small[:, 9:10], small[:, 8:9], 1.0, None, ALU.min))
                for c in range(NC):
                    dve.wait_ge(s.lerr, c + 1)
                    TT(A(3, *ch(c)), A(1, *ch(c)), bank(c), ALU.mult).then_inc(s.lgrad, 1)
                dve.wait_ge(s.lgrad, NC)
                for b in range(B):
                    m = dve.tensor_tensor_scan(A(4, b * N, b * N + N), bc(row("one"), (P, N)), A(3, b * N, b * N + N), 0.0,
                                               ALU.mult, ALU.add)
                link(m)
                for c in range(NC):
                    dve.wait_ge(s.lq, c + 1)
                    a = c * CW
                    f = 1 if c % 2 == 0 else 0
                    link(STT(A(5, *ch(c)), bank(4 + c), small[:, 9:10], row("pos")[:, (c % 2) * CW:(c % 2) * CW + CW],
                             ALU.mult, ALU.mult))
                    link(TT(A(5, a + f, a + CW), A(5, a + f, a + CW), A(4, a + f - 1, a + CW - 1), ALU.mult))
                    if f:
                        dve.tensor_copy(A(6, a, a + 1), A(2, a, a + 1))
                    link(TT(A(6, a + f, a + CW), A(2, a + f, a + CW), A(5, a + f, a + CW), ALU.subtract))
                    dve.wait_ge(s.lgs, c + 1)
                    TT(A(6, *ch(c)), A(6, *ch(c)), A(7, *ch(c)), ALU.mult).then_inc(s.lo1, 1)
                for c in range(NC):
                    dve.wait_ge(s.lwo, c + 1)
                    STT(A(8, *ch(c)), bank(4 + c), w("lsg"), u[:, c * CW:c * CW + CW], ALU.mult, ALU.add).then_inc(s.y, 1)

            dve.wait_ge(s.x_in, 16)
            for bi, (kind, n, ln0, tr0, tk0, y0) in enumerate(plan):
                ln(ln0, tiles_of(x), stats=bi == 0)
                dve.wait_ge(w_in[PART.get(kind, 2)], 16)
                if kind == "mlla":
                    TS(small[:, 0:1], wc("cpe1", 1, 1), 1.0, None, ALU.add)
                    link(TS(small[:, 1:2], wc("cpe2", 1, 1), 1.0, None, ALU.add))
                else:
                    dve.wait_ge(s.row_in, 16)
                    dve.wait_ge(s.prep, 1)
                if kind in attn_of:
                    attention(attn_of[kind], kind, ln0, tr0, y0)
                elif kind == "gated":
                    gated(n, ln0, tr0, tk0, y0, bi)
                else:
                    {"mlla": mlla, "moe": moe, "fastw": fastw}[kind](n, ln0, tr0, tk0, y0)
                if kind != "gated":
                    residual(y0, bi)

        @block.gpsimd
        def _(pool):
            pool.memset(orow[:, :], 1.0)
            pool.wait_ge(s.w_in0, 16)
            pool.tensor_copy(identb[:, :], ident)
            pool.wait_ge(s.k_in, 16)
            pool.tensor_copy(maskb[:, 0, :], kw("cmask"))
            pool.tensor_copy(maskb[:, 1, :], kw("fmask"))
            pool.tensor_copy(trib[:, :], kw("tri"))
            pool.tensor_copy(onesb[:, :], kw("ones"))
            pool.tensor_copy(iota16[:, :], kw("iota"))
            pool.tensor_copy(eselb[:, :], kw("esel")).then_inc(s.prep, 1)
            pool.wait_ge(s.prep, 1)

            def mlla():
                for c in range(NC):
                    for k, (dst, src) in enumerate(((3, 9), (4, 8))):
                        pool.wait_ge(s.kq_exp, 2 * c + k + 1)
                        pool.tensor_tensor(A(dst, *ch(c)), A(dst, *ch(c)), A(src, *ch(c)), ALU.add).then_inc(s.qk, 1)

            def stage_max(i, par):
                for jp in range(2):
                    for dst, src in loads(2 + par, i, jp):
                        pool.dma_start(dst, src).then_inc(pm_ld[par], 16)

            def attention(a, kind, ln0, tr0, bi):
                wait_ln(pool, ln0)
                pool.memset(heap[:, 7:9, :], 1.0).then_inc(s.v_one, 1)
                if kind == "causal":
                    tmp = tn[:, (ln0 + 1) % 2].rearrange("p (k t) c -> p k (t c)", k=4)
                    for k, slot in enumerate((5, 6, 9)):
                        for c in range(NC):
                            p = NC * k + c
                            pool.wait_ge(s.rope_t, p + 1)
                            pool.tensor_tensor(A(slot, *ch(c)), tmp[:, 2 * (p % 2), :], tmp[:, 2 * (p % 2) + 1, :],
                                               ALU.add).then_inc(s.rope, 1)
                pool.wait_ge(s.qkv_mm, NC * (a + 1))
                pool.memset(zeroed(2), 0.0).then_inc(s.m_zero, 1)
                pool.wait_ge(s.m_zero, 2 * a + 1)
                pool.wait_ge(s.qs_st0, 16 * 12 * (a + 1))
                stage_max(0, 0)
                pool.wait_ge(s.v_st0, 16 * TC * 2 * (a + 1))
                pool.memset(zeroed(3), 0.0).then_inc(s.m_zero, 1)
                pool.wait_ge(s.m_zero, 2 * a + 2)
                stage_max(1, 1)
                pool.wait_ge(s.qs_st1, 16 * 12 * (a + 1))
                for k in range(2):
                    pool.memset(zeroed(k), 0.0).then_inc(s.e_zero, 1)

                def group(i, par, ahead):
                    g = GROUPS * a + i
                    if ahead:
                        pool.wait_ge(s.mx_mm, MAXU * g + MAXU)
                        stage_max(i + 2, par)
                    d = 0
                    for k, (qh, kt, off) in enumerate(STEPS):
                        if kt < 4 * qh:
                            continue
                        pool.wait_ge(s.pexp, 2 * UNITS * g + (2 * k + 2))
                        pool.nop(nofuse=True)
                        if kind == "fhn":
                            m = pool.memset(pbuf(k)[64:P, :, 0:64], 0.0)
                        else:
                            m = pool.affine_select(out=pbuf(k)[:, :, 0:P], in_=pbuf(k)[:, :, 0:P],
                                                   compare_op=ALU.is_ge, fill=0.0, base=0,
                                                   pattern=[[0, 4], [1, P]], channel_multiplier=-1)
                        m.then_inc(s.pmask, 1)

                with pool.Fori(0, GROUPS // 2 - 1) as it:
                    for par in range(2):
                        group(2 * it + par, par, True)
                group(GROUPS - 2, 0, False)
                group(GROUPS - 1, 1, False)

            def gated(n, ln0, bi):
                if bi:
                    pool.wait_ge(s.res, NC * bi)
                pool.memset(heap[:, 3:5, :], 0.0).then_inc(s.g_zero, 1)
                wait_ln(pool, ln0)
                pool.wait_ge(s.row_in, 16)
                pool.tensor_tensor(x[:, :, :], x[:, :, :], bc(row("finb").unsqueeze(1), (P, NT, C)),
                                   ALU.add).then_inc(s.x_fb, 1)

            for bi, (kind, n, ln0, tr0, tk0, y0) in enumerate(plan):
                if kind == "mlla":
                    mlla()
                elif kind == "gated":
                    gated(n, ln0, bi)
                elif kind in attn_of:
                    attention(attn_of[kind], kind, ln0, tr0, bi)


def kernel(**inputs):
    import numpy as np
    import concourse.bacc as bacc
    from concourse.bass_utils import run_bass_kernel_spmd

    i = {k: np.asarray(v) for k, v in inputs.items()}
    m, h, f, q = "L0_attn_a_", "L0_attn_b_", "L0_ffn_", "L1_attn_a_"
    b, g = "L1_attn_b_", "L1_ffn_"
    f4 = np.float32
    p = np.arange(P)
    half = C // 2
    th = (1.0 / (10000.0 ** (np.arange(half, dtype=f4) / half))).astype(f4)
    rot = np.zeros((C, C), f4)
    k = np.arange(half)
    rot[2 * k, 2 * k] = rot[2 * k + 1, 2 * k + 1] = np.cos(th)
    rot[2 * k, 2 * k + 1] = np.sin(th)
    rot[2 * k + 1, 2 * k] = -np.sin(th)
    theta = (f4(10000.0) ** (f4(-2.0) * (np.arange(half, dtype=f4) - f4(1.0)) / f4(C))).astype(f4)
    ang = (np.arange(N, dtype=f4)[:, None] * theta[None, :]).astype(f4)
    cos_t = np.repeat(np.cos(ang), 2, axis=1).T.astype(f4)
    sin_t = np.stack([np.sin(ang), -np.sin(ang)], -1).reshape(N, C).T.astype(f4)
    swap = p ^ 1
    pos = np.arange(1, N + 1, dtype=f4)

    def col(v):
        return v.reshape(-1, 1)

    def tiles(v, n):
        return v.reshape(n, P, -1).transpose(1, 0, 2).reshape(P, -1)

    def taps(wt, bias):
        return np.concatenate([wt.reshape(C, 3), col(bias)], 1)

    W = h + "W_qkv"
    ip, ib = i[q + "in_proj_w"], i[q + "in_proj_b"]
    cols = {
        "ident": np.eye(P, dtype=f4), "rot": rot, "rotT": rot.T,
        "blockm": (p[:, None] // D == p[None, :] // D).astype(f4) / f4(N),
        "headm": (p[:, None] // D == np.arange(H)[None, :]).astype(f4),
        "cpe1": taps(i[m + "cpe1_w"], i[m + "cpe1_b"]), "g1": col(i[m + "norm1_g"]), "bn1": col(i[m + "norm1_b"]),
        "inb": col(i[m + "in_b"]), "actb": col(i[m + "actp_b"]), "dwc": taps(i[m + "dwc_w"], i[m + "dwc_b"]),
        "qb": col(i[m + "qk_b"][:C]), "kb": col(i[m + "qk_b"][C:]), "lepe": taps(i[m + "lepe_w"], i[m + "lepe_b"]),
        "outb": col(i[m + "out_b"]), "cpe2": taps(i[m + "cpe2_w"], i[m + "cpe2_b"]),
        "g2": col(i[m + "norm2_g"]), "bn2": col(i[m + "norm2_b"]), "fc1b": i[m + "fc1_b"].reshape(4, P).T,
        "fc2b": col(i[m + "fc2_b"]), "in": i[m + "in_w"], "actp": i[m + "actp_w"],
        "qw": i[m + "qk_w"][:, :C], "kw": i[m + "qk_w"][:, C:], "ow": i[m + "out_w"],
        "fc1": i[m + "fc1_w"], "fc2": tiles(i[m + "fc2_w"], 4),
        "tri": (p[:, None] <= p[None, :]).astype(f4), "ones": np.ones((P, P), f4),
        "iota": np.broadcast_to(np.arange(SLOTS, dtype=f4), (P, SLOTS)),
        "pcol": (p[:, None] + CAP * np.arange(E)[None, :]).astype(f4),
        "wsw": i[f + "w_switch"], "b1": i[f + "b1"].reshape(E * 4, P).T,
        "w1": i[f + "w1"].transpose(1, 0, 2).reshape(C, E * HID),
        "w2": i[f + "w2"].reshape(E * 4, P, C).transpose(1, 0, 2).reshape(P, -1),
        "cmask": np.where(p[None, :] > p[:, None], f4(NEG), f4(0)),
        "fmask": np.where((p[None, :] >= 64) & (p[:, None] < 64), f4(NEG), f4(0)),
        "fq": i[W][:C].T, "fk": i[W][C:2 * C].T, "fv": i[W][2 * C:].T, "fo": i[h + "W_out"].T,
        "fabd": np.broadcast_to(np.stack([i[h + "a"], i[h + "b"], i[h + "dt"]]), (P, 3)),
        "rq": i[q + "wq"].T, "rqs": i[q + "wq"].T[:, swap], "rk": i[q + "wk"].T, "rks": i[q + "wk"].T[:, swap],
        "rv": i[q + "wv"].T, "rvs": i[q + "wv"].T[:, swap],
        "pq": ip[:C].T, "pk": ip[C:2 * C].T, "pv": ip[2 * C:].T, "pqb": col(ib[:C]), "pkb": col(ib[C:2 * C]),
        "co": i[q + "out_w"].T, "cob": col(i[q + "out_b"]), "cosT": cos_t, "sinT": sin_t,
        "W0": i[b + "W0"], "AT": i[b + "A_init"].T, "Bi": i[b + "B_init"],
        "Wq": i[b + "Wq"].T, "Wk": i[b + "Wk"].T, "Wv": i[b + "Wv"].T, "Wo": i[b + "Wo"].T, "Wg": i[b + "Wg"].T,
        "lr": col(i[b + "log_lr"]), "lng": col(i[b + "ln_g"]), "lnb": col(i[b + "ln_b"]), "lsg": col(i[b + "ls_g"]),
        "enc": i[g + "enc_W"], "encb": i[g + "enc_b"].reshape(2, P).T, "s2c": tiles(i[g + "s2c_W"], 2),
        "s2cb": col(i[g + "s2c_b"]), "rW1": np.tile(i[g + "rW1"], (2, 1)), "rb1": col(i[g + "rb1"]), "rW2": i[g + "rW2"],
        "We1": np.tile(i[g + "We1"].transpose(1, 0, 2).reshape(M, -1), (2, 1)), "be1": i[g + "be1"].T,
        "We2": i[g + "We2"].transpose(1, 0, 2).reshape(P, -1), "be2": i[g + "be2"],
        "c2s": np.tile(i[g + "c2s_W"], (2, 1)), "c2sb": i[g + "c2s_b"].reshape(2, P).T, "dec": tiles(i[g + "dec_W"], 2),
        "decb": col(i[g + "dec_b"]),
        "esel": np.kron(np.tile(np.eye(E, dtype=f4), (3, 1)), np.ones((1, P), f4)),
    }
    weights = np.zeros((P, sum(wd for part in COLS for _, wd in part)), f4)
    for name, (at, width) in W_AT.items():
        v = cols[name]
        assert v.shape[1] == width, (name, v.shape, width)
        weights[:v.shape[0], at:at + width] = v
    consts = np.concatenate([np.broadcast_to(cols[name][:P] if name != "esel" else
                                             np.pad(cols[name], ((0, P - 24), (0, 0))), (P, width))
                             for name, (_, width) in K_AT.items()], 1)
    tables = np.concatenate([cols[name] for name in TAB_AT], 1)
    row_values = {
        "bsw": i[f + "b_switch"], "rev": E - np.arange(E, dtype=f4), "base": CAP * np.arange(E, dtype=f4),
        "b2": i[f + "b2"].reshape(-1), "rb2": i[g + "rb2"], "fing": i[g + "ln_g"], "finb": i[g + "ln_b"],
        "pos": f4(1.0) / (f4(1.0) + f4(0.1) * np.log(pos)), "vb": ib[2 * C:], "one": np.ones(1, f4),
    }
    rows = np.zeros(R_WIDTH, f4)
    for name, (at, width) in R_AT.items():
        rows[at:at + width] = row_values[name]
    x = np.ascontiguousarray(i[m + "x"]).reshape(T, C)

    nc = bacc.Bacc("TRN2", target_bir_lowering=False, num_devices=1)
    x_d = nc.dram_tensor("x_in", x.shape, F32, kind="ExternalInput").ap()
    w_d = nc.dram_tensor("weights_in", weights.shape, F32, kind="ExternalInput").ap()
    r_d = nc.dram_tensor("rows_in", rows.shape, F32, kind="ExternalInput").ap()
    k_d = nc.dram_tensor("consts_in", consts.shape, F32, kind="ExternalInput").ap()
    tab_d = nc.dram_tensor("tables_in", tables.shape, F32, kind="ExternalInput").ap()
    out_d = nc.dram_tensor("out", (T, C), F32, kind="ExternalOutput").ap()
    build(nc, x_d, w_d, r_d, k_d, tab_d, out_d)
    r = run_bass_kernel_spmd(nc, [{"x_in": x, "weights_in": weights, "rows_in": rows, "consts_in": consts, "tables_in": tables}], core_ids=[0])
    return r.results[0]["out"].reshape(B, N, C)
```
